# Optimizing a Trainium2 kernel written in Bass

```python
import numpy as np
import jax
import jax.numpy as jnp

def _softmax(x, axis=-1):
    return jax.nn.softmax(x, axis=axis)

def _gelu(x):
    return jax.nn.gelu(x, approximate=True)

def _silu(x):
    return jax.nn.silu(x)

def _sigmoid(x):
    return jax.nn.sigmoid(x)

def _layernorm(x, axis=-1, eps=1e-05):
    m = jnp.mean(x, axis=axis, keepdims=True)
    v = jnp.var(x, axis=axis, keepdims=True)
    return (x - m) / jnp.sqrt(v + eps)

def _scatter_add(tgt, idx, src, axis=0):
    return tgt.at[idx].add(src)

def _segment_sum(src, seg, n):
    return jax.ops.segment_sum(src, seg, n)
kernel_name = 'mk_vit_tower_cls_d1_tok_img768_r4_8e9c15'

def setup_inputs(seed: int=0):
    np.random.seed(seed)
    _w = jnp.asarray

    def _rec_inputs():
        import jax
        import jax.numpy as jnp
        _rk = jax.random.key(seed)
        x = -0.000125008 + 0.999885 * jax.random.normal(jax.random.fold_in(_rk, 1), (32, 1, 256, 256), jnp.float32)
        cls_tok = 0.02 * jax.random.normal(jax.random.fold_in(_rk, 5), (1, 1, 192), jnp.float32)
        return (x, cls_tok)
    x, cls_tok = _rec_inputs()

    def _L0_tok_setup():
        import jax, jax.numpy as jnp
        import numpy as np
        C, H, W = (1, 256, 256)
        P = 32
        D_TOK = 192
        B = 32
        D_PATCH = C * P * P

        def _patchify(x):
            Bx = x.shape[0]
            x = x.reshape(Bx, C, H // P, P, W // P, P)
            x = x.transpose(0, 2, 4, 1, 3, 5)
            return x.reshape(Bx, H // P * (W // P), D_PATCH)
        key = jax.random.key(seed)
        k_x, k_w, k_b = jax.random.split(key, 3)
        x = jax.random.normal(k_x, (B, C, H, W), dtype=jnp.float32)
        bound = 1.0 / np.sqrt(D_PATCH)
        w = jax.random.uniform(k_w, (D_TOK, D_PATCH), jnp.float32, -bound, bound)
        b = jax.random.uniform(k_b, (D_TOK,), jnp.float32, -bound, bound)
        return {'x': x, 'w': w, 'b': b}
    _L0_tok_all = _L0_tok_setup()
    _L0_tok_in = {k: v for k, v in _L0_tok_all.items() if k in ('w', 'b')}
    del _L0_tok_all

    def _L0_attn_setup():
        import jax, jax.numpy as jnp
        import numpy as np
        N_HEAD = 12
        N_EMBD = 192
        BLOCK = 512
        THETA = 10000.0

        def _rope_tables(head_dim, end, theta=THETA):
            half = head_dim // 2
            freqs = 1.0 / theta ** (jnp.arange(0, head_dim, 2, dtype=jnp.float32) / head_dim)
            t = jnp.arange(end, dtype=jnp.float32)
            ang = jnp.outer(t, freqs)
            return (jnp.cos(ang), jnp.sin(ang))

        def _apply_rope(x, cos, sin):
            B, H, T, hd = x.shape
            xr = x.reshape(B, H, T, hd // 2, 2)
            x0, x1 = (xr[..., 0], xr[..., 1])
            c = cos[None, None, :T, :]
            s = sin[None, None, :T, :]
            o0 = x0 * c - x1 * s
            o1 = x0 * s + x1 * c
            return jnp.stack([o0, o1], axis=-1).reshape(B, H, T, hd)
        key = jax.random.key(seed)
        ks = jax.random.split(key, 9)
        B, T, C = (2, 512, N_EMBD)
        std = 0.02
        return {'x': jax.random.normal(ks[0], (B, T, C), jnp.float32), 'norm_scale': jnp.ones((C,), jnp.float32), 'norm_bias': jnp.zeros((C,), jnp.float32), 'W_attn': jax.random.normal(ks[1], (C, 3 * C), jnp.float32) * std, 'b_attn': jax.random.normal(ks[2], (3 * C,), jnp.float32) * std, 'W_proj': jax.random.normal(ks[3], (C, C), jnp.float32) * std, 'b_proj': jax.random.normal(ks[4], (C,), jnp.float32) * std, 'sinks': jax.random.normal(ks[5], (N_HEAD,), jnp.float32) * 0.5, 'rezero': jax.random.normal(ks[6], (1,), jnp.float32) * 0.1}
    _L0_attn_all = _L0_attn_setup()
    _L0_attn_in = {k: v for k, v in _L0_attn_all.items() if k in ('norm_scale', 'norm_bias', 'W_attn', 'b_attn', 'W_proj', 'b_proj', 'sinks', 'rezero')}
    del _L0_attn_all

    def _L0_ffn_setup():
        import jax, jax.numpy as jnp
        import numpy as np
        E, TOPK = (32, 2)
        D, HID, BOT, OUT = (192, 512, 64, 192)
        B, S = (2, 128)
        key = jax.random.key(seed)
        ks = jax.random.split(key, 7)
        p = lambda k, shape: jax.random.normal(k, shape, dtype=jnp.float32) * 0.02
        return {'x': jax.random.normal(ks[0], (B, S, D), dtype=jnp.float32), 'gate_w': p(ks[1], (E, D)), 'W1': p(ks[2], (E, D, HID)), 'b1': jnp.zeros((E, HID), jnp.float32), 'W2': p(ks[3], (E, HID, HID)), 'b2': jnp.zeros((E, HID), jnp.float32), 'W3': p(ks[4], (E, HID, BOT)), 'b3': jnp.zeros((E, BOT), jnp.float32), 'Wl': p(ks[5], (E, BOT, OUT)), 'bl': jnp.zeros((E, OUT), jnp.float32)}
    _L0_ffn_all = _L0_ffn_setup()
    _L0_ffn_in = {k: v for k, v in _L0_ffn_all.items() if k in ('gate_w', 'W1', 'b1', 'W2', 'b2', 'W3', 'b3', 'Wl', 'bl')}
    del _L0_ffn_all
    return {'x': x, 'cls_tok': cls_tok, 'L0_tok_w': _L0_tok_in['w'], 'L0_tok_b': _L0_tok_in['b'], 'L0_attn_norm_scale': _L0_attn_in['norm_scale'], 'L0_attn_norm_bias': _L0_attn_in['norm_bias'], 'L0_attn_W_attn': _L0_attn_in['W_attn'], 'L0_attn_b_attn': _L0_attn_in['b_attn'], 'L0_attn_W_proj': _L0_attn_in['W_proj'], 'L0_attn_b_proj': _L0_attn_in['b_proj'], 'L0_attn_sinks': _L0_attn_in['sinks'], 'L0_attn_rezero': _L0_attn_in['rezero'], 'L0_ffn_gate_w': _L0_ffn_in['gate_w'], 'L0_ffn_W1': _L0_ffn_in['W1'], 'L0_ffn_b1': _L0_ffn_in['b1'], 'L0_ffn_W2': _L0_ffn_in['W2'], 'L0_ffn_b2': _L0_ffn_in['b2'], 'L0_ffn_W3': _L0_ffn_in['W3'], 'L0_ffn_b3': _L0_ffn_in['b3'], 'L0_ffn_Wl': _L0_ffn_in['Wl'], 'L0_ffn_bl': _L0_ffn_in['bl']}

def reference(x, cls_tok, L0_tok_w, L0_tok_b, L0_attn_norm_scale, L0_attn_norm_bias, L0_attn_W_attn, L0_attn_b_attn, L0_attn_W_proj, L0_attn_b_proj, L0_attn_sinks, L0_attn_rezero, L0_ffn_gate_w, L0_ffn_W1, L0_ffn_b1, L0_ffn_W2, L0_ffn_b2, L0_ffn_W3, L0_ffn_b3, L0_ffn_Wl, L0_ffn_bl):
    import jax
    import jax.numpy as jnp

    def _L0_tok_ref(x, w, b):
        import jax, jax.numpy as jnp
        import numpy as np
        C, H, W = (1, 256, 256)
        P = 32
        D_TOK = 192
        B = 32
        D_PATCH = C * P * P

        def _patchify(x):
            Bx = x.shape[0]
            x = x.reshape(Bx, C, H // P, P, W // P, P)
            x = x.transpose(0, 2, 4, 1, 3, 5)
            return x.reshape(Bx, H // P * (W // P), D_PATCH)
        patches = _patchify(x)
        return jnp.einsum('bld,td->blt', patches, w) + b

    def _L0_attn_ref(x, norm_scale, norm_bias, W_attn, b_attn, W_proj, b_proj, sinks, rezero):
        import jax, jax.numpy as jnp
        import numpy as np
        N_HEAD = 12
        N_EMBD = 192
        BLOCK = 512
        THETA = 10000.0

        def _rope_tables(head_dim, end, theta=THETA):
            half = head_dim // 2
            freqs = 1.0 / theta ** (jnp.arange(0, head_dim, 2, dtype=jnp.float32) / head_dim)
            t = jnp.arange(end, dtype=jnp.float32)
            ang = jnp.outer(t, freqs)
            return (jnp.cos(ang), jnp.sin(ang))

        def _apply_rope(x, cos, sin):
            B, H, T, hd = x.shape
            xr = x.reshape(B, H, T, hd // 2, 2)
            x0, x1 = (xr[..., 0], xr[..., 1])
            c = cos[None, None, :T, :]
            s = sin[None, None, :T, :]
            o0 = x0 * c - x1 * s
            o1 = x0 * s + x1 * c
            return jnp.stack([o0, o1], axis=-1).reshape(B, H, T, hd)
        B, T, C = x.shape
        H = N_HEAD
        hd = C // H
        xn = norm_scale * x + norm_bias
        qkv = xn @ W_attn + b_attn
        q, k, v = jnp.split(qkv, 3, axis=-1)
        q = q.reshape(B, T, H, hd).transpose(0, 2, 1, 3)
        k = k.reshape(B, T, H, hd).transpose(0, 2, 1, 3)
        v = v.reshape(B, T, H, hd).transpose(0, 2, 1, 3)
        cos, sin = _rope_tables(hd, T)
        q = _apply_rope(q, cos, sin)
        k = _apply_rope(k, cos, sin)
        scale = 1.0 / jnp.sqrt(jnp.float32(hd))
        att = jnp.einsum('bhqd,bhkd->bhqk', q, k) * scale
        causal = jnp.tril(jnp.ones((T, T), dtype=bool))
        att = jnp.where(causal[None, None], att, -jnp.inf)
        sink_col = jnp.broadcast_to(sinks.reshape(1, H, 1, 1), (B, H, T, 1))
        att = jnp.concatenate([sink_col, att], axis=-1)
        att = jax.nn.softmax(att, axis=-1)[..., 1:]
        y = jnp.einsum('bhqk,bhkd->bhqd', att, v)
        y = y.transpose(0, 2, 1, 3).reshape(B, T, C)
        y = (y @ W_proj + b_proj) * rezero
        return y

    def _L0_ffn_ref(x, gate_w, W1, b1, W2, b2, W3, b3, Wl, bl):
        import jax, jax.numpy as jnp
        import numpy as np
        E, TOPK = (32, 2)
        D, HID, BOT, OUT = (192, 512, 64, 192)
        B, S = (2, 128)
        Bz, Sl, d = x.shape
        xt = x.reshape(-1, d)
        scores = jax.nn.softmax(xt @ gate_w.T, axis=-1)
        topk_w, topk_idx = jax.lax.top_k(scores, TOPK)
        topk_w = topk_w / (topk_w.sum(-1, keepdims=True) + 1e-20)
        gelu = lambda v: jax.nn.gelu(v, approximate=False)
        h = gelu(jnp.einsum('nd,edh->enh', xt, W1) + b1[:, None, :])
        h = gelu(jnp.einsum('enh,ehg->eng', h, W2) + b2[:, None, :])
        z = jnp.einsum('eng,egb->enb', h, W3) + b3[:, None, :]
        out_all = jnp.einsum('enb,ebo->eno', z, Wl) + bl[:, None, :]
        sel = jnp.take_along_axis(out_all.transpose(1, 0, 2), topk_idx[:, :, None], axis=1)
        y = (sel * topk_w[:, :, None]).sum(axis=1)
        return y.reshape(Bz, Sl, OUT)
    h = _L0_tok_ref(x, L0_tok_w, L0_tok_b)
    h = jnp.concatenate([jnp.broadcast_to(cls_tok, (h.shape[0], 1, h.shape[2])), h], axis=1)
    h = h + _L0_attn_ref(_layernorm(h, axis=-1), L0_attn_norm_scale, L0_attn_norm_bias, L0_attn_W_attn, L0_attn_b_attn, L0_attn_W_proj, L0_attn_b_proj, L0_attn_sinks, L0_attn_rezero)
    h = h + _L0_ffn_ref(_layernorm(h, axis=-1), L0_ffn_gate_w, L0_ffn_W1, L0_ffn_b1, L0_ffn_W2, L0_ffn_b2, L0_ffn_W3, L0_ffn_b3, L0_ffn_Wl, L0_ffn_bl)
    return h

_drawn_inputs = setup_inputs


def setup_inputs(seed=0):
    import zlib

    import numpy as np

    out = dict(_drawn_inputs(seed))
    spreads = {'L0_attn_norm_scale': (1.0, 0.6),
     'L0_attn_norm_bias': (0.0, 0.8),
     'L0_ffn_b1': (0.0, 0.8),
     'L0_ffn_b2': (0.0, 0.8),
     'L0_ffn_b3': (0.0, 1.295),
     'L0_ffn_bl': (0.0, 0.566)}
    factors = {'cls_tok': 3.557,
     'L0_attn_W_attn': 6.182,
     'L0_attn_b_attn': 8.0,
     'L0_attn_W_proj': 6.606,
     'L0_attn_b_proj': 4.451,
     'L0_attn_sinks': 8.0,
     'L0_ffn_W1': 8.0,
     'L0_ffn_W2': 8.0,
     'L0_ffn_W3': 8.0,
     'L0_ffn_Wl': 2.815}
    for name, (base, spread) in spreads.items():
        noise = np.random.default_rng([zlib.crc32(name.encode()), seed]).standard_normal(out[name].shape)
        drawn = base * np.exp(spread * noise) if base else spread * noise
        out[name] = jnp.asarray(drawn.astype(out[name].dtype))
    for name, factor in factors.items():
        out[name] = (out[name] * factor).astype(out[name].dtype)
    return out
```

```python
import concourse.bass as bass
from concourse import mybir
from contextlib import ExitStack

IMAGES, SIDE, PATCH = 32, 256, 32
D = 192
GRID = SIDE // PATCH
PATCHES = GRID * GRID
DP = PATCH * PATCH
HEADS, HD = 12, 16
EXPERTS, HID, BOT = 32, 512, 64
P = 128
HALF = D // 2
HH = HEADS // 2
TILE_IMAGES = P // PATCHES
TILES = IMAGES // TILE_IMAGES
NT = TILES + 1
GROUPS = DP // P
ROWS = P // PATCH
KEYS = PATCHES + 1
EPS = 1e-5
MASKED = -1e30

TOKENS = IMAGES * PATCHES + 1
CHUNKS = -(-TOKENS // P)
CAP = TOKENS + P
ROW = D + 2
SPARE2 = EXPERTS * CAP
SPARE0 = SPARE2 + CAP
SPARE1 = SPARE0 + P
SLOTS = SPARE1 + P
RESULTS = NT * P * 2
LOOP_START, LOOP_TURNS = 8, 2
LOOP_END = LOOP_START + 4 * LOOP_TURNS
OUT_RING = 6
RING = 4

C_ID, C_TRI, C_ROPE_C, C_ROPE_S = 0, P, 2 * P, 2 * P + 2 * HD
C_CAUSAL = C_ROPE_S + 2 * HD
C_IOTA = C_CAUSAL + HH * KEYS
C_ECAP = C_IOTA + EXPERTS
C_STEP = C_ECAP + EXPERTS
C_HEAD = C_STEP + CHUNKS - 1
C_KEEP = C_HEAD + HH
C_SPARE = C_KEEP + NT
C_PADID = C_SPARE + 2 * NT
C_DEST = C_PADID + 1
C_END = C_DEST + 2 * NT


def vit_moe_kernel(nc, x, cls_tok, tok_w, tok_b, n_scale, n_bias, w_attn, b_attn, w_proj, b_proj,
                   sinks, rezero, gate_w, w1, b1, w2, b2, w3, b3, wl, bl, table, out):
    f32, bf16 = mybir.dt.float32, mybir.dt.bfloat16
    i32, u32 = mybir.dt.int32, mybir.dt.uint32
    ALU, ACT, AX = mybir.AluOpType, mybir.ActivationFunctionType, mybir.AxisListType

    slots = nc.dram_tensor("slots", (SLOTS, ROW), f32).ap()
    results = nc.dram_tensor("results", (RESULTS + P, D), f32).ap()
    x_v = x.rearrange("b c (i g r) w -> (b c i) g (r w)", i=GRID, g=GROUPS)
    res_v = results[0:RESULTS, :].rearrange("(n p k) d -> n p (k d)", p=P, k=2)

    ctx = ExitStack()
    with ctx:
        def sb(name, shape, dt=f32):
            return ctx.enter_context(nc.sbuf_tensor(name, shape, dt))

        sems = {}

        def sem(name):
            if name not in sems:
                sems[name] = ctx.enter_context(nc.semaphore(name))
            return sems[name]

        def need(eng, name, value):
            if not isinstance(value, int) or value > 0:
                eng.wait_ge(sem(name), value)

        def alone(eng):
            eng.nop(nofuse=True)

        cst = sb("cst", [P, C_END])
        ident = cst[:, C_ID:C_ID + P]
        causal = sb("causal", [P, HH * KEYS], bf16)
        identb = sb("identb", [P, P], bf16)
        earlier = sb("earlier", [P, P], bf16)
        onesb = sb("onesb", [P, P], bf16)
        iota = cst[:, C_IOTA:C_IOTA + EXPERTS]
        ecap = cst[:, C_ECAP:C_ECAP + EXPERTS]
        scratch = sb("scratch", [P, 2 * DP])
        tokw = scratch[0:HALF, :].rearrange("p (c n) -> p c n", c=2)
        h1b = scratch[:, 0:4 * P].rearrange("p (c t) -> p c t", c=4)
        h2b = scratch[:, 4 * P:8 * P].rearrange("p (c t) -> p c t", c=4)
        xeT = scratch[0:HALF, 8 * P:10 * P].rearrange("p (c t) -> p c t", c=2)
        yb = scratch[:, 10 * P:10 * P + D]
        tokwT = sb("tokwT", [P, GROUPS, D])
        tokb = sb("tokb", [P, D])
        scalec = sb("scalec", [HALF, 2])
        biasc = sb("biasc", [HALF, 2])
        wa = sb("wa", [HALF + 1, 2, 3 * D])
        was = sb("was", [HALF + 1, 2, 3 * D])
        wp = sb("wp", [HALF + 1, 2, D])
        wps = sb("wps", [HALF + 1, 2, D])
        rez = sb("rez", [HALF + 1, 1])
        sinkb = sb("sinkb", [P, HEADS])
        gw = sb("gw", [EXPERTS, D])
        gwT = sb("gwT", [HALF, 2, EXPERTS])
        b3r = sb("b3r", [EXPERTS, BOT])
        b12T = sb("b12T", [P, EXPERTS + 1, 8])
        bcur = [sb(f"bcur{i}", [P, 8]) for i in range(2)]
        b3T = sb("b3T", [BOT, EXPERTS + 1])
        raw = [sb(f"raw{i}", [P, ROWS * SIDE]) for i in range(4)]
        pix = [sb(f"pix{i}", [P, P * GRID]) for i in range(2)]
        b1r = pix[0][0:EXPERTS, 0:HID]
        b2r = pix[0][0:EXPERTS, HID:2 * HID]
        h = sb("h", [P, NT, D])
        st6 = sb("st6", [P, 6])
        mv = sb("mv", [P, NT, 2])
        ve1 = sb("ve1", [P, NT])
        rs1 = sb("rs1", [P, NT])
        mhalf = sb("mhalf", [P, NT])
        xhat = [sb(f"xhat{i}", [P, D]) for i in range(2)]
        xT = [sb(f"xT{i}", [HALF + 1, 2, P]) for i in range(2)]
        rope_c = [sb(f"ropec{i}", [P, 2 * D]) for i in range(2)]
        rope_s = [sb(f"ropes{i}", [P, 2 * D]) for i in range(2)]
        qk = [sb(f"qk{i}", [P, 2 * D]) for i in range(2)]
        qkT = [sb(f"qkT{i}", [HALF, 4, P]) for i in range(2)]
        kblk = [[sb(f"kblk{i}{b}", [HALF, 2, HH, KEYS]) for b in range(2)] for i in range(2)]
        vblk = [sb(f"vblk{i}", [P, 2, HH, 2, HD + 1]) for i in range(4)]
        mx = [sb(f"mx{i}", [P, HEADS]) for i in range(2)]
        probs = [sb(f"probs{i}", [P, HEADS * (PATCHES + 2)]) for i in range(2)]
        p_patch = [t[:, 0:HEADS * PATCHES] for t in probs]
        p_class = [t[:, HEADS * PATCHES:HEADS * KEYS] for t in probs]
        p_sink = [t[:, HEADS * KEYS:HEADS * (KEYS + 1)] for t in probs]
        pT = [sb(f"pT{i}", [P, HH, P]) for i in range(2)]
        vcls = sb("vcls", [P, D])
        pvc = [sb(f"pvc{i}", [P, D]) for i in range(2)]
        psum2 = [sb(f"psum2{i}", [P, HEADS]) for i in range(2)]
        den = [sb(f"den{i}", [P, HEADS]) for i in range(2)]
        rden = [sb(f"rden{i}", [P, HEADS]) for i in range(2)]
        yv = [sb(f"yv{i}", [P, D]) for i in range(2)]
        y = [sb(f"y{i}", [P, D]) for i in range(2)]
        yT = [sb(f"yT{i}", [HALF + 1, 2, P]) for i in range(2)]
        st6b = sb("st6b", [P, 6])
        mv2 = [sb(f"mv2{i}", [P, 3]) for i in range(2)]
        rs2 = [sb(f"rs2{i}", [P, 1]) for i in range(2)]
        row = [[sb(f"row{c}{i}", [P, ROW]) for i in range(4)] for c in range(2)]
        x2T = [sb(f"x2T{i}", [HALF, 2, P]) for i in range(2)]
        logits = sb("logits", [P, NT, EXPERTS])
        top2 = sb("top2", [P, NT, 2])
        lgs = [sb(f"lgs{i}", [P, EXPERTS]) for i in range(2)]
        top8 = [sb(f"top8{i}", [P, 8]) for i in range(2)]
        idx8 = [sb(f"idx8{i}", [P, 8], u32) for i in range(2)]
        idxf = [sb(f"idxf{i}", [P, 2]) for i in range(2)]
        pick = [sb(f"pick{i}", [P, 2, EXPERTS]) for i in range(2)]
        member = [sb(f"member{i}", [P, EXPERTS], bf16) for i in range(2)]
        before = sb("before", [P, EXPERTS], bf16)
        rankc = [sb(f"rankc{i}", [P, EXPERTS]) for i in range(2)]
        slp = [sb(f"slp{i}", [P, 2, EXPERTS]) for i in range(2)]
        slf = [sb(f"slf{i}", [P, 2]) for i in range(2)]
        sls = [sb(f"sls{i}", [P, 2]) for i in range(2)]
        slu = [sb(f"slu{i}", [P, 2], u32) for i in range(4)]
        wgt = sb("wgt", [P, NT, 2])
        gmx = sb("gmx", [P, NT, EXPERTS])
        gz = sb("gz", [P, NT])
        gri = sb("gri", [P, NT])
        gs2 = sb("gs2", [P, NT, 2])
        gden = sb("gden", [P, NT])
        cnt = sb("cnt", [1, EXPERTS])
        over = sb("over", [1, EXPERTS, CHUNKS - 1])
        ntile = sb("ntile", [1, EXPERTS])
        ones1 = sb("ones1", [1, EXPERTS])
        startf = sb("startf", [1, EXPERTS + 1])
        cnt_i = sb("cnt_i", [1, EXPERTS + 1], i32)
        start_i = sb("start_i", [1, EXPERTS + 2], i32)
        W1 = [sb(f"W1_{i}", [HALF, 2, HID]) for i in range(RING)]
        W2 = [sb(f"W2_{i}", [P, 4, HID]) for i in range(RING)]
        blocks = [W2[RING - 1][:, 2 * i:2 * i + 2, :].rearrange("p a (j n) -> p (a j) n", j=4) for i in range(2)]
        W3 = [sb(f"W3_{i}", [P, 4, BOT]) for i in range(RING)]
        WL = [sb(f"WL_{i}", [P, D]) for i in range(RING)]
        pad = sb("pad", [P, ROW])
        xs = [[sb(f"xs{a}{b}", [P, ROW]) for b in range(2)] for a in range(2)]
        zb = sb("zb", [P, P])
        dest_new = sb("dest_new", [P, 1], u32)
        dest_old = sb("dest_old", [P, 1], u32)
        end = [W2[i // 2][:, 2 * (i % 2):2 * (i % 2) + 2, :].rearrange("p a n -> p (a n)") for i in range(OUT_RING)]
        res_flat = [t[:, 0:2 * D] for t in end]
        res = [t.rearrange("p (k d) -> p k d", k=2) for t in res_flat]
        o1 = [t[:, 2 * D:3 * D] for t in end]
        o2 = [t[:, 3 * D:4 * D] for t in end]

        PS = ctx.enter_context(nc.psum_tensor("PS", [P, 8, 512], f32))
        p_xT = PS[0:HALF, 0, 0:256].rearrange("p (c t) -> p c t", c=2)
        p_v = PS[:, 0, 256:256 + D]
        p_qkT = PS[0:HALF, 1, :].rearrange("p (c t) -> p c t", c=4)
        p_yT = PS[0:HALF, 1, 0:256].rearrange("p (c t) -> p c t", c=2)
        p_x2T = PS[0:HALF, 1, 256:512].rearrange("p (c t) -> p c t", c=2)
        p_qk = PS[:, 2, 0:2 * D]
        p_pTa = PS[:, 3, :].rearrange("p (g t) -> p g t", g=4)
        p_pTb = PS[:, 4, 0:256].rearrange("p (g t) -> p g t", g=2)
        p_y = PS[:, 4, 256:256 + HEADS * (HD + 1)].rearrange("p (h d) -> p h d", d=HD + 1)
        p_s = PS[:, 5:7, 0:HH * KEYS].rearrange("p c (g k) -> p c g k", k=KEYS)
        p_proj = PS[:, 7, 0:D]
        p_gate = PS[:, 7, D:D + EXPERTS]
        p_rank = PS[:, 7, D + EXPERTS:D + 2 * EXPERTS]

        L1_BANKS, L2_BANKS = (1, 2, 3, 4), (5, 6, 1, 2)

        INIT = 14

        block = ctx.enter_context(nc.Block())

        def scattered(eng, n, jn):
            if not isinstance(n, int) or n >= 0:
                for ch in range(2):
                    eng.wait_ge(sem(f"scattered{ch}{jn % 4}"), 4 * (n - jn % 4) + 16)

        def pipeline(eng, step):
            def stages(k):
                s = {c for i, c in enumerate("ABC") if 1 <= k - i < NT}
                return s | {c for i, c in enumerate("DEFG", 3) if 0 <= k - i < NT}
            for k in range(1, LOOP_START):
                step(k, k, stages(k))
            with eng.Fori(0, LOOP_TURNS) as q:
                for j in range(4):
                    step(4 * q + LOOP_START + j, LOOP_START + j, set("ABCDEFG"))
            for k in range(LOOP_END, NT + 6):
                step(k, k, stages(k))

        def experts(eng, tile, enter=None, then=None):
            eng.wait_ge(sem("tables"), 2)
            with eng.Fori(0, EXPERTS // RING) as q:
                e0 = RING * q
                for u in range(RING):
                    e = e0 + u
                    n = eng.value_load(cnt_i[0:1, bass.ds(e, 1)], min_val=0, max_val=TOKENS)
                    s = eng.value_load(start_i[0:1, bass.ds(e + 1, 1)], min_val=0, max_val=2 * EXPERTS)
                    if enter:
                        enter(e0, u)
                    tile(e, u, 0, s)
                    if then:
                        then(e, u)
                    with eng.If(n > P):
                        tile(e, u, 1, s + 1)
                        with eng.If(n > 2 * P):
                            tile(e, u, 2, s + 2)
                            with eng.If(n > 3 * P):
                                with eng.Fori(3, CHUNKS) as c:
                                    with eng.If(n > c * P):
                                        tile(e, u, c, s + c)
                                    eng.nop()
                            eng.nop()
                        eng.nop()
                    eng.nop()

        def buf(u, c):
            return xs[u % 2][0 if isinstance(c, int) and c in (0, 2) else 1]

        @block.sync
        def _(sp):
            sp.dma_start(cst[:, :], table).then_inc(sem("cst_in"), 16)
            sp.dma_start(tokw[:, :, :], tok_w.rearrange("(c p) n -> p c n", p=HALF)).then_inc(sem("tokw_in"), 16)
            for n in range(2):
                sp.dma_start(raw[n][:, :], x_v[0:P, n, :]).then_inc(sem(f"raw_in{n}"), 16)
            sp.wait_ge(sem("wa_in"), 64)
            for n in range(2, 4):
                sp.dma_start(raw[n][:, :], x_v[0:P, n, :]).then_inc(sem(f"raw_in{n}"), 16)
            def expert_load(slot, e):
                w_in = sem(f"w_in{slot}")
                one = bass.ds(e, 1)
                sp.dma_start(W1[slot][:, :, :], w1[one].rearrange("a (c p) n -> p (a c) n", p=HALF)).then_inc(w_in, 16)
                sp.dma_start(W2[slot][:, :, :], w2[one].rearrange("a (c p) n -> p (a c) n", p=P)).then_inc(w_in, 16)
                sp.dma_start(W3[slot][:, :, :], w3[one].rearrange("a (c p) n -> p (a c) n", p=P)).then_inc(w_in, 16)
                sp.dma_start(WL[slot][0:BOT, :], wl[one].rearrange("a p n -> (a p) n")).then_inc(w_in, 16)
                sp.dma_start(WL[slot][BOT:BOT + 1, :], bl[one, :]).then_inc(w_in, 16)
            for n in range(4, 2 * GROUPS):
                sp.wait_ge(sem("blocks"), n - 3)
                half, g = n // GROUPS, n % GROUPS
                sp.dma_start(raw[n % 4][:, :], x_v[half * P:(half + 1) * P, g, :]).then_inc(sem(f"raw_in{n % 4}"), 16)
            sp.wait_ge(sem("init"), INIT)
            for e in range(2):
                expert_load(e, e)
            sp.wait_ge(sem("tables"), 2)
            sp.wait_ge(sem("pad_set"), 1)
            sp.sem_inc(sem("xs_in"), 16)
            n0 = sp.value_load(cnt_i[0:1, 0:1], min_val=0, max_val=TOKENS)
            sp.dma_start(slots[bass.ds(n0, P), :], pad[:, :]).then_inc(sem("pad_out0"), 16)
            for n in range(NT - 4, NT):
                scattered(sp, n, n)

            def xs_load(e, u, c, g, free):
                sp.wait_ge(sem("xe_t"), free)
                sp.wait_ge(sem("dest"), free)
                sp.wait_ge(sem("xs_in"), 16 * g + 16)
                sp.dma_start(buf(u, c)[:, :],
                             slots[bass.ds(e * CAP + c * P, P), :]).then_inc(sem("xs_in"), 16)

            def group(e0, full):
                for u in range(RING):
                    e = e0 + u
                    nn = sp.value_load(cnt_i[0:1, bass.ds(e + 1, 1)], min_val=0, max_val=TOKENS)
                    sp.dma_start(slots[bass.ds((e + 1) * CAP + nn, P), :], pad[:, :]).then_inc(sem(f"pad_out{(u + 1) % 2}"), 16)
                    n = sp.value_load(cnt_i[0:1, bass.ds(e, 1)], min_val=0, max_val=TOKENS)
                    s = sp.value_load(start_i[0:1, bass.ds(e + 1, 1)], min_val=0, max_val=2 * EXPERTS)
                    back = sp.value_load(start_i[0:1, bass.ds(e, 1)], min_val=0, max_val=2 * EXPERTS)
                    sp.wait_ge(sem(f"pad_out{u % 2}"), 8 * e0 + 16 * (u // 2 + 1))
                    alone(sp)
                    xs_load(e, u, 0, s, back + 1)
                    with sp.If(n > P):
                        xs_load(e, u, 1, s + 1, back + 1)
                        with sp.If(n > 2 * P):
                            xs_load(e, u, 2, s + 2, s + 2)
                            with sp.If(n > 3 * P):
                                with sp.Fori(3, CHUNKS) as c:
                                    with sp.If(n > c * P):
                                        xs_load(e, u, c, s + c, s + c + 1)
                                    sp.nop()
                            sp.nop()
                        sp.nop()
                    sp.nop()
                    if full or u < RING - 2:
                        sp.wait_ge(sem("l4"), back + 1)
                        alone(sp)
                        expert_load((u + 2) % RING, e + 2)

            with sp.Fori(0, EXPERTS // RING - 1) as q:
                group(RING * q, True)
            group(EXPERTS - RING, False)

            tiles = sp.value_load(start_i[0:1, EXPERTS + 1:EXPERTS + 2], min_val=EXPERTS, max_val=2 * EXPERTS)
            sp.wait_ge(sem("result_out"), 16 * tiles + 16)
            sp.wait_ge(sem("pad_out0"), 8 * EXPERTS + 16)
            sp.wait_ge(sem("pad_out1"), 8 * EXPERTS)
            for n in range(NT):
                i = n % OUT_RING
                need(sp, "o1", n - OUT_RING + 1)
                need(sp, "o2", n - OUT_RING + 1)
                if n == 0:
                    sp.dma_start(res[0][0:IMAGES, 0, :], bass.AP(results.tensor, 0, [[0, IMAGES], [1, D]])).then_inc(sem("res_in0"), 16)
                    sp.dma_start(res[0][0:IMAGES, 1, :], bass.AP(results.tensor, D, [[0, IMAGES], [1, D]])).then_inc(sem("res_in0"), 16)
                else:
                    sp.dma_start(res_flat[i], res_v[n]).then_inc(sem(f"res_in{i}"), 16)

        @block.gpsimd
        def _(pool):
            pool.memset(pad[:, :], 0.0).then_inc(sem("pad_zero"), 1)
            pool.wait_ge(sem("pad_zero"), 1)
            pool.wait_ge(sem("cst_in"), 16)
            pool.tensor_copy(pad[:, D:D + 1].bitcast(u32), cst[:, C_PADID:C_PADID + 1]).then_inc(sem("pad_set"), 1)
            pool.tensor_copy(dest_new[:, :], cst[:, C_PADID:C_PADID + 1]).then_inc(sem("pad_set"), 1)
            pool.sem_inc(sem("kept"), 4)
            pool.wait_ge(sem("cls_ve"), 1)
            pool.tensor_tensor(rs1[:, 0:1], ve1[:, 0:1], mhalf[:, 0:1], ALU.pow).then_inc(sem("cls_rs"), 1)
            for hf in range(2):
                pool.wait_ge(sem("ve1"), hf + 1)
                pool.tensor_tensor(rs1[:, 8 * hf + 1:8 * hf + 9], ve1[:, 8 * hf + 1:8 * hf + 9], mhalf[:, 0:8], ALU.pow).then_inc(sem("rs1"), 1)

            def step(k, j, stages):
                a, b, c, d, e, _, f = (k - i for i in range(7))
                ja, jb, jc, jd, je, _, jf = (j - i for i in range(7))
                if "B" in stages:
                    pool.wait_ge(sem("qkT"), b)
                    need(pool, "scores", b - 2)
                    for half in range(2):
                        ins = pool.tensor_tensor(
                            kblk[jb % 2][1][:, half, :, 0:PATCHES],
                            qkT[jb % 2][:, 2 + half:3 + half, PATCHES:P].to_broadcast([HALF, HH, PATCHES]),
                            cst[0:HALF, C_HEAD:C_HEAD + HH].unsqueeze(2).to_broadcast([HALF, HH, PATCHES]), ALU.mult)
                    ins.then_inc(sem("kblk1"), 1)
                if "G" in stages:
                    pool.wait_ge(sem("top8"), f + 1)
                    pool.tensor_copy(logits[:, bass.ds(f, 1), :].rearrange("p a e -> p (a e)"), lgs[jf % 2][:, :]).then_inc(sem("kept"), 1)
                    pool.tensor_copy(top2[:, bass.ds(f, 1), :].rearrange("p a e -> p (a e)"), top8[jf % 2][:, 0:2]).then_inc(sem("kept"), 1)
                    pool.wait_ge(sem("slot"), f + 1)
                    pool.wait_ge(sem("row"), 3 * f + 3)
                    alone(pool)
                    for ch in range(2):
                        pool.indirect_dma_start(
                            out=slots, out_offset=bass.IndirectOffsetOnAxis(ap=slu[jf % 4][:, ch:ch + 1], axis=0),
                            in_=row[ch][jf % 4][:, :], in_offset=None).then_inc(sem(f"scattered{ch}{jf % 4}"), 16)
                if "C" in stages:
                    pool.wait_ge(sem("exp"), c)
                    need(pool, "yv", c - 2)
                    need(pool, "den", c - 2)
                    pool.tensor_tensor(pvc[jc % 2][:, :].rearrange("p (h d) -> p h d", d=HD),
                                       p_class[jc % 2].unsqueeze(2).to_broadcast([P, HEADS, HD]),
                                       vcls[:, :].rearrange("p (h d) -> p h d", d=HD), ALU.mult).then_inc(sem("pvc"), 1)
                    pool.tensor_tensor(psum2[jc % 2][:, :], p_class[jc % 2], p_sink[jc % 2], ALU.add).then_inc(sem("psum2"), 1)
                if "E" in stages:
                    pool.wait_ge(sem("x2"), e + 1)
                    scattered(pool, e - 4, je - 4)
                    alone(pool)
                    pool.tensor_copy(row[1][je % 4][:, 0:D], row[0][je % 4][:, 0:D]).then_inc(sem("row"), 1)
                    for ch in range(2):
                        pool.tensor_copy(row[ch][je % 4][:, D:D + 1].bitcast(u32),
                                         cst[:, bass.ds(C_DEST + ch * NT + e, 1)]).then_inc(sem("row"), 1)
                if "A" in stages:
                    pool.wait_ge(sem("rope_c"), a)
                    pool.wait_ge(sem("rope_s"), a)
                    need(pool, "qk_t", a - 2)
                    pool.tensor_tensor(qk[ja % 2][:, :], rope_c[ja % 2][:, :], rope_s[ja % 2][:, :], ALU.add).then_inc(sem("qk"), 1)
                if "D" in stages:
                    pool.wait_ge(sem("ve2"), d + 1)
                    need(pool, "x2", d - 1)
                    pool.tensor_tensor(rs2[jd % 2][:, :], mv2[jd % 2][:, 2:3], mhalf[:, 0:1], ALU.pow).then_inc(sem("rs2"), 1)

            pipeline(pool, step)

            pool.sem_inc(sem("sent"), 1)
            def send(g):
                pool.wait_ge(sem("result"), g + 2)
                alone(pool)
                pool.indirect_dma_start(
                    out=results, out_offset=bass.IndirectOffsetOnAxis(ap=dest_old[:, :], axis=0),
                    in_=yb[:, :], in_offset=None).then_inc(sem("result_out"), 16)
                pool.wait_ge(sem("result_out"), 16 * g + 16)
                pool.sem_inc(sem("sent"), 1)

            experts(pool, lambda e, u, c, g: send(g))
            tiles = pool.value_load(start_i[0:1, EXPERTS + 1:EXPERTS + 2], min_val=EXPERTS, max_val=2 * EXPERTS)
            send(tiles)

        @block.scalar
        def _(act):
            act.dma_start(h[:, 0, :], cls_tok.rearrange("a b d -> (a b) d").broadcast_to([P, D])).then_inc(sem("cls_in"), 16)
            act.dma_start(wa[0:HALF, :, :], w_attn.rearrange("(c p) n -> p c n", p=HALF)).then_inc(sem("wa_in"), 16)
            act.dma_start(wa[HALF:HALF + 1, 1, :], b_attn.rearrange("(a n) -> a n", a=1)).then_inc(sem("wa_in"), 16)
            with nc.allow_non_contiguous_dma("per-feature scale and bias, once"):
                act.dma_start(scalec[:, :], n_scale.rearrange("(c p) -> p c", p=HALF)).then_inc(sem("wa_in"), 16)
                act.dma_start(biasc[:, :], n_bias.rearrange("(c p) -> p c", p=HALF)).then_inc(sem("wa_in"), 16)
            act.dma_start(sinkb[:, :], sinks.rearrange("(a n) -> a n", a=1).broadcast_to([P, HEADS])).then_inc(sem("sink_in"), 16)
            act.dma_start(wp[0:HALF, :, :], w_proj.rearrange("(c p) n -> p c n", p=HALF)).then_inc(sem("wp_in"), 16)
            act.dma_start(wp[HALF:HALF + 1, 1, :], b_proj.rearrange("(a n) -> a n", a=1)).then_inc(sem("wp_in"), 16)
            act.dma_start(rez[:, :], rezero.rearrange("(a n) -> a n", a=1).broadcast_to([HALF + 1, 1])).then_inc(sem("wp_in"), 16)
            act.dma_start(gw[:, :], gate_w).then_inc(sem("bias_in"), 16)
            act.dma_start(b1r[:, :], b1).then_inc(sem("bias_in"), 16)
            act.dma_start(b2r[:, :], b2).then_inc(sem("bias_in"), 16)
            act.dma_start(b3r[:, :], b3).then_inc(sem("bias_in"), 16)
            act.dma_start(tokb[:, :], tok_b.rearrange("(a n) -> a n", a=1).broadcast_to([P, D])).then_inc(sem("tokb_in"), 16)
            act.wait_ge(sem("cst_in"), 16)
            act.activation(identb[:, :], ident, ACT.Copy).then_inc(sem("tab"), 1)
            act.activation(earlier[:, :], cst[:, C_TRI:C_TRI + P], ACT.Copy).then_inc(sem("tab"), 1)
            act.activation(causal[:, :], cst[:, C_CAUSAL:C_CAUSAL + HH * KEYS], ACT.Copy).then_inc(sem("tab"), 1)
            for q in range(4):
                act.wait_ge(sem("tokw_t"), q + 1)
                act.activation(tokwT[:, 2 * q:2 * q + 2, :], PS[:, q, 0:2 * D].rearrange("p (g n) -> p g n", g=2), ACT.Copy).then_inc(sem("tokwT"), 1)
            act.wait_ge(sem("bias_t"), 1)
            for w in range(2):
                act.activation(b12T[:, 0:EXPERTS, 4 * w:4 * w + 4], PS[:, 4, w * P:(w + 1) * P].rearrange("p (c e) -> p e c", c=4), ACT.Copy).then_inc(sem("biasT"), 1)
            act.activation(gwT[:, :, :], PS[0:HALF, 4, 2 * P:2 * P + 64].rearrange("p (c e) -> p c e", c=2), ACT.Copy).then_inc(sem("biasT"), 1)
            act.activation(b3T[:, 1:EXPERTS + 1], PS[0:BOT, 4, 320:352], ACT.Copy).then_inc(sem("biasT"), 1)
            act.wait_ge(sem("cls_xt"), 1)
            act.wait_ge(sem("init"), INIT)
            act.activation(xT[0][0:HALF, :, :], p_xT, ACT.Copy).then_inc(sem("cls_xT"), 1)
            act.wait_ge(sem("cls_qkv"), 1)
            act.activation(vcls[:, :], p_v, ACT.Copy).then_inc(sem("vcls"), 1)
            act.activation(qk[0][:, 0:D], p_qk[:, 0:D], ACT.Copy, scale=HD ** -0.5).then_inc(sem("cls_qk"), 1)
            act.activation(qk[0][:, D:2 * D], p_qk[:, D:2 * D], ACT.Copy).then_inc(sem("cls_qk"), 1)
            act.wait_ge(sem("cls_kt"), 1)
            act.activation(qkT[0][:, 2:4, :], p_qkT[:, 2:4, :], ACT.Copy).then_inc(sem("cls_kT"), 1)
            act.wait_ge(sem("cls_sub"), 3)
            act.activation(psum2[0][:, :], psum2[0][:, :], ACT.Exp).then_inc(sem("cls_exp"), 1)
            act.activation(psum2[1][:, :], psum2[1][:, :], ACT.Exp).then_inc(sem("cls_exp"), 1)
            def sort_pixels(n):
                act.wait_ge(sem(f"raw_in{n % 4}"), 16 * (n // 4 + 1))
                need(act, "pix_t", n - 1)
                act.activation(blocks[n % 2][:, :, :].rearrange("p j (r c) -> p j r c", r=ROWS),
                               raw[n % 4][:, :].rearrange("p (r j c) -> p j r c", r=ROWS, j=GRID), ACT.Copy).then_inc(sem("blocks"), 1)
            sort_pixels(0)
            sort_pixels(1)
            for hf in range(2):
                for g in range(GROUPS):
                    n = hf * GROUPS + g
                    act.wait_ge(sem("pix_t"), n + 1)
                    need(act, "embed", n - 1)
                    act.activation(pix[n % 2][:, :].rearrange("p (t j) -> p j t", j=GRID)[:, 0:4, :],
                                   PS[:, 4 + 2 * (n % 2), :].rearrange("p (j t) -> p j t", j=4), ACT.Copy).then_inc(sem("pix_a"), 1)
                    if n + 2 < 2 * GROUPS:
                        sort_pixels(n + 2)

            def step(k, j, stages):
                a, b, c, d, e, f = (k - i for i in range(6))
                ja, jb, jc, jd, je, jf = (j - i for i in range(6))
                if "B" in stages:
                    act.wait_ge(sem("qk_t"), b)
                    need(act, "kblk0", b - 2)
                    need(act, "kblk1", b - 2)
                    need(act, "scores", b - 2)
                    act.activation(qkT[jb % 2][:, :, :], p_qkT, ACT.Copy).then_inc(sem("qkT"), 1)
                if "A" in stages:
                    act.wait_ge(sem("x_t"), a)
                    need(act, "qkv", a - 2)
                    act.activation(xT[ja % 2][0:HALF, :, :], p_xT, ACT.Copy).then_inc(sem("xT"), 1)
                if "C" in stages:
                    act.wait_ge(sem("p_t"), c)
                    need(act, "pv", c - 2)
                    act.activation(pT[jc % 2][:, 0:4, :], p_pTa, ACT.Copy).then_inc(sem("pTa"), 1)
                if "A" in stages:
                    act.wait_ge(sem("qkv"), a)
                    need(act, "pv", a - 4)
                    for b_ in range(2):
                        for odd in range(2):
                            ins = act.activation(
                                vblk[ja % 4][odd * PATCHES:(odd + 1) * PATCHES, b_, :, odd, 0:HD],
                                PS[b_ * PATCHES:(b_ + 1) * PATCHES, 0, 256:256 + D].rearrange("p (g o d) -> p g o d", o=2, d=HD)[:, :, odd, :],
                                ACT.Copy)
                    ins.then_inc(sem("vblk"), 1)
                if "D" in stages:
                    act.wait_ge(sem("yx_t"), k - 2)
                    need(act, "tail", d - 1)
                    act.activation(yT[jd % 2][0:HALF, :, :], p_yT, ACT.Copy).then_inc(sem("yT"), 1)
                if "E" in stages:
                    act.wait_ge(sem("yx_t"), k - 2)
                    need(act, "tail", e)
                    act.activation(x2T[je % 2][:, :, :], p_x2T, ACT.Copy).then_inc(sem("x2T"), 1)
                if "B" in stages:
                    act.wait_ge(sem("shifted"), 3 * b)
                    act.activation(probs[jb % 2][:, :], probs[jb % 2][:, :], ACT.Exp).then_inc(sem("exp"), 1)

            pipeline(act, step)
            act.wait_ge(sem("g_sub"), 2)
            act.activation(gmx[:, :, :], gmx[:, :, :], ACT.Exp).then_inc(sem("g_exp"), 1)
            act.activation(gs2[:, :, :], gs2[:, :, :], ACT.Exp).then_inc(sem("g_exp"), 1)

            act.wait_ge(sem("last_zero"), 3)
            act.sem_inc(sem("g2"), 4)

            def tile(e, u, c, g):
                for m in range(4):
                    act.wait_ge(sem("l1"), 4 * g + m + 1)
                    act.activation(h1b[:, m, :], PS[:, L1_BANKS[m], 0:P], ACT.Gelu,
                                   bias=bcur[u % 2][:, m:m + 1]).then_inc(sem("g1"), 1)
                for m in range(4):
                    act.wait_ge(sem("l2"), 4 * g + m + 1)
                    act.activation(h2b[:, m, :], PS[:, L2_BANKS[m], 0:P], ACT.Gelu,
                                   bias=bcur[u % 2][:, 4 + m:5 + m]).then_inc(sem("g2"), 1)

            def enter(e0, u):
                act.wait_ge(sem("bcur"), e0 + u + 1)

            experts(act, tile, enter=enter)
            for n in range(NT):
                i = n % OUT_RING
                act.wait_ge(sem("o2"), n + 1)
                if n == 0:
                    act.dma_start(out[:, 0, :], o2[0][0:IMAGES, :]).then_inc(sem("out0"), 16)
                else:
                    for b_ in range(2):
                        act.dma_start(out[2 * (n - 1) + b_, 1:KEYS, :], o2[i][b_ * PATCHES:(b_ + 1) * PATCHES, :]).then_inc(sem(f"out{i}"), 16)
            for i in range(OUT_RING):
                act.wait_ge(sem(f"out{i}"), sum(16 if n == 0 else 32 for n in range(i, NT, OUT_RING)))

        @block.tensor
        def _(pe):
            pe.wait_ge(sem("cst_in"), 16)
            pe.wait_ge(sem("tokw_in"), 16)
            for q in range(4):
                for i in range(2):
                    for c in range(2):
                        ins = pe.transpose(PS[:, q, i * D + c * HALF:i * D + (c + 1) * HALF],
                                           tokw[:, c, (2 * q + i) * P:(2 * q + i + 1) * P], ident[0:HALF, 0:HALF])
                ins.then_inc(sem("tokw_t"), 1)
            pe.wait_ge(sem("bias_in"), 64)
            for c in range(4):
                pe.transpose(PS[:, 4, 32 * c:32 * c + 32], b1r[:, c * P:(c + 1) * P], ident[0:EXPERTS, 0:EXPERTS])
                pe.transpose(PS[:, 4, P + 32 * c:P + 32 * c + 32], b2r[:, c * P:(c + 1) * P], ident[0:EXPERTS, 0:EXPERTS])
            for c in range(2):
                pe.transpose(PS[0:HALF, 4, 2 * P + 32 * c:2 * P + 32 * c + 32], gw[:, c * HALF:(c + 1) * HALF], ident[0:EXPERTS, 0:EXPERTS])
            pe.transpose(PS[0:BOT, 4, 320:352], b3r[:, :], ident[0:EXPERTS, 0:EXPERTS]).then_inc(sem("bias_t"), 1)
            pe.wait_ge(sem("wa_in"), 64)
            for j in range(2):
                for c in range(2):
                    ins = pe.matmul(PS[HALF:HALF + 1, 5 + j, 0:288], biasc[:, c:c + 1], wa[0:HALF, c, 288 * j:288 * (j + 1)],
                                    start=(c == 0), stop=(c == 1), tile_position=(0, HALF))
            ins.then_inc(sem("bias_w"), 1)
            pe.wait_ge(sem("tokwT"), 4)
            pe.wait_ge(sem("cls_xhat"), 1)
            for c in range(2):
                ins = pe.transpose(p_xT[:, c, :], xhat[0][:, c * HALF:(c + 1) * HALF], ident)
            ins.then_inc(sem("cls_xt"), 1)
            pe.wait_ge(sem("cls_xT"), 1)
            pe.wait_ge(sem("was"), 3)

            def project_in(src):
                for c in range(2):
                    kk = HALF + c
                    pe.matmul(p_qk, src[0:kk, c, :], was[0:kk, c, 0:2 * D], start=(c == 0), stop=(c == 1))
                for c in range(2):
                    kk = HALF + c
                    ins = pe.matmul(p_v, src[0:kk, c, :], was[0:kk, c, 2 * D:3 * D], start=(c == 0), stop=(c == 1))
                return ins
            project_in(xT[0]).then_inc(sem("cls_qkv"), 1)
            pe.wait_ge(sem("cls_qk"), 2)
            for c in range(2):
                ins = pe.transpose(p_qkT[:, 2 + c, :], qk[0][:, D + c * HALF:D + (c + 1) * HALF], ident)
            ins.then_inc(sem("cls_kt"), 1)

            pe.wait_ge(sem("vcls"), 1)
            pe.wait_ge(sem("cls_kT"), 1)
            pe.wait_ge(sem("biasT"), 4)
            pe.wait_ge(sem("was"), 3)

            def pixels(n):
                pe.wait_ge(sem("blocks"), n + 1)
                need(pe, "pix_a", n - 1)
                need(pe, "pix_v", n - 1)
                for j in range(GRID):
                    ins = pe.transpose(PS[:, 4 + 2 * (n % 2) + j // 4, (j % 4) * P:(j % 4 + 1) * P], blocks[n % 2][:, j, :], ident)
                ins.then_inc(sem("pix_t"), 1)

            def embed(n):
                g = n % GROUPS
                pe.wait_ge(sem("pix_a"), n + 1)
                pe.wait_ge(sem("pix_v"), n + 1)
                if g == 0 and n:
                    pe.wait_ge(sem("h"), GROUPS)
                for t in range(8):
                    ins = pe.matmul(PS[:, t // 2, (t % 2) * D:(t % 2 + 1) * D], pix[n % 2][:, t * P:(t + 1) * P], tokwT[:, g, :],
                                    start=(g == 0 and t % 2 == 0), stop=(g == GROUPS - 1), skip_group_check=True)
                ins.then_inc(sem("embed"), 1)

            pixels(0)
            for n in range(2 * GROUPS):
                if n + 1 < 2 * GROUPS:
                    pixels(n + 1)
                embed(n)

            def step(k, j, stages):
                a, b, c, d, e, f = (k - i for i in range(6))
                ja, jb, jc, jd, je, jf = (j - i for i in range(6))
                if "B" in stages:
                    pe.wait_ge(sem("qk"), b)
                    need(pe, "yT", d)
                    need(pe, "x2T", e)
                    for q in range(4):
                        ins = pe.transpose(p_qkT[:, q, :], qk[jb % 2][:, q * HALF:(q + 1) * HALF], ident)
                    ins.then_inc(sem("qk_t"), 1)
                if "A" in stages:
                    pe.wait_ge(sem("xhat"), a)
                    need(pe, "vblk", a - 1)
                    for q in range(2):
                        ins = pe.transpose(p_xT[:, q, :], xhat[ja % 2][:, q * HALF:(q + 1) * HALF], ident)
                    ins.then_inc(sem("x_t"), 1)
                if "C" in stages:
                    pe.wait_ge(sem("exp"), c)
                    need(pe, "pTa", c - 1)
                    need(pe, "yv", c - 1)
                    need(pe, "den", c - 1)
                    for q in range(HH):
                        dst = p_pTa[:, q, :] if q < 4 else p_pTb[:, q - 4, :]
                        ins = pe.transpose(dst, p_patch[jc % 2][:, q * P:(q + 1) * P], ident)
                    ins.then_inc(sem("p_t"), 1)
                if "A" in stages:
                    pe.wait_ge(sem("xT"), a)
                    need(pe, "rope_c", a - 1)
                    need(pe, "rope_s", a - 1)
                    project_in(xT[ja % 2]).then_inc(sem("qkv"), 1)
                if "B" in stages:
                    pe.wait_ge(sem("kblk0"), b)
                    pe.wait_ge(sem("kblk1"), b)
                    need(pe, "shifted", 3 * b - 3)
                    for half in range(2):
                        pe.matmul(PS[:, 5 + half, 0:HH * KEYS], identb[:, :], causal[:, :], start=True, stop=False, skip_group_check=True)
                        for b_ in range(2):
                            ins = pe.matmul(PS[b_ * PATCHES:(b_ + 1) * PATCHES, 5 + half, 0:HH * KEYS],
                                            qkT[jb % 2][:, half, b_ * PATCHES:(b_ + 1) * PATCHES],
                                            kblk[jb % 2][b_][:, half, :, :].rearrange("p g k -> p (g k)"),
                                            start=False, stop=True, skip_group_check=True)
                    ins.then_inc(sem("scores"), 1)
                if "D" in stages or "E" in stages:
                    if "B" in stages:
                        pe.wait_ge(sem("qkT"), b)
                    if "D" in stages:
                        pe.wait_ge(sem("y"), d + 1)
                        if "B" not in stages:
                            need(pe, "yT", d)
                        for q in range(2):
                            ins = pe.transpose(p_yT[:, q, :], y[jd % 2][:, q * HALF:(q + 1) * HALF], ident)
                    if "E" in stages:
                        pe.wait_ge(sem("x2"), e + 1)
                        if "B" not in stages:
                            need(pe, "x2T", e)
                            need(pe, "yT", min(d, NT) if isinstance(d, int) else d)
                        for q in range(2):
                            ins = pe.transpose(p_x2T[:, q, :], row[0][je % 4][:, q * HALF:(q + 1) * HALF], ident)
                    ins.then_inc(sem("yx_t"), 1)
                if "C" in stages:
                    pe.wait_ge(sem("pTa"), c)
                    pe.wait_ge(sem("pTb"), c)
                    pe.wait_ge(sem("vblk"), c)
                    for b_ in range(2):
                        for q in range(HH):
                            ins = pe.matmul(PS[b_ * PATCHES:(b_ + 1) * PATCHES, 4, 256 + 34 * q:256 + 34 * (q + 1)],
                                            pT[jc % 2][:, q, b_ * PATCHES:(b_ + 1) * PATCHES],
                                            vblk[jc % 4][:, b_, q, :, :].rearrange("p o d -> p (o d)"), start=True, stop=True)
                    ins.then_inc(sem("pv"), 1)
                if "D" in stages:
                    need(pe, "h1", d)
                if "F" in stages:
                    pe.wait_ge(sem("logits"), f + 1)
                    need(pe, "rankc", f)
                if "D" in stages:
                    pe.wait_ge(sem("yT"), d + 1)
                    if "E" not in stages:
                        need(pe, "h1", d)
                    for q in range(2):
                        kk = HALF + q
                        ins = pe.matmul(p_proj, yT[jd % 2][0:kk, q, :], wps[0:kk, q, :], start=(q == 0), stop=(q == 1))
                if "E" in stages:
                    pe.wait_ge(sem("x2T"), e + 1)
                    if "D" not in stages:
                        pe.wait_ge(sem("h1"), NT)
                    for q in range(2):
                        ins = pe.matmul(p_gate, x2T[je % 2][:, q, :], gwT[:, q, :], start=(q == 0), stop=(q == 1))
                if "F" in stages:
                    pe.wait_ge(sem("member"), f + 1)
                    need(pe, "before", f)
                    pe.matmul(p_rank, earlier[:, :], member[jf % 2][:, :], start=True, stop=False)
                    ins = pe.matmul(p_rank, onesb[:, :], before[:, :], start=False, stop=True)
                if "D" in stages or "E" in stages or "F" in stages:
                    ins.then_inc(sem("tail"), 1)

            pe.wait_ge(sem("h"), 2 * GROUPS)
            pe.wait_ge(sem("kcls"), 4)
            pe.wait_ge(sem("vones"), 8)
            pe.wait_ge(sem("tab"), 3)
            pe.wait_ge(sem("wps"), 2)
            pe.wait_ge(sem("before_zero"), 6)
            pipeline(pe, step)
            pe.wait_ge(sem("before"), NT)
            pe.wait_ge(sem("rankc"), NT)
            pe.matmul(p_rank, onesb[:, :], before[:, :], start=True, stop=True).then_inc(sem("counts"), 1)

            def tile(e, u, c, g):
                first = isinstance(c, int) and c == 0
                src = buf(u, c)
                slot = u % RING
                back = (u + RING - 1) % RING if first else slot
                pe.wait_ge(sem("xs_in"), 16 * g + 32)
                for q in range(2):
                    ins = pe.transpose(PS[0:HALF, 0, q * P:(q + 1) * P], src[:, q * HALF:(q + 1) * HALF], ident)
                ins.then_inc(sem("xe_t"), 1)
                pe.wait_ge(sem("result"), g + 1)
                for q in range(4):
                    pe.wait_ge(sem("g2"), 4 * g + q + 1)
                    ins = pe.matmul(PS[0:BOT, 7, 256:256 + P], W3[back][:, q, :], h2b[:, q, :], start=(q == 0), stop=(q == 3))
                ins.then_inc(sem("l3"), 1)
                if first:
                    pe.wait_ge(sem(f"w_in{u}"), (80 // RING) * (e - u) + 80)
                pe.wait_ge(sem("xeT"), g + 1)
                for m in range(4):
                    for q in range(2):
                        ins = pe.matmul(PS[:, L1_BANKS[m], 0:P], W1[slot][:, q, m * P:(m + 1) * P], xeT[:, q, :],
                                        start=(q == 0), stop=(q == 1))
                    ins.then_inc(sem("l1"), 1)
                pe.wait_ge(sem("z"), g + 1)
                pe.matmul(PS[:, 7, 0:D], zb[:, :], WL[back][:, :], start=True, stop=True).then_inc(sem("l4"), 1)
                for m in range(4):
                    for q in range(4):
                        if m == 0:
                            pe.wait_ge(sem("g1"), 4 * g + q + 1)
                        ins = pe.matmul(PS[:, L2_BANKS[m], 0:P], W2[slot][:, q, m * P:(m + 1) * P], h1b[:, q, :],
                                        start=(q == 0), stop=(q == 3))
                    ins.then_inc(sem("l2"), 1)

            pe.wait_ge(sem("zb_zero"), 2)
            pe.wait_ge(sem("last_zero"), 3)
            pe.sem_inc(sem("xe_t"), 1)
            experts(pe, tile)
            tiles = pe.value_load(start_i[0:1, EXPERTS + 1:EXPERTS + 2], min_val=EXPERTS, max_val=2 * EXPERTS)
            pe.wait_ge(sem("result"), tiles + 1)
            for q in range(4):
                pe.wait_ge(sem("g2"), 4 * tiles + q + 1)
                ins = pe.matmul(PS[0:BOT, 7, 256:256 + P], W3[RING - 1][:, q, :], h2b[:, q, :], start=(q == 0), stop=(q == 3))
            ins.then_inc(sem("l3"), 1)
            pe.wait_ge(sem("z"), tiles + 1)
            pe.matmul(PS[:, 7, 0:D], zb[:, :], WL[RING - 1][:, :], start=True, stop=True).then_inc(sem("l4"), 1)

        @block.vector
        def _(dve):
            init = sem("init")
            dve.memset(mhalf[:, :], -0.5).then_inc(init, 1)
            for t in (xT[0], xT[1], yT[0], yT[1]):
                dve.memset(t[HALF:HALF + 1, :, :], 1.0).then_inc(init, 1)
            for t in vblk:
                dve.memset(t[:, :, :, :, :], 0.0).then_inc(init, 1)
            dve.memset(onesb[:, :], 1.0).then_inc(init, 1)
            for t in WL:
                dve.memset(t[BOT:P, :], 0.0).then_inc(init, 1)
            dve.wait_ge(init, INIT)
            for t in vblk:
                dve.memset(t[0:PATCHES, :, :, 0, HD:HD + 1], 1.0).then_inc(sem("vones"), 1)
                dve.memset(t[PATCHES:P, :, :, 1, HD:HD + 1], 1.0).then_inc(sem("vones"), 1)
            dve.memset(before[:, :], 0.0).then_inc(sem("before_zero"), 1)
            dve.memset(cnt_i[:, :], 0).then_inc(sem("before_zero"), 1)
            dve.memset(ones1[:, :], 1.0).then_inc(sem("before_zero"), 1)
            dve.memset(start_i[:, :], 0).then_inc(sem("before_zero"), 1)
            dve.memset(b12T[:, EXPERTS, :], 0.0).then_inc(sem("before_zero"), 1)
            dve.memset(b3T[:, 0:1], 0.0).then_inc(sem("before_zero"), 1)
            dve.memset(zb[:, :], 0.0).then_inc(sem("zb_zero"), 1)
            dve.wait_ge(sem("zb_zero"), 1)
            dve.memset(zb[BOT:BOT + 1, :], 1.0).then_inc(sem("zb_zero"), 1)
            for c in range(2):
                for i in range(4):
                    dve.memset(row[c][i][:, D + 1:D + 2], 0.0).then_inc(sem("row_zero"), 1)
            dve.wait_ge(sem("cls_in"), 16)
            dve.bn_stats(st6[:, :], h[:, 0, :]).then_inc(sem("cls_st"), 1)
            dve.wait_ge(sem("cls_st"), 1)
            dve.bn_aggr(mv[:, 0, :], st6[:, :]).then_inc(sem("cls_st"), 1)
            dve.wait_ge(sem("cls_st"), 2)
            dve.tensor_scalar(ve1[:, 0:1], mv[:, 0, 1:2], EPS, None, ALU.add).then_inc(sem("cls_ve"), 1)
            dve.wait_ge(sem("wa_in"), 64)
            for c in range(2):
                dve.tensor_scalar(was[0:HALF, c, :], wa[0:HALF, c, :], scalec[:, c:c + 1], None, ALU.mult).then_inc(sem("was"), 1)
            dve.wait_ge(sem("bias_w"), 1)
            dve.tensor_tensor(was[HALF:HALF + 1, 1, :].rearrange("p (j n) -> p j n", j=2), PS[HALF:HALF + 1, 5:7, 0:288],
                              wa[HALF:HALF + 1, 1, :].rearrange("p (j n) -> p j n", j=2), ALU.add).then_inc(sem("was"), 1)
            dve.wait_ge(sem("cls_rs"), 1)
            dve.tensor_scalar(xhat[0][:, :], h[:, 0, :], mv[:, 0, 0:1], rs1[:, 0:1], ALU.subtract, ALU.mult).then_inc(sem("cls_xhat"), 1)
            dve.wait_ge(sem("wp_in"), 48)
            dve.tensor_scalar(wps[0:HALF, 0, :], wp[0:HALF, 0, :], rez[0:HALF, :], None, ALU.mult).then_inc(sem("wps"), 1)
            dve.tensor_scalar(wps[:, 1, :], wp[:, 1, :], rez[:, :], None, ALU.mult).then_inc(sem("wps"), 1)
            dve.wait_ge(sem("cls_qk"), 2)
            dve.wait_ge(sem("sink_in"), 16)
            dve.tensor_tensor(pvc[0][:, :], qk[0][:, 0:D], qk[0][:, D:2 * D], ALU.mult).then_inc(sem("cls_s"), 1)
            dve.wait_ge(sem("cls_s"), 1)
            dve.tensor_reduce(den[0][:, :], pvc[0][:, :].rearrange("p (h d) -> p h d", d=HD), AX.X, ALU.add).then_inc(sem("cls_s"), 1)
            dve.wait_ge(sem("cls_s"), 2)
            dve.tensor_tensor(mx[0][:, :], den[0][:, :], sinkb[:, :], ALU.max).then_inc(sem("cls_sub"), 1)
            dve.wait_ge(sem("cls_sub"), 1)
            dve.tensor_tensor(psum2[0][:, :], den[0][:, :], mx[0][:, :], ALU.subtract).then_inc(sem("cls_sub"), 1)
            dve.tensor_tensor(psum2[1][:, :], sinkb[:, :], mx[0][:, :], ALU.subtract).then_inc(sem("cls_sub"), 1)
            dve.wait_ge(sem("cls_kT"), 1)
            for i in range(2):
                for b_ in range(2):
                    dve.tensor_tensor(kblk[i][b_][:, :, :, PATCHES], qkT[0][:, 2:4, 0:1].to_broadcast([HALF, 2, HH]),
                                      cst[0:HALF, C_HEAD:C_HEAD + HH].unsqueeze(1).to_broadcast([HALF, 2, HH]), ALU.mult).then_inc(sem("kcls"), 1)
            dve.wait_ge(sem("cls_exp"), 2)
            dve.tensor_tensor(den[1][:, :], psum2[0][:, :], psum2[1][:, :], ALU.add).then_inc(sem("cls_y"), 1)
            dve.wait_ge(sem("cls_y"), 1)
            dve.reciprocal(rden[1][:, :], den[1][:, :]).then_inc(sem("cls_y"), 1)
            dve.wait_ge(sem("cls_y"), 2)
            dve.tensor_tensor(rden[0][:, :], rden[1][:, :], psum2[0][:, :], ALU.mult).then_inc(sem("cls_y"), 1)
            dve.wait_ge(sem("cls_y"), 3)
            dve.wait_ge(sem("vcls"), 1)
            dve.tensor_tensor(y[0][:, :].rearrange("p (h d) -> p h d", d=HD), vcls[:, :].rearrange("p (h d) -> p h d", d=HD),
                              rden[0][:, :].unsqueeze(2).to_broadcast([P, HEADS, HD]), ALU.mult).then_inc(sem("y"), 1)
            dve.wait_ge(sem("init"), INIT)
            dve.memset(WL[RING - 1][0:BOT, :], 0.0).then_inc(sem("last_zero"), 1)
            dve.memset(W3[RING - 1][:, :, :], 0.0).then_inc(sem("last_zero"), 1)
            dve.wait_ge(sem("tokw_t"), 4)
            dve.memset(h2b[:, :, :], 0.0).then_inc(sem("last_zero"), 1)

            def norm1_stats(n):
                dve.wait_ge(sem("h"), n)
                need(dve, "mv1", n - 1)
                dve.bn_stats(st6[:, :], h[:, n, :]).then_inc(sem("st1"), 1)
                dve.wait_ge(sem("st1"), n)
                dve.bn_aggr(mv[:, n, :], st6[:, :]).then_inc(sem("mv1"), 1)
                if n % 8 == 0:
                    dve.wait_ge(sem("mv1"), n)
                    dve.tensor_scalar(ve1[:, n - 7:n + 1], mv[:, n - 7:n + 1, 1], EPS, None, ALU.add).then_inc(sem("ve1"), 1)

            def norm1(n, j):
                need(dve, "x_t", n - 2)
                dve.tensor_scalar(xhat[j % 2][:, :], h[:, bass.ds(n, 1), :].rearrange("p a d -> p (a d)"), mv[:, bass.ds(n, 1), 0],
                                  rs1[:, bass.ds(n, 1)], ALU.subtract, ALU.mult).then_inc(sem("xhat"), 1)

            dve.wait_ge(sem("tokb_in"), 16)
            for hf in range(2):
                for g in range(GROUPS):
                    n = hf * GROUPS + g
                    dve.wait_ge(sem("pix_t"), n + 1)
                    need(dve, "embed", n - 1)
                    dve.tensor_copy(pix[n % 2][:, :].rearrange("p (t j) -> p j t", j=GRID)[:, 4:8, :],
                                    PS[:, 5 + 2 * (n % 2), :].rearrange("p (j t) -> p j t", j=4)).then_inc(sem("pix_v"), 1)
                    if hf:
                        norm1_stats(g + 1)
                dve.wait_ge(sem("embed"), (hf + 1) * GROUPS)
                for t in range(8):
                    n = 1 + 8 * hf + t
                    dve.tensor_tensor(h[:, n, :], PS[:, t // 2, (t % 2) * D:(t % 2 + 1) * D], tokb[:, :], ALU.add).then_inc(sem("h"), 1)
            def step(k, j, stages):
                a, b, c, d, e, f = (k - i for i in range(6))
                ja, jb, jc, jd, je, jf = (j - i for i in range(6))
                if "B" in stages:
                    dve.wait_ge(sem("qkT"), b)
                    need(dve, "scores", b - 2)
                    for half in range(2):
                        ins = dve.tensor_tensor(
                            kblk[jb % 2][0][:, half, :, 0:PATCHES],
                            qkT[jb % 2][:, 2 + half:3 + half, 0:PATCHES].to_broadcast([HALF, HH, PATCHES]),
                            cst[0:HALF, C_HEAD:C_HEAD + HH].unsqueeze(2).to_broadcast([HALF, HH, PATCHES]), ALU.mult)
                    ins.then_inc(sem("kblk0"), 1)
                if "C" in stages:
                    dve.wait_ge(sem("p_t"), c)
                    need(dve, "pv", c - 2)
                    dve.tensor_copy(pT[jc % 2][:, 4:6, :], p_pTb).then_inc(sem("pTb"), 1)
                if not isinstance(k, int) or k < TILES:
                    norm1(k + 1, j + 1)
                if "F" in stages:
                    dve.wait_ge(sem("tail"), f + 2)
                    lg, t8 = lgs[jf % 2][:, :], top8[jf % 2][:, :]
                    dve.wait_ge(sem("kept"), 2 * (f + 1))
                    dve.tensor_copy(lg, p_gate).then_inc(sem("logits"), 1)
                    dve.wait_ge(sem("logits"), f + 1)
                    alone(dve)
                    dve.max(t8, lg).then_inc(sem("top8"), 1)
                    dve.wait_ge(sem("top8"), f + 1)
                    alone(dve)
                    dve.max_index(idx8[jf % 2][:, :], t8, lg).then_inc(sem("idx8"), 1)
                    dve.wait_ge(sem("idx8"), f + 1)
                    dve.tensor_copy(idxf[jf % 2][:, :], idx8[jf % 2][:, 0:2]).then_inc(sem("idxf"), 1)
                    dve.wait_ge(sem("idxf"), f + 1)
                    for ch in range(2):
                        dve.tensor_scalar(pick[jf % 2][:, ch, :], iota, idxf[jf % 2][:, ch:ch + 1],
                                          cst[:, bass.ds(C_KEEP + f, 1)], ALU.is_equal, ALU.mult).then_inc(sem("pick"), 1)
                    dve.wait_ge(sem("pick"), 2 * f + 2)
                    dve.tensor_tensor(member[jf % 2][:, :], pick[jf % 2][:, 0, :], pick[jf % 2][:, 1, :], ALU.add).then_inc(sem("member"), 1)
                if "A" in stages:
                    dve.wait_ge(sem("qkv"), a)
                    need(dve, "qk", a - 2)
                    src = p_qk.rearrange("p (w h d) -> p w h d", w=2, d=HD)
                    dve.tensor_tensor(rope_c[ja % 2][:, :].rearrange("p (w h d) -> p w h d", w=2, d=HD), src,
                                      cst[:, C_ROPE_C:C_ROPE_C + 2 * HD].rearrange("p (w a d) -> p w a d", w=2, a=1).to_broadcast([P, 2, HEADS, HD]),
                                      ALU.mult).then_inc(sem("rope_c"), 1)
                    for w in range(2):
                        ins = dve.tensor_tensor(
                            rope_s[ja % 2][:, w * D:(w + 1) * D].rearrange("p (h d o) -> p h d o", h=HEADS, o=2),
                            p_qk[:, w * D:(w + 1) * D].rearrange("p (h d o) -> p h d o", h=HEADS, o=2)[:, :, :, ::-1],
                            cst[:, C_ROPE_S + w * HD:C_ROPE_S + (w + 1) * HD].rearrange("p (a d o) -> p a d o", a=1, o=2).to_broadcast([P, HEADS, HD // 2, 2]),
                            ALU.mult)
                    ins.then_inc(sem("rope_s"), 1)
                if "B" in stages:
                    dve.wait_ge(sem("scores"), b)
                    dve.tensor_reduce(mx[jb % 2][:, :].rearrange("p (c g) -> p c g", c=2), p_s, AX.X, ALU.max).then_inc(sem("rowmax"), 1)
                    dve.wait_ge(sem("rowmax"), b)
                    dve.tensor_tensor(mx[jb % 2][:, :], mx[jb % 2][:, :], sinkb[:, :], ALU.max).then_inc(sem("max"), 1)
                    dve.wait_ge(sem("max"), b)
                    need(dve, "p_t", b - 2)
                    need(dve, "pvc", b - 2)
                    need(dve, "psum2", b - 2)
                    dve.tensor_tensor(p_sink[jb % 2], sinkb[:, :], mx[jb % 2][:, :], ALU.subtract).then_inc(sem("shifted"), 1)
                    dve.tensor_tensor(p_class[jb % 2].rearrange("p (c g) -> p c g", c=2), p_s[:, :, :, PATCHES],
                                      mx[jb % 2][:, :].rearrange("p (c g) -> p c g", c=2), ALU.subtract).then_inc(sem("shifted"), 1)
                    dve.tensor_tensor(p_patch[jb % 2].rearrange("p (c g k) -> p c g k", c=2, g=HH), p_s[:, :, :, 0:PATCHES],
                                      mx[jb % 2][:, :].rearrange("p (c g a) -> p c g a", c=2, a=1).to_broadcast([P, 2, HH, PATCHES]),
                                      ALU.subtract).then_inc(sem("shifted"), 1)
                if "C" in stages:
                    dve.wait_ge(sem("pv"), c)
                    dve.wait_ge(sem("psum2"), c)
                    dve.tensor_tensor(den[jc % 2][:, :], psum2[jc % 2][:, :], p_y[:, :, HD], ALU.add).then_inc(sem("den"), 1)
                    dve.wait_ge(sem("pvc"), c)
                    dve.tensor_tensor(yv[jc % 2][:, :].rearrange("p (h d) -> p h d", d=HD), pvc[jc % 2][:, :].rearrange("p (h d) -> p h d", d=HD),
                                      p_y[:, :, 0:HD], ALU.add).then_inc(sem("yv"), 1)
                    dve.wait_ge(sem("den"), c)
                    dve.reciprocal(rden[jc % 2][:, :], den[jc % 2][:, :]).then_inc(sem("rden"), 1)
                    dve.wait_ge(sem("rden"), c)
                    dve.wait_ge(sem("yv"), c)
                    need(dve, "yx_t", c - 1)
                    dve.tensor_tensor(y[jc % 2][:, :].rearrange("p (h d) -> p h d", d=HD), yv[jc % 2][:, :].rearrange("p (h d) -> p h d", d=HD),
                                      rden[jc % 2][:, :].unsqueeze(2).to_broadcast([P, HEADS, HD]), ALU.mult).then_inc(sem("y"), 1)
                if "D" in stages:
                    hd_ = h[:, bass.ds(d, 1), :].rearrange("p a d -> p (a d)")
                    dve.wait_ge(sem("tail"), d + 1)
                    dve.tensor_tensor(hd_, hd_, p_proj, ALU.add).then_inc(sem("h1"), 1)
                    dve.wait_ge(sem("h1"), d + 1)
                    need(dve, "mv2", d)
                    alone(dve)
                    dve.bn_stats(st6b[:, :], hd_).then_inc(sem("st2"), 1)
                    dve.wait_ge(sem("st2"), d + 1)
                    need(dve, "x2", d - 1)
                    alone(dve)
                    dve.bn_aggr(mv2[jd % 2][:, 0:2], st6b[:, :]).then_inc(sem("mv2"), 1)
                    dve.wait_ge(sem("mv2"), d + 1)
                    need(dve, "rs2", d - 1)
                    dve.tensor_scalar(mv2[jd % 2][:, 2:3], mv2[jd % 2][:, 1:2], EPS, None, ALU.add).then_inc(sem("ve2"), 1)
                if "F" in stages:
                    dve.wait_ge(sem("tail"), f + 3)
                    dve.tensor_tensor(before[:, :], before[:, :], member[jf % 2][:, :], ALU.add).then_inc(sem("before"), 1)
                    dve.tensor_tensor(rankc[jf % 2][:, :], p_rank, ecap, ALU.add).then_inc(sem("rankc"), 1)
                    dve.wait_ge(sem("rankc"), f + 1)
                    dve.tensor_tensor(slp[jf % 2][:, :, :], pick[jf % 2][:, :, :], rankc[jf % 2][:, :].unsqueeze(1).to_broadcast([P, 2, EXPERTS]),
                                      ALU.mult).then_inc(sem("slp"), 1)
                    dve.wait_ge(sem("slp"), f + 1)
                    dve.tensor_reduce(slf[jf % 2][:, :], slp[jf % 2][:, :, :], AX.X, ALU.add).then_inc(sem("slf"), 1)
                    dve.wait_ge(sem("slf"), f + 1)
                    scattered(dve, f - 3, jf - 3)
                    dve.tensor_tensor(slu[jf % 4][:, :], slf[jf % 2][:, :],
                                      cst[:, bass.ds(C_SPARE + 2 * f, 2)], ALU.add).then_inc(sem("slot"), 1)
                if "D" in stages:
                    dve.wait_ge(sem("rs2"), d + 1)
                    scattered(dve, d - 4, jd - 4)
                    dve.tensor_scalar(row[0][jd % 4][:, 0:D], hd_, mv2[jd % 2][:, 0:1], rs2[jd % 2][:, :],
                                      ALU.subtract, ALU.mult).then_inc(sem("x2"), 1)

            dve.wait_ge(sem("rs1"), 1)
            norm1(1, 1)
            for n in range(9, NT):
                norm1_stats(n)
            dve.wait_ge(sem("rs1"), 2)
            dve.wait_ge(sem("kcls"), 4)
            dve.wait_ge(sem("row_zero"), 8)
            dve.wait_ge(sem("before_zero"), 6)
            pipeline(dve, step)

            dve.wait_ge(sem("counts"), 1)
            dve.tensor_copy(cnt[:, :], p_rank[0:1, :]).then_inc(sem("cnt"), 1)
            dve.wait_ge(sem("cnt"), 1)
            dve.tensor_copy(cnt_i[0:1, 0:EXPERTS], cnt[:, :]).then_inc(sem("tables"), 1)
            dve.tensor_tensor(over[:, :, :], cnt[:, :].unsqueeze(2).to_broadcast([1, EXPERTS, CHUNKS - 1]),
                              cst[0:1, C_STEP:C_STEP + CHUNKS - 1].unsqueeze(1).to_broadcast([1, EXPERTS, CHUNKS - 1]), ALU.is_gt).then_inc(sem("over"), 1)
            dve.wait_ge(sem("over"), 1)
            dve.tensor_reduce(ntile[:, :], over[:, :, :], AX.X, ALU.add).then_inc(sem("over"), 1)
            dve.memset(startf[:, 0:1], 0.0).then_inc(sem("over"), 1)
            dve.wait_ge(sem("over"), 3)
            dve.tensor_tensor_scan(startf[:, 1:EXPERTS + 1], ones1[:, :], ntile[:, :], 0.0, ALU.add, ALU.add).then_inc(sem("over"), 1)
            dve.wait_ge(sem("over"), 4)
            dve.tensor_copy(start_i[:, 1:EXPERTS + 2], startf[:, :]).then_inc(sem("tables"), 1)

            dve.wait_ge(sem("kept"), 4 + 2 * NT)
            dve.tensor_tensor(gmx[:, :, :], logits[:, :, :], top2[:, :, 0:1].to_broadcast([P, NT, EXPERTS]), ALU.subtract).then_inc(sem("g_sub"), 1)
            dve.tensor_tensor(gs2[:, :, :], top2[:, :, 0:2], top2[:, :, 0:1].to_broadcast([P, NT, 2]), ALU.subtract).then_inc(sem("g_sub"), 1)
            dve.wait_ge(sem("g_exp"), 2)
            dve.tensor_reduce(gz[:, :], gmx[:, :, :], AX.X, ALU.add).then_inc(sem("g_w"), 1)
            dve.wait_ge(sem("g_w"), 1)
            dve.reciprocal(gri[:, :], gz[:, :]).then_inc(sem("g_w"), 1)
            dve.wait_ge(sem("g_w"), 2)
            dve.tensor_tensor(wgt[:, :, :], gs2[:, :, :], gri[:, :].unsqueeze(2).to_broadcast([P, NT, 2]), ALU.mult).then_inc(sem("g_w"), 1)
            dve.wait_ge(sem("g_w"), 3)
            dve.scalar_tensor_tensor(gden[:, :], wgt[:, :, 0], 1e-20, wgt[:, :, 1], ALU.add, ALU.add).then_inc(sem("g_w"), 1)
            dve.wait_ge(sem("g_w"), 4)
            dve.reciprocal(gz[:, :], gden[:, :]).then_inc(sem("g_w"), 1)
            dve.wait_ge(sem("g_w"), 5)
            dve.tensor_tensor(wgt[:, :, :], wgt[:, :, :], gz[:, :].unsqueeze(2).to_broadcast([P, NT, 2]), ALU.mult).then_inc(sem("g_w"), 1)

            dve.wait_ge(sem("pad_set"), 2)
            dve.wait_ge(sem("zb_zero"), 2)
            dve.wait_ge(sem("biasT"), 4)
            dve.sem_inc(sem("dest"), 1)
            dve.sem_inc(sem("result"), 1)

            def z_out(column, g):
                dve.wait_ge(sem("l3"), g + 1)
                dve.tensor_scalar(zb[0:BOT, :], PS[0:BOT, 7, 256:256 + P], b3T[:, bass.ds(column, 1)], None, ALU.add).then_inc(sem("z"), 1)

            def result_out(g):
                dve.wait_ge(sem("sent"), g + 1)
                dve.wait_ge(sem("dest"), g + 1)
                dve.tensor_copy(dest_old[:, :], dest_new[:, :]).then_inc(sem("dest_old"), 1)
                dve.wait_ge(sem("l4"), g + 1)
                dve.tensor_copy(yb[:, :], PS[:, 7, 0:D]).then_inc(sem("result"), 1)
                dve.wait_ge(sem("dest_old"), g + 1)

            def tile(e, u, c, g):
                first = isinstance(c, int) and c == 0
                dve.wait_ge(sem("xe_t"), g + 2)
                dve.tensor_copy(xeT[:, :, :], PS[0:HALF, 0, 0:2 * P].rearrange("p (c t) -> p c t", c=2)).then_inc(sem("xeT"), 1)
                z_out(e if first else e + 1, g)
                result_out(g)
                dve.tensor_copy(dest_new[:, :], buf(u, c)[:, D:D + 1].bitcast(u32)).then_inc(sem("dest"), 1)

            def biases(e, u):
                dve.tensor_copy(bcur[(u + 1) % 2][:, :], b12T[:, bass.ds(e + 1, 1), :].rearrange("p a c -> p (a c)")).then_inc(sem("bcur"), 1)

            dve.tensor_copy(bcur[0][:, :], b12T[:, 0, :]).then_inc(sem("bcur"), 1)
            experts(dve, tile, then=biases)
            tiles = dve.value_load(start_i[0:1, EXPERTS + 1:EXPERTS + 2], min_val=EXPERTS, max_val=2 * EXPERTS)
            z_out(EXPERTS, tiles)
            result_out(tiles)

            dve.wait_ge(sem("g_w"), 6)
            for n in range(NT):
                i, turn = n % OUT_RING, n // OUT_RING
                rows = IMAGES if n == 0 else P
                if n == 0:
                    dve.wait_ge(sem("res_in0"), 32)
                else:
                    dve.wait_ge(sem(f"res_in{i}"), 16 * turn + (32 if i == 0 else 16))
                need(dve, "o2", n - OUT_RING + 1)
                dve.scalar_tensor_tensor(o1[i][0:rows, :], res[i][0:rows, 0, :], wgt[0:rows, n, 0:1], h[0:rows, n, :], ALU.mult, ALU.add).then_inc(sem("o1"), 1)
                dve.wait_ge(sem("o1"), n + 1)
                if turn:
                    dve.wait_ge(sem(f"out{i}"), 32 * turn - (16 if i == 0 else 0))
                dve.scalar_tensor_tensor(o2[i][0:rows, :], res[i][0:rows, 1, :], wgt[0:rows, n, 1:2], o1[i][0:rows, :], ALU.mult, ALU.add).then_inc(sem("o2"), 1)


def constants():
    import numpy as np
    t = np.zeros((P, C_END), np.float32)
    p = np.arange(P)
    t[:, C_ID:C_ID + P] = np.eye(P)
    t[:, C_TRI:C_TRI + P] = p[:, None] < p[None, :]
    freqs = np.float32(1.0) / np.power(np.float32(10000.0), np.arange(0, HD, 2, dtype=np.float32) / np.float32(HD))
    ang = (1 + p % PATCHES).astype(np.float32)[:, None] * freqs.astype(np.float32)[None, :]
    cos, sin = np.cos(ang), np.sin(ang)
    for w, scale in enumerate((HD ** -0.5, 1.0)):
        t[:, C_ROPE_C + w * HD:C_ROPE_C + (w + 1) * HD] = np.repeat(cos, 2, 1) * scale
        t[:, C_ROPE_S + w * HD:C_ROPE_S + (w + 1) * HD] = np.stack([-sin, sin], -1).reshape(P, HD) * scale
    mask = np.zeros((P, HH, KEYS), np.float32)
    mask[:, :, 0:PATCHES] = np.where(np.arange(PATCHES)[None, :] > (p % PATCHES)[:, None], MASKED, 0.0)[:, None, :]
    t[:, C_CAUSAL:C_CAUSAL + HH * KEYS] = mask.reshape(P, -1)
    t[:, C_IOTA:C_IOTA + EXPERTS] = np.arange(EXPERTS)
    t[:, C_ECAP:C_ECAP + EXPERTS] = np.arange(EXPERTS) * CAP
    t[:, C_STEP:C_STEP + CHUNKS - 1] = P * np.arange(1, CHUNKS)
    t[:HALF, C_HEAD:C_HEAD + HH] = (p[:HALF] // HD)[:, None] == np.arange(HH)[None, :]
    t[:, C_KEEP:C_KEEP + NT] = 1.0
    t[1:, C_KEEP] = 0.0
    t[1:, C_SPARE] = SPARE0 + p[1:]
    t[1:, C_SPARE + 1] = SPARE1 + p[1:]
    t[:, C_PADID] = RESULTS + p
    for ch in range(2):
        t[:, C_DEST + ch * NT:C_DEST + (ch + 1) * NT] = (np.arange(NT)[None, :] * P + p[:, None]) * 2 + ch
    return t


_INS = ['x', 'cls_tok', 'L0_tok_w', 'L0_tok_b', 'L0_attn_norm_scale', 'L0_attn_norm_bias', 'L0_attn_W_attn', 'L0_attn_b_attn',
        'L0_attn_W_proj', 'L0_attn_b_proj', 'L0_attn_sinks', 'L0_attn_rezero', 'L0_ffn_gate_w', 'L0_ffn_W1', 'L0_ffn_b1',
        'L0_ffn_W2', 'L0_ffn_b2', 'L0_ffn_W3', 'L0_ffn_b3', 'L0_ffn_Wl', 'L0_ffn_bl']


def kernel(**inputs):
    import numpy as _np
    import concourse.bacc as _bacc
    from concourse import mybir as _mybir
    from concourse.bass_utils import run_bass_kernel_spmd as _run

    nc = _bacc.Bacc("TRN2", target_bir_lowering=False, num_devices=1)
    arrays, args = {}, []
    for name in _INS + ["table"]:
        a = constants() if name == "table" else _np.ascontiguousarray(inputs[name])
        arrays[f"in_{name}_dram"] = a
        args.append(nc.dram_tensor(f"in_{name}_dram", a.shape, _mybir.dt.from_np(a.dtype), kind="ExternalInput").ap())
    args.append(nc.dram_tensor("out_0_dram", (IMAGES, KEYS, D), _mybir.dt.float32, kind="ExternalOutput").ap())
    vit_moe_kernel(nc, *args)
    r = _run(nc, [arrays], core_ids=[0])
    return r.results[0]["out_0_dram"]
```

```python
import concourse.bass as bass
from concourse import mybir
from contextlib import ExitStack

IMAGES, SIDE, PATCH = 32, 256, 32
D = 192
GRID = SIDE // PATCH
PATCHES = GRID * GRID
DP = PATCH * PATCH
HEADS, HD = 12, 16
EXPERTS, HID, BOT = 32, 512, 64
P = 128
HALF = D // 2
HH = HEADS // 2
TILE_IMAGES = P // PATCHES
TILES = IMAGES // TILE_IMAGES
NT = TILES + 1
GROUPS = DP // P
ROWS = P // PATCH
KEYS = PATCHES + 1
EPS = 1e-5
MASKED = -1e30

TOKENS = IMAGES * PATCHES + 1
CHUNKS = -(-TOKENS // P)
CAP = TOKENS + P
ROW = D + 2
SPARE2 = EXPERTS * CAP
SPARE0 = SPARE2 + CAP
SPARE1 = SPARE0 + P
SLOTS = SPARE1 + P
WIDE = 2 * HALF
TILE_STEPS = [WIDE, P + WIDE, 3 * P] + [P * c for c in range(4, CHUNKS)]
WIDE_STEPS = [P, WIDE, 2 * P, P + WIDE]
PACK_WIDE, PACK_COUNT = 128, 256
RESULTS = NT * P * 2
LOOP_START, LOOP_TURNS = 8, 2
LOOP_END = LOOP_START + 4 * LOOP_TURNS
OUT_RING = 6
RING = 4

C_ID, C_TRI, C_ROPE_C, C_ROPE_S = 0, P, 2 * P, 2 * P + 2 * HD
C_CAUSAL = C_ROPE_S + 2 * HD
C_IOTA = C_CAUSAL + HH * KEYS
C_ECAP = C_IOTA + EXPERTS
C_STEP = C_ECAP + EXPERTS
C_WIDE = C_STEP + CHUNKS - 1
C_HEAD = C_WIDE + 8
C_KEEP = C_HEAD + HH
C_SPARE = C_KEEP + NT
C_PADID = C_SPARE + 2 * NT
C_DEST = C_PADID + 1
C_END = C_DEST + 2 * NT


def vit_moe_kernel(nc, x, cls_tok, tok_w, tok_b, n_scale, n_bias, w_attn, b_attn, w_proj, b_proj,
                   sinks, rezero, gate_w, w1, b1, w2, b2, w3, b3, wl, bl, table, out):
    f32, bf16 = mybir.dt.float32, mybir.dt.bfloat16
    i32, u32 = mybir.dt.int32, mybir.dt.uint32
    ALU, ACT, AX = mybir.AluOpType, mybir.ActivationFunctionType, mybir.AxisListType

    slots = nc.dram_tensor("slots", (SLOTS, ROW), f32).ap()
    results = nc.dram_tensor("results", (RESULTS + P, D), f32).ap()
    x_v = x.rearrange("b c (i g r) w -> (b c i) g (r w)", i=GRID, g=GROUPS)
    res_v = results[0:RESULTS, :].rearrange("(n p k) d -> n p (k d)", p=P, k=2)

    ctx = ExitStack()
    with ctx:
        def sb(name, shape, dt=f32):
            return ctx.enter_context(nc.sbuf_tensor(name, shape, dt))

        sems = {}

        def sem(name):
            if name not in sems:
                sems[name] = ctx.enter_context(nc.semaphore(name))
            return sems[name]

        def need(eng, name, value):
            if not isinstance(value, int) or value > 0:
                eng.wait_ge(sem(name), value)

        def alone(eng):
            eng.nop(nofuse=True)

        cst = sb("cst", [P, C_END])
        ident = cst[:, C_ID:C_ID + P]
        causal = sb("causal", [P, HH * KEYS], bf16)
        identb = sb("identb", [P, P], bf16)
        earlier = sb("earlier", [P, P], bf16)
        onesb = sb("onesb", [P, P], bf16)
        iota = cst[:, C_IOTA:C_IOTA + EXPERTS]
        ecap = cst[:, C_ECAP:C_ECAP + EXPERTS]
        scratch = sb("scratch", [P, 2 * DP])
        tokw = scratch[0:HALF, :].rearrange("p (c n) -> p c n", c=2)
        h1b = scratch[:, 0:4 * WIDE].rearrange("p (c t) -> p c t", c=4)
        h2b = scratch[:, 4 * WIDE:8 * WIDE].rearrange("p (c t) -> p c t", c=4)
        xeT = scratch[0:HALF, 8 * WIDE:10 * WIDE]
        tokwT = sb("tokwT", [P, GROUPS, D])
        tokb = sb("tokb", [P, D])
        scalec = sb("scalec", [HALF, 2])
        biasc = sb("biasc", [HALF, 2])
        wa = sb("wa", [HALF + 1, 2, 3 * D])
        was = sb("was", [HALF + 1, 2, 3 * D])
        wp = sb("wp", [HALF + 1, 2, D])
        wps = sb("wps", [HALF + 1, 2, D])
        rez = sb("rez", [HALF + 1, 1])
        sinkb = sb("sinkb", [P, HEADS])
        gw = sb("gw", [EXPERTS, D])
        gwT = sb("gwT", [HALF, 2, EXPERTS])
        b3r = sb("b3r", [EXPERTS, BOT])
        b12T = sb("b12T", [P, EXPERTS + 1, 8])
        bcur = [sb(f"bcur{i}", [P, 8]) for i in range(2)]
        b3T = sb("b3T", [BOT, EXPERTS + 1])
        raw = [sb(f"raw{i}", [P, ROWS * SIDE]) for i in range(4)]
        pix = [sb(f"pix{i}", [P, P * GRID]) for i in range(2)]
        b1r = pix[0][0:EXPERTS, 0:HID]
        b2r = pix[0][0:EXPERTS, HID:2 * HID]
        h = sb("h", [P, NT, D])
        st6 = sb("st6", [P, 6])
        mv = sb("mv", [P, NT, 2])
        ve1 = sb("ve1", [P, NT])
        rs1 = sb("rs1", [P, NT])
        mhalf = sb("mhalf", [P, NT])
        xhat = [sb(f"xhat{i}", [P, D]) for i in range(2)]
        xT = [sb(f"xT{i}", [HALF + 1, 2, P]) for i in range(2)]
        rope_c = [sb(f"ropec{i}", [P, 2 * D]) for i in range(2)]
        rope_s = [sb(f"ropes{i}", [P, 2 * D]) for i in range(2)]
        qk = [sb(f"qk{i}", [P, 2 * D]) for i in range(2)]
        qkT = [sb(f"qkT{i}", [HALF, 4, P]) for i in range(2)]
        kblk = [[sb(f"kblk{i}{b}", [HALF, 2, HH, KEYS]) for b in range(2)] for i in range(2)]
        vblk = [sb(f"vblk{i}", [P, 2, HH, 2, HD + 1]) for i in range(4)]
        mx = [sb(f"mx{i}", [P, HEADS]) for i in range(2)]
        probs = [sb(f"probs{i}", [P, HEADS * (PATCHES + 2)]) for i in range(2)]
        p_patch = [t[:, 0:HEADS * PATCHES] for t in probs]
        p_class = [t[:, HEADS * PATCHES:HEADS * KEYS] for t in probs]
        p_sink = [t[:, HEADS * KEYS:HEADS * (KEYS + 1)] for t in probs]
        pT = [sb(f"pT{i}", [P, HH, P]) for i in range(2)]
        vcls = sb("vcls", [P, D])
        pvc = [sb(f"pvc{i}", [P, D]) for i in range(2)]
        psum2 = [sb(f"psum2{i}", [P, HEADS]) for i in range(2)]
        den = [sb(f"den{i}", [P, HEADS]) for i in range(2)]
        rden = [sb(f"rden{i}", [P, HEADS]) for i in range(2)]
        yv = [sb(f"yv{i}", [P, D]) for i in range(2)]
        y = [sb(f"y{i}", [P, D]) for i in range(2)]
        yT = [sb(f"yT{i}", [HALF + 1, 2, P]) for i in range(2)]
        st6b = sb("st6b", [P, 6])
        mv2 = [sb(f"mv2{i}", [P, 3]) for i in range(2)]
        rs2 = [sb(f"rs2{i}", [P, 1]) for i in range(2)]
        row = [[sb(f"row{c}{i}", [P, ROW]) for i in range(4)] for c in range(2)]
        x2T = [sb(f"x2T{i}", [HALF, 2, P]) for i in range(2)]
        logits = sb("logits", [P, NT, EXPERTS])
        top2 = sb("top2", [P, NT, 2])
        lgs = [sb(f"lgs{i}", [P, EXPERTS]) for i in range(2)]
        top8 = [sb(f"top8{i}", [P, 8]) for i in range(2)]
        idx8 = [sb(f"idx8{i}", [P, 8], u32) for i in range(2)]
        idxf = [sb(f"idxf{i}", [P, 2]) for i in range(2)]
        pick = [sb(f"pick{i}", [P, 2, EXPERTS]) for i in range(2)]
        member = [sb(f"member{i}", [P, EXPERTS], bf16) for i in range(2)]
        before = sb("before", [P, EXPERTS], bf16)
        rankc = [sb(f"rankc{i}", [P, EXPERTS]) for i in range(2)]
        slp = [sb(f"slp{i}", [P, 2, EXPERTS]) for i in range(2)]
        slf = [sb(f"slf{i}", [P, 2]) for i in range(2)]
        sls = [sb(f"sls{i}", [P, 2]) for i in range(2)]
        slu = [sb(f"slu{i}", [P, 2], u32) for i in range(4)]
        wgt = sb("wgt", [P, NT, 2])
        gmx = sb("gmx", [P, NT, EXPERTS])
        gz = sb("gz", [P, NT])
        gri = sb("gri", [P, NT])
        gs2 = sb("gs2", [P, NT, 2])
        gden = sb("gden", [P, NT])
        cnt = sb("cnt", [1, EXPERTS])
        over = sb("over", [1, EXPERTS, CHUNKS - 1])
        ntile = sb("ntile", [1, EXPERTS])
        ones1 = sb("ones1", [1, EXPERTS])
        over4 = sb("over4", [1, EXPERTS, 4])
        widef = sb("widef", [1, EXPERTS])
        startf = sb("startf", [1, EXPERTS + 1])
        cnt_i = sb("cnt_i", [1, EXPERTS + 1], i32)
        packedf = sb("packedf", [1, EXPERTS + 1])
        packed_i = sb("packed_i", [1, EXPERTS + 1], i32)
        widesf = sb("widesf", [1, EXPERTS])
        wides_i = sb("wides_i", [1, EXPERTS + 1], i32)
        start_i = sb("start_i", [1, EXPERTS + 2], i32)
        W1 = [sb(f"W1_{i}", [HALF, 2, HID]) for i in range(RING)]
        W2 = [sb(f"W2_{i}", [P, 4, HID]) for i in range(RING)]
        blocks = [W2[RING - 1][:, 2 * i:2 * i + 2, :].rearrange("p a (j n) -> p (a j) n", j=4) for i in range(2)]
        W3 = [sb(f"W3_{i}", [P, 4, BOT]) for i in range(RING)]
        WL = [sb(f"WL_{i}", [P, D]) for i in range(RING)]
        pad = sb("pad", [P, ROW])
        xs = [[raw[2 * a + b][:, 0:2 * ROW] for b in range(2)] for a in range(2)]
        yb = raw[0][:, 2 * ROW:2 * ROW + 2 * D]
        zb = sb("zb", [P, WIDE])
        dest_new = sb("dest_new", [P, 2], u32)
        dest_old = sb("dest_old", [P, 2], u32)
        end = [W2[i // 2][:, 2 * (i % 2):2 * (i % 2) + 2, :].rearrange("p a n -> p (a n)") for i in range(OUT_RING)]
        res_flat = [t[:, 0:2 * D] for t in end]
        res = [t.rearrange("p (k d) -> p k d", k=2) for t in res_flat]
        o1 = [t[:, 2 * D:3 * D] for t in end]
        o2 = [t[:, 3 * D:4 * D] for t in end]

        PS = ctx.enter_context(nc.psum_tensor("PS", [P, 8, 512], f32))
        p_xT = PS[0:HALF, 0, 0:256].rearrange("p (c t) -> p c t", c=2)
        p_v = PS[:, 0, 256:256 + D]
        p_qkT = PS[0:HALF, 1, :].rearrange("p (c t) -> p c t", c=4)
        p_yT = PS[0:HALF, 1, 0:256].rearrange("p (c t) -> p c t", c=2)
        p_x2T = PS[0:HALF, 1, 256:512].rearrange("p (c t) -> p c t", c=2)
        p_qk = PS[:, 2, 0:2 * D]
        p_pTa = PS[:, 3, :].rearrange("p (g t) -> p g t", g=4)
        p_pTb = PS[:, 4, 0:256].rearrange("p (g t) -> p g t", g=2)
        p_y = PS[:, 4, 256:256 + HEADS * (HD + 1)].rearrange("p (h d) -> p h d", d=HD + 1)
        p_s = PS[:, 5:7, 0:HH * KEYS].rearrange("p c (g k) -> p c g k", k=KEYS)
        p_proj = PS[:, 7, 0:D]
        p_gate = PS[:, 7, D:D + EXPERTS]
        p_rank = PS[:, 7, D + EXPERTS:D + 2 * EXPERTS]

        L1_BANKS, L2_BANKS = (1, 2, 3, 4), (5, 6, 1, 2)
        p_z = PS[0:BOT, 4, :]

        INIT = 14

        block = ctx.enter_context(nc.Block())

        def scattered(eng, n, jn):
            if not isinstance(n, int) or n >= 0:
                for ch in range(2):
                    eng.wait_ge(sem(f"scattered{ch}{jn % 4}"), 4 * (n - jn % 4) + 16)

        def pipeline(eng, step):
            def stages(k):
                s = {c for i, c in enumerate("ABC") if 1 <= k - i < NT}
                return s | {c for i, c in enumerate("DEFG", 3) if 0 <= k - i < NT}
            for k in range(1, LOOP_START):
                step(k, k, stages(k))
            with eng.Fori(0, LOOP_TURNS) as q:
                for j in range(4):
                    step(4 * q + LOOP_START + j, LOOP_START + j, set("ABCDEFG"))
            for k in range(LOOP_END, NT + 6):
                step(k, k, stages(k))

        def walk(eng, more, s, tile, wide):
            with eng.If(more(WIDE)):
                tile(0, s, P, wide)
                with eng.If(more(P + WIDE)):
                    tile(1, s + 1, P, False)
                    tile(2, s + 2, P, False)
                    with eng.If(more(3 * P)):
                        with eng.Fori(3, CHUNKS) as c:
                            with eng.If(more(c * P)):
                                tile(c, s + c, P, False)
                            eng.nop()
                    eng.nop()
                with eng.Else():
                    with eng.If(more(2 * P)):
                        tile(1, s + 1, WIDE, False)
                    with eng.Else():
                        tile(1, s + 1, P, False)
                    eng.nop()
                eng.nop()
            with eng.Else():
                with eng.If(more(P)):
                    tile(0, s, WIDE, wide)
                with eng.Else():
                    tile(0, s, P, wide)
                eng.nop()
            eng.nop()

        def experts(eng, tile, enter=None, layouts=True):
            eng.wait_ge(sem("tables"), 3)
            with eng.Fori(0, EXPERTS // RING) as q:
                for u in range(RING):
                    e = RING * q + u
                    v = packed(eng, e)
                    s = eng.snap(v & (PACK_WIDE - 1))
                    if enter:
                        enter(RING * q, u)
                    walk(eng, lambda x: v >= (x + 1) * PACK_COUNT, s,
                         lambda c, g, width, wide: tile(e, u, c, g, width, wide), v & PACK_WIDE if layouts else False)

        def packed(eng, e):
            return eng.value_load(packed_i[0:1, bass.ds(e, 1)], min_val=0, max_val=(TOKENS + 1) * PACK_COUNT - 1)

        def by_layout(eng, wide, do):
            if wide is False:
                do(False)
            else:
                with eng.If(wide > 0):
                    do(True)
                with eng.Else():
                    do(False)
                eng.nop()

        def is_first(c):
            return isinstance(c, int) and c == 0

        def buf(u, c):
            return xs[u % 2][0 if isinstance(c, int) and c in (0, 2) else 1]

        @block.sync
        def _(sp):
            sp.dma_start(cst[:, :], table).then_inc(sem("cst_in"), 16)
            sp.dma_start(tokw[:, :, :], tok_w.rearrange("(c p) n -> p c n", p=HALF)).then_inc(sem("tokw_in"), 16)
            for n in range(2):
                sp.dma_start(raw[n][:, :], x_v[0:P, n, :]).then_inc(sem(f"raw_in{n}"), 16)
            sp.wait_ge(sem("wa_in"), 64)
            for n in range(2, 4):
                sp.dma_start(raw[n][:, :], x_v[0:P, n, :]).then_inc(sem(f"raw_in{n}"), 16)
            def expert_load(slot, e):
                w_in = sem(f"w_in{slot}")
                one = bass.ds(e, 1)
                sp.dma_start(W1[slot][:, :, :], w1[one].rearrange("a (c p) n -> p (a c) n", p=HALF)).then_inc(w_in, 16)
                sp.dma_start(W2[slot][:, :, :], w2[one].rearrange("a (c p) n -> p (a c) n", p=P)).then_inc(w_in, 16)
                sp.dma_start(W3[slot][:, :, :], w3[one].rearrange("a (c p) n -> p (a c) n", p=P)).then_inc(w_in, 16)
                sp.dma_start(WL[slot][0:BOT, :], wl[one].rearrange("a p n -> (a p) n")).then_inc(w_in, 16)
                sp.dma_start(WL[slot][BOT:BOT + 1, :], bl[one, :]).then_inc(w_in, 16)
            for n in range(4, 2 * GROUPS):
                sp.wait_ge(sem("blocks"), n - 3)
                half, g = n // GROUPS, n % GROUPS
                sp.dma_start(raw[n % 4][:, :], x_v[half * P:(half + 1) * P, g, :]).then_inc(sem(f"raw_in{n % 4}"), 16)
            sp.wait_ge(sem("init"), INIT)
            for e in range(2):
                expert_load(e, e)
            sp.wait_ge(sem("tables"), 3)
            sp.wait_ge(sem("pad_set"), 1)
            sp.sem_inc(sem("xs_in"), 16)
            n0 = sp.value_load(cnt_i[0:1, 0:1], min_val=0, max_val=TOKENS)
            sp.dma_start(slots[bass.ds(n0, P), :], pad[:, :]).then_inc(sem("pad_out0"), 16)
            for n in range(NT - 4, NT):
                scattered(sp, n, n)

            def xs_load(e, u, c, g, free, width):
                sp.wait_ge(sem("xe_t"), free)
                sp.wait_ge(sem("dest"), free)
                sp.wait_ge(sem("xs_in"), 16 * g + 16)
                if width == WIDE:
                    sp.dma_start(buf(u, c)[0:HALF, :].rearrange("p (k d) -> p k d", k=2),
                                 slots[bass.ds(e * CAP + c * P, WIDE), :].rearrange("(k p) d -> p k d", p=HALF)).then_inc(sem("xs_in"), 16)
                else:
                    sp.dma_start(buf(u, c)[:, 0:ROW],
                                 slots[bass.ds(e * CAP + c * P, P), :]).then_inc(sem("xs_in"), 16)

            def group(e0, full):
                for u in range(RING):
                    e = e0 + u
                    nn = sp.value_load(cnt_i[0:1, bass.ds(e + 1, 1)], min_val=0, max_val=TOKENS)
                    sp.dma_start(slots[bass.ds((e + 1) * CAP + nn, P), :], pad[:, :]).then_inc(sem(f"pad_out{(u + 1) % 2}"), 16)
                    n = sp.value_load(cnt_i[0:1, bass.ds(e, 1)], min_val=0, max_val=TOKENS)
                    s = sp.value_load(start_i[0:1, bass.ds(e + 1, 1)], min_val=0, max_val=2 * EXPERTS)
                    back = sp.value_load(start_i[0:1, bass.ds(e, 1)], min_val=0, max_val=2 * EXPERTS)
                    sp.wait_ge(sem(f"pad_out{u % 2}"), 8 * e0 + 16 * (u // 2 + 1))
                    alone(sp)
                    def load(c, g, width, _):
                        free = back + 1 if isinstance(c, int) and c < 2 else s + 2 if isinstance(c, int) else s + c + 1
                        xs_load(e, u, c, g, free, width)
                    walk(sp, lambda x: n > x, s, load, False)
                    if full or u < RING - 2:
                        sp.wait_ge(sem("l4"), back + 1)
                        alone(sp)
                        expert_load((u + 2) % RING, e + 2)

            with sp.Fori(0, EXPERTS // RING - 1) as q:
                group(RING * q, True)
            group(EXPERTS - RING, False)

            tiles = sp.value_load(start_i[0:1, EXPERTS + 1:EXPERTS + 2], min_val=EXPERTS, max_val=2 * EXPERTS)
            sp.wait_ge(sem("sent"), tiles + 2)
            sp.wait_ge(sem("pad_out0"), 8 * EXPERTS + 16)
            sp.wait_ge(sem("pad_out1"), 8 * EXPERTS)
            for n in range(NT):
                i = n % OUT_RING
                need(sp, "o1", n - OUT_RING + 1)
                need(sp, "o2", n - OUT_RING + 1)
                if n == 0:
                    sp.dma_start(res[0][0:IMAGES, 0, :], bass.AP(results.tensor, 0, [[0, IMAGES], [1, D]])).then_inc(sem("res_in0"), 16)
                    sp.dma_start(res[0][0:IMAGES, 1, :], bass.AP(results.tensor, D, [[0, IMAGES], [1, D]])).then_inc(sem("res_in0"), 16)
                else:
                    sp.dma_start(res_flat[i], res_v[n]).then_inc(sem(f"res_in{i}"), 16)

        @block.gpsimd
        def _(pool):
            pool.memset(pad[:, :], 0.0).then_inc(sem("pad_zero"), 1)
            pool.wait_ge(sem("pad_zero"), 1)
            pool.wait_ge(sem("cst_in"), 16)
            pool.tensor_copy(pad[:, D:D + 1].bitcast(u32), cst[:, C_PADID:C_PADID + 1]).then_inc(sem("pad_set"), 1)
            pool.tensor_copy(dest_new[:, :], cst[:, C_PADID:C_PADID + 1].to_broadcast([P, 2])).then_inc(sem("pad_set"), 1)
            pool.sem_inc(sem("kept"), 4)
            pool.wait_ge(sem("cls_ve"), 1)
            pool.tensor_tensor(rs1[:, 0:1], ve1[:, 0:1], mhalf[:, 0:1], ALU.pow).then_inc(sem("cls_rs"), 1)
            for hf in range(2):
                pool.wait_ge(sem("ve1"), hf + 1)
                pool.tensor_tensor(rs1[:, 8 * hf + 1:8 * hf + 9], ve1[:, 8 * hf + 1:8 * hf + 9], mhalf[:, 0:8], ALU.pow).then_inc(sem("rs1"), 1)

            def step(k, j, stages):
                a, b, c, d, e, _, f = (k - i for i in range(7))
                ja, jb, jc, jd, je, _, jf = (j - i for i in range(7))
                if "B" in stages:
                    pool.wait_ge(sem("qkT"), b)
                    need(pool, "scores", b - 2)
                    for half in range(2):
                        ins = pool.tensor_tensor(
                            kblk[jb % 2][1][:, half, :, 0:PATCHES],
                            qkT[jb % 2][:, 2 + half:3 + half, PATCHES:P].to_broadcast([HALF, HH, PATCHES]),
                            cst[0:HALF, C_HEAD:C_HEAD + HH].unsqueeze(2).to_broadcast([HALF, HH, PATCHES]), ALU.mult)
                    ins.then_inc(sem("kblk1"), 1)
                if "G" in stages:
                    pool.wait_ge(sem("top8"), f + 1)
                    pool.tensor_copy(logits[:, bass.ds(f, 1), :].rearrange("p a e -> p (a e)"), lgs[jf % 2][:, :]).then_inc(sem("kept"), 1)
                    pool.tensor_copy(top2[:, bass.ds(f, 1), :].rearrange("p a e -> p (a e)"), top8[jf % 2][:, 0:2]).then_inc(sem("kept"), 1)
                    pool.wait_ge(sem("slot"), f + 1)
                    pool.wait_ge(sem("row"), 3 * f + 3)
                    alone(pool)
                    for ch in range(2):
                        pool.indirect_dma_start(
                            out=slots, out_offset=bass.IndirectOffsetOnAxis(ap=slu[jf % 4][:, ch:ch + 1], axis=0),
                            in_=row[ch][jf % 4][:, :], in_offset=None).then_inc(sem(f"scattered{ch}{jf % 4}"), 16)
                if "C" in stages:
                    pool.wait_ge(sem("exp"), c)
                    need(pool, "yv", c - 2)
                    need(pool, "den", c - 2)
                    pool.tensor_tensor(pvc[jc % 2][:, :].rearrange("p (h d) -> p h d", d=HD),
                                       p_class[jc % 2].unsqueeze(2).to_broadcast([P, HEADS, HD]),
                                       vcls[:, :].rearrange("p (h d) -> p h d", d=HD), ALU.mult).then_inc(sem("pvc"), 1)
                    pool.tensor_tensor(psum2[jc % 2][:, :], p_class[jc % 2], p_sink[jc % 2], ALU.add).then_inc(sem("psum2"), 1)
                if "E" in stages:
                    pool.wait_ge(sem("x2"), e + 1)
                    scattered(pool, e - 4, je - 4)
                    alone(pool)
                    pool.tensor_copy(row[1][je % 4][:, 0:D], row[0][je % 4][:, 0:D]).then_inc(sem("row"), 1)
                    for ch in range(2):
                        pool.tensor_copy(row[ch][je % 4][:, D:D + 1].bitcast(u32),
                                         cst[:, bass.ds(C_DEST + ch * NT + e, 1)]).then_inc(sem("row"), 1)
                if "A" in stages:
                    pool.wait_ge(sem("rope_c"), a)
                    pool.wait_ge(sem("rope_s"), a)
                    need(pool, "qk_t", a - 2)
                    pool.tensor_tensor(qk[ja % 2][:, :], rope_c[ja % 2][:, :], rope_s[ja % 2][:, :], ALU.add).then_inc(sem("qk"), 1)
                if "D" in stages:
                    pool.wait_ge(sem("ve2"), d + 1)
                    need(pool, "x2", d - 1)
                    pool.tensor_tensor(rs2[jd % 2][:, :], mv2[jd % 2][:, 2:3], mhalf[:, 0:1], ALU.pow).then_inc(sem("rs2"), 1)

            pipeline(pool, step)

            pool.sem_inc(sem("sent"), 1)
            def send(e, g, wide):
                pool.wait_ge(sem("result"), g + 2)
                alone(pool)
                def parts(was_wide):
                    for k in range(1 + was_wide):
                        rows = HALF if was_wide else P
                        pool.indirect_dma_start(
                            out=results, out_offset=bass.IndirectOffsetOnAxis(ap=dest_old[0:rows, k:k + 1], axis=0),
                            in_=yb[0:rows, k * D:(k + 1) * D], in_offset=None).then_inc(sem(("result_out", "second_out")[k]), 16)
                    if was_wide:
                        wides = pool.value_load(wides_i[0:1, bass.ds(e, 1)], min_val=1, max_val=EXPERTS)
                        pool.wait_ge(sem("second_out"), 16 * wides)
                by_layout(pool, wide, parts)
                pool.wait_ge(sem("result_out"), 16 * g + 16)
                pool.sem_inc(sem("sent"), 1)

            pool.wait_ge(sem("wides"), 1)
            experts(pool, lambda e, u, c, g, width, wide: send(e, g, wide))
            v = packed(pool, EXPERTS)
            send(EXPERTS, pool.snap(v & (PACK_WIDE - 1)), v & PACK_WIDE)

        @block.scalar
        def _(act):
            act.dma_start(h[:, 0, :], cls_tok.rearrange("a b d -> (a b) d").broadcast_to([P, D])).then_inc(sem("cls_in"), 16)
            act.dma_start(wa[0:HALF, :, :], w_attn.rearrange("(c p) n -> p c n", p=HALF)).then_inc(sem("wa_in"), 16)
            act.dma_start(wa[HALF:HALF + 1, 1, :], b_attn.rearrange("(a n) -> a n", a=1)).then_inc(sem("wa_in"), 16)
            with nc.allow_non_contiguous_dma("per-feature scale and bias, once"):
                act.dma_start(scalec[:, :], n_scale.rearrange("(c p) -> p c", p=HALF)).then_inc(sem("wa_in"), 16)
                act.dma_start(biasc[:, :], n_bias.rearrange("(c p) -> p c", p=HALF)).then_inc(sem("wa_in"), 16)
            act.dma_start(sinkb[:, :], sinks.rearrange("(a n) -> a n", a=1).broadcast_to([P, HEADS])).then_inc(sem("sink_in"), 16)
            act.dma_start(wp[0:HALF, :, :], w_proj.rearrange("(c p) n -> p c n", p=HALF)).then_inc(sem("wp_in"), 16)
            act.dma_start(wp[HALF:HALF + 1, 1, :], b_proj.rearrange("(a n) -> a n", a=1)).then_inc(sem("wp_in"), 16)
            act.dma_start(rez[:, :], rezero.rearrange("(a n) -> a n", a=1).broadcast_to([HALF + 1, 1])).then_inc(sem("wp_in"), 16)
            act.dma_start(gw[:, :], gate_w).then_inc(sem("bias_in"), 16)
            act.dma_start(b1r[:, :], b1).then_inc(sem("bias_in"), 16)
            act.dma_start(b2r[:, :], b2).then_inc(sem("bias_in"), 16)
            act.dma_start(b3r[:, :], b3).then_inc(sem("bias_in"), 16)
            act.dma_start(tokb[:, :], tok_b.rearrange("(a n) -> a n", a=1).broadcast_to([P, D])).then_inc(sem("tokb_in"), 16)
            act.wait_ge(sem("cst_in"), 16)
            act.activation(identb[:, :], ident, ACT.Copy).then_inc(sem("tab"), 1)
            act.activation(earlier[:, :], cst[:, C_TRI:C_TRI + P], ACT.Copy).then_inc(sem("tab"), 1)
            act.activation(causal[:, :], cst[:, C_CAUSAL:C_CAUSAL + HH * KEYS], ACT.Copy).then_inc(sem("tab"), 1)
            for q in range(4):
                act.wait_ge(sem("tokw_t"), q + 1)
                act.activation(tokwT[:, 2 * q:2 * q + 2, :], PS[:, q, 0:2 * D].rearrange("p (g n) -> p g n", g=2), ACT.Copy).then_inc(sem("tokwT"), 1)
            act.wait_ge(sem("bias_t"), 1)
            for w in range(2):
                act.activation(b12T[:, 0:EXPERTS, 4 * w:4 * w + 4], PS[:, 4, w * P:(w + 1) * P].rearrange("p (c e) -> p e c", c=4), ACT.Copy).then_inc(sem("biasT"), 1)
            act.activation(gwT[:, :, :], PS[0:HALF, 4, 2 * P:2 * P + 64].rearrange("p (c e) -> p c e", c=2), ACT.Copy).then_inc(sem("biasT"), 1)
            act.activation(b3T[:, 1:EXPERTS + 1], PS[0:BOT, 4, 320:352], ACT.Copy).then_inc(sem("biasT"), 1)
            act.wait_ge(sem("cls_xt"), 1)
            act.wait_ge(sem("init"), INIT)
            act.activation(xT[0][0:HALF, :, :], p_xT, ACT.Copy).then_inc(sem("cls_xT"), 1)
            act.wait_ge(sem("cls_qkv"), 1)
            act.activation(vcls[:, :], p_v, ACT.Copy).then_inc(sem("vcls"), 1)
            act.activation(qk[0][:, 0:D], p_qk[:, 0:D], ACT.Copy, scale=HD ** -0.5).then_inc(sem("cls_qk"), 1)
            act.activation(qk[0][:, D:2 * D], p_qk[:, D:2 * D], ACT.Copy).then_inc(sem("cls_qk"), 1)
            act.wait_ge(sem("cls_kt"), 1)
            act.activation(qkT[0][:, 2:4, :], p_qkT[:, 2:4, :], ACT.Copy).then_inc(sem("cls_kT"), 1)
            act.wait_ge(sem("cls_sub"), 3)
            act.activation(psum2[0][:, :], psum2[0][:, :], ACT.Exp).then_inc(sem("cls_exp"), 1)
            act.activation(psum2[1][:, :], psum2[1][:, :], ACT.Exp).then_inc(sem("cls_exp"), 1)
            def sort_pixels(n):
                act.wait_ge(sem(f"raw_in{n % 4}"), 16 * (n // 4 + 1))
                need(act, "pix_t", n - 1)
                act.activation(blocks[n % 2][:, :, :].rearrange("p j (r c) -> p j r c", r=ROWS),
                               raw[n % 4][:, :].rearrange("p (r j c) -> p j r c", r=ROWS, j=GRID), ACT.Copy).then_inc(sem("blocks"), 1)
            sort_pixels(0)
            sort_pixels(1)
            for hf in range(2):
                for g in range(GROUPS):
                    n = hf * GROUPS + g
                    act.wait_ge(sem("pix_t"), n + 1)
                    need(act, "embed", n - 1)
                    act.activation(pix[n % 2][:, :].rearrange("p (t j) -> p j t", j=GRID)[:, 0:4, :],
                                   PS[:, 4 + 2 * (n % 2), :].rearrange("p (j t) -> p j t", j=4), ACT.Copy).then_inc(sem("pix_a"), 1)
                    if n + 2 < 2 * GROUPS:
                        sort_pixels(n + 2)

            def step(k, j, stages):
                a, b, c, d, e, f = (k - i for i in range(6))
                ja, jb, jc, jd, je, jf = (j - i for i in range(6))
                if "B" in stages:
                    act.wait_ge(sem("qk_t"), b)
                    need(act, "kblk0", b - 2)
                    need(act, "kblk1", b - 2)
                    need(act, "scores", b - 2)
                    act.activation(qkT[jb % 2][:, :, :], p_qkT, ACT.Copy).then_inc(sem("qkT"), 1)
                if "A" in stages:
                    act.wait_ge(sem("x_t"), a)
                    need(act, "qkv", a - 2)
                    act.activation(xT[ja % 2][0:HALF, :, :], p_xT, ACT.Copy).then_inc(sem("xT"), 1)
                if "C" in stages:
                    act.wait_ge(sem("p_t"), c)
                    need(act, "pv", c - 2)
                    act.activation(pT[jc % 2][:, 0:4, :], p_pTa, ACT.Copy).then_inc(sem("pTa"), 1)
                if "A" in stages:
                    act.wait_ge(sem("qkv"), a)
                    need(act, "pv", a - 4)
                    for b_ in range(2):
                        for odd in range(2):
                            ins = act.activation(
                                vblk[ja % 4][odd * PATCHES:(odd + 1) * PATCHES, b_, :, odd, 0:HD],
                                PS[b_ * PATCHES:(b_ + 1) * PATCHES, 0, 256:256 + D].rearrange("p (g o d) -> p g o d", o=2, d=HD)[:, :, odd, :],
                                ACT.Copy)
                    ins.then_inc(sem("vblk"), 1)
                if "D" in stages:
                    act.wait_ge(sem("yx_t"), k - 2)
                    need(act, "tail", d - 1)
                    act.activation(yT[jd % 2][0:HALF, :, :], p_yT, ACT.Copy).then_inc(sem("yT"), 1)
                if "E" in stages:
                    act.wait_ge(sem("yx_t"), k - 2)
                    need(act, "tail", e)
                    act.activation(x2T[je % 2][:, :, :], p_x2T, ACT.Copy).then_inc(sem("x2T"), 1)
                if "B" in stages:
                    act.wait_ge(sem("shifted"), 3 * b)
                    act.activation(probs[jb % 2][:, :], probs[jb % 2][:, :], ACT.Exp).then_inc(sem("exp"), 1)

            pipeline(act, step)
            act.wait_ge(sem("g_sub"), 2)
            act.activation(gmx[:, :, :], gmx[:, :, :], ACT.Exp).then_inc(sem("g_exp"), 1)
            act.activation(gs2[:, :, :], gs2[:, :, :], ACT.Exp).then_inc(sem("g_exp"), 1)

            act.wait_ge(sem("last_zero"), 3)
            act.sem_inc(sem("g2"), 4)

            def tile(e, u, c, g, width, wide):
                for m in range(4):
                    act.wait_ge(sem("l1"), 4 * g + m + 1)
                    act.activation(h1b[:, m, 0:width], PS[:, L1_BANKS[m], 0:width], ACT.Gelu,
                                   bias=bcur[u % 2][:, m:m + 1]).then_inc(sem("g1"), 1)
                for m in range(4):
                    act.wait_ge(sem("l2"), 4 * g + m + 1)
                    act.activation(h2b[:, m, 0:width], PS[:, L2_BANKS[m], 0:width], ACT.Gelu,
                                   bias=bcur[u % 2][:, 4 + m:5 + m]).then_inc(sem("g2"), 1)

            def enter(e0, u):
                act.wait_ge(sem("bcur"), e0 + u + 1)
                alone(act)

            experts(act, tile, enter=enter, layouts=False)
            for n in range(NT):
                i = n % OUT_RING
                act.wait_ge(sem("o2"), n + 1)
                if n == 0:
                    act.dma_start(out[:, 0, :], o2[0][0:IMAGES, :]).then_inc(sem("out0"), 16)
                else:
                    for b_ in range(2):
                        act.dma_start(out[2 * (n - 1) + b_, 1:KEYS, :], o2[i][b_ * PATCHES:(b_ + 1) * PATCHES, :]).then_inc(sem(f"out{i}"), 16)
            for i in range(OUT_RING):
                act.wait_ge(sem(f"out{i}"), sum(16 if n == 0 else 32 for n in range(i, NT, OUT_RING)))

        @block.tensor
        def _(pe):
            pe.wait_ge(sem("cst_in"), 16)
            pe.wait_ge(sem("tokw_in"), 16)
            for q in range(4):
                for i in range(2):
                    for c in range(2):
                        ins = pe.transpose(PS[:, q, i * D + c * HALF:i * D + (c + 1) * HALF],
                                           tokw[:, c, (2 * q + i) * P:(2 * q + i + 1) * P], ident[0:HALF, 0:HALF])
                ins.then_inc(sem("tokw_t"), 1)
            pe.wait_ge(sem("bias_in"), 64)
            for c in range(4):
                pe.transpose(PS[:, 4, 32 * c:32 * c + 32], b1r[:, c * P:(c + 1) * P], ident[0:EXPERTS, 0:EXPERTS])
                pe.transpose(PS[:, 4, P + 32 * c:P + 32 * c + 32], b2r[:, c * P:(c + 1) * P], ident[0:EXPERTS, 0:EXPERTS])
            for c in range(2):
                pe.transpose(PS[0:HALF, 4, 2 * P + 32 * c:2 * P + 32 * c + 32], gw[:, c * HALF:(c + 1) * HALF], ident[0:EXPERTS, 0:EXPERTS])
            pe.transpose(PS[0:BOT, 4, 320:352], b3r[:, :], ident[0:EXPERTS, 0:EXPERTS]).then_inc(sem("bias_t"), 1)
            pe.wait_ge(sem("wa_in"), 64)
            for j in range(2):
                for c in range(2):
                    ins = pe.matmul(PS[HALF:HALF + 1, 5 + j, 0:288], biasc[:, c:c + 1], wa[0:HALF, c, 288 * j:288 * (j + 1)],
                                    start=(c == 0), stop=(c == 1), tile_position=(0, HALF))
            ins.then_inc(sem("bias_w"), 1)
            pe.wait_ge(sem("tokwT"), 4)
            pe.wait_ge(sem("cls_xhat"), 1)
            for c in range(2):
                ins = pe.transpose(p_xT[:, c, :], xhat[0][:, c * HALF:(c + 1) * HALF], ident)
            ins.then_inc(sem("cls_xt"), 1)
            pe.wait_ge(sem("cls_xT"), 1)
            pe.wait_ge(sem("was"), 3)

            def project_in(src):
                for c in range(2):
                    kk = HALF + c
                    pe.matmul(p_qk, src[0:kk, c, :], was[0:kk, c, 0:2 * D], start=(c == 0), stop=(c == 1))
                for c in range(2):
                    kk = HALF + c
                    ins = pe.matmul(p_v, src[0:kk, c, :], was[0:kk, c, 2 * D:3 * D], start=(c == 0), stop=(c == 1))
                return ins
            project_in(xT[0]).then_inc(sem("cls_qkv"), 1)
            pe.wait_ge(sem("cls_qk"), 2)
            for c in range(2):
                ins = pe.transpose(p_qkT[:, 2 + c, :], qk[0][:, D + c * HALF:D + (c + 1) * HALF], ident)
            ins.then_inc(sem("cls_kt"), 1)

            pe.wait_ge(sem("vcls"), 1)
            pe.wait_ge(sem("cls_kT"), 1)
            pe.wait_ge(sem("biasT"), 4)
            pe.wait_ge(sem("was"), 3)

            def pixels(n):
                pe.wait_ge(sem("blocks"), n + 1)
                need(pe, "pix_a", n - 1)
                need(pe, "pix_v", n - 1)
                for j in range(GRID):
                    ins = pe.transpose(PS[:, 4 + 2 * (n % 2) + j // 4, (j % 4) * P:(j % 4 + 1) * P], blocks[n % 2][:, j, :], ident)
                ins.then_inc(sem("pix_t"), 1)

            def embed(n):
                g = n % GROUPS
                pe.wait_ge(sem("pix_a"), n + 1)
                pe.wait_ge(sem("pix_v"), n + 1)
                if g == 0 and n:
                    pe.wait_ge(sem("h"), GROUPS)
                for t in range(8):
                    ins = pe.matmul(PS[:, t // 2, (t % 2) * D:(t % 2 + 1) * D], pix[n % 2][:, t * P:(t + 1) * P], tokwT[:, g, :],
                                    start=(g == 0 and t % 2 == 0), stop=(g == GROUPS - 1), skip_group_check=True)
                ins.then_inc(sem("embed"), 1)

            pixels(0)
            for n in range(2 * GROUPS):
                if n + 1 < 2 * GROUPS:
                    pixels(n + 1)
                embed(n)

            def step(k, j, stages):
                a, b, c, d, e, f = (k - i for i in range(6))
                ja, jb, jc, jd, je, jf = (j - i for i in range(6))
                if "B" in stages:
                    pe.wait_ge(sem("qk"), b)
                    need(pe, "yT", d)
                    need(pe, "x2T", e)
                    for q in range(4):
                        ins = pe.transpose(p_qkT[:, q, :], qk[jb % 2][:, q * HALF:(q + 1) * HALF], ident)
                    ins.then_inc(sem("qk_t"), 1)
                if "A" in stages:
                    pe.wait_ge(sem("xhat"), a)
                    need(pe, "vblk", a - 1)
                    for q in range(2):
                        ins = pe.transpose(p_xT[:, q, :], xhat[ja % 2][:, q * HALF:(q + 1) * HALF], ident)
                    ins.then_inc(sem("x_t"), 1)
                if "C" in stages:
                    pe.wait_ge(sem("exp"), c)
                    need(pe, "pTa", c - 1)
                    need(pe, "yv", c - 1)
                    need(pe, "den", c - 1)
                    for q in range(HH):
                        dst = p_pTa[:, q, :] if q < 4 else p_pTb[:, q - 4, :]
                        ins = pe.transpose(dst, p_patch[jc % 2][:, q * P:(q + 1) * P], ident)
                    ins.then_inc(sem("p_t"), 1)
                if "A" in stages:
                    pe.wait_ge(sem("xT"), a)
                    need(pe, "rope_c", a - 1)
                    need(pe, "rope_s", a - 1)
                    project_in(xT[ja % 2]).then_inc(sem("qkv"), 1)
                if "B" in stages:
                    pe.wait_ge(sem("kblk0"), b)
                    pe.wait_ge(sem("kblk1"), b)
                    need(pe, "shifted", 3 * b - 3)
                    for half in range(2):
                        pe.matmul(PS[:, 5 + half, 0:HH * KEYS], identb[:, :], causal[:, :], start=True, stop=False, skip_group_check=True)
                        for b_ in range(2):
                            ins = pe.matmul(PS[b_ * PATCHES:(b_ + 1) * PATCHES, 5 + half, 0:HH * KEYS],
                                            qkT[jb % 2][:, half, b_ * PATCHES:(b_ + 1) * PATCHES],
                                            kblk[jb % 2][b_][:, half, :, :].rearrange("p g k -> p (g k)"),
                                            start=False, stop=True, skip_group_check=True)
                    ins.then_inc(sem("scores"), 1)
                if "D" in stages or "E" in stages:
                    if "B" in stages:
                        pe.wait_ge(sem("qkT"), b)
                    if "D" in stages:
                        pe.wait_ge(sem("y"), d + 1)
                        if "B" not in stages:
                            need(pe, "yT", d)
                        for q in range(2):
                            ins = pe.transpose(p_yT[:, q, :], y[jd % 2][:, q * HALF:(q + 1) * HALF], ident)
                    if "E" in stages:
                        pe.wait_ge(sem("x2"), e + 1)
                        if "B" not in stages:
                            need(pe, "x2T", e)
                            need(pe, "yT", min(d, NT) if isinstance(d, int) else d)
                        for q in range(2):
                            ins = pe.transpose(p_x2T[:, q, :], row[0][je % 4][:, q * HALF:(q + 1) * HALF], ident)
                    ins.then_inc(sem("yx_t"), 1)
                if "C" in stages:
                    pe.wait_ge(sem("pTa"), c)
                    pe.wait_ge(sem("pTb"), c)
                    pe.wait_ge(sem("vblk"), c)
                    for b_ in range(2):
                        for q in range(HH):
                            ins = pe.matmul(PS[b_ * PATCHES:(b_ + 1) * PATCHES, 4, 256 + 34 * q:256 + 34 * (q + 1)],
                                            pT[jc % 2][:, q, b_ * PATCHES:(b_ + 1) * PATCHES],
                                            vblk[jc % 4][:, b_, q, :, :].rearrange("p o d -> p (o d)"), start=True, stop=True)
                    ins.then_inc(sem("pv"), 1)
                if "D" in stages:
                    need(pe, "h1", d)
                if "F" in stages:
                    pe.wait_ge(sem("logits"), f + 1)
                    need(pe, "rankc", f)
                if "D" in stages:
                    pe.wait_ge(sem("yT"), d + 1)
                    if "E" not in stages:
                        need(pe, "h1", d)
                    for q in range(2):
                        kk = HALF + q
                        ins = pe.matmul(p_proj, yT[jd % 2][0:kk, q, :], wps[0:kk, q, :], start=(q == 0), stop=(q == 1))
                if "E" in stages:
                    pe.wait_ge(sem("x2T"), e + 1)
                    if "D" not in stages:
                        pe.wait_ge(sem("h1"), NT)
                    for q in range(2):
                        ins = pe.matmul(p_gate, x2T[je % 2][:, q, :], gwT[:, q, :], start=(q == 0), stop=(q == 1))
                if "F" in stages:
                    pe.wait_ge(sem("member"), f + 1)
                    need(pe, "before", f)
                    pe.matmul(p_rank, earlier[:, :], member[jf % 2][:, :], start=True, stop=False)
                    ins = pe.matmul(p_rank, onesb[:, :], before[:, :], start=False, stop=True)
                if "D" in stages or "E" in stages or "F" in stages:
                    ins.then_inc(sem("tail"), 1)

            pe.wait_ge(sem("h"), 2 * GROUPS)
            pe.wait_ge(sem("kcls"), 4)
            pe.wait_ge(sem("vones"), 8)
            pe.wait_ge(sem("tab"), 3)
            pe.wait_ge(sem("wps"), 2)
            pe.wait_ge(sem("before_zero"), 8)
            pipeline(pe, step)
            pe.wait_ge(sem("before"), NT)
            pe.wait_ge(sem("rankc"), NT)
            pe.matmul(p_rank, onesb[:, :], before[:, :], start=True, stop=True).then_inc(sem("counts"), 1)

            def finish_z(g, place, wide):
                width = WIDE if wide else P
                for q in range(4):
                    pe.wait_ge(sem("g2"), 4 * g + q + 1)
                    ins = pe.matmul(p_z[:, 0:width], W3[place][:, q, :], h2b[:, q, 0:width], start=(q == 0), stop=(q == 3))
                ins.then_inc(sem("l3"), 1)

            def finish_results(g, place, wide):
                pieces, piece = (2, HALF) if wide else (1, P)
                pe.wait_ge(sem("z"), g + 1)
                pe.wait_ge(sem("result"), g + 1)
                for k in range(pieces):
                    ins = pe.matmul(PS[0:piece, 7, k * D:(k + 1) * D], zb[:, k * piece:(k + 1) * piece], WL[place][:, :], start=True, stop=True)
                ins.then_inc(sem("l4"), 1)

            def tile(e, u, c, g, width, wide):
                src, slot = buf(u, c), u % RING
                pieces, piece = (2, HALF) if width == WIDE else (1, P)
                stride = pieces * piece

                pe.wait_ge(sem("xs_in"), 16 * g + 32)
                for q in range(2):
                    for k in range(pieces):
                        ins = pe.transpose(PS[0:HALF, 0, q * stride + k * piece:q * stride + (k + 1) * piece],
                                           src[0:piece, k * ROW + q * HALF:k * ROW + (q + 1) * HALF], ident[0:piece, 0:piece])
                ins.then_inc(sem("xe_t"), 1)
                place = (u + RING - 1) % RING if is_first(c) else slot
                by_layout(pe, wide, lambda was_wide: finish_z(g, place, was_wide))
                if is_first(c):
                    pe.wait_ge(sem(f"w_in{u}"), (80 // RING) * (e - u) + 80)
                pe.wait_ge(sem("xeT"), g + 1)
                for m in range(4):
                    if m == 3:
                        pe.wait_ge(sem("z"), g + 1)
                    for q in range(2):
                        ins = pe.matmul(PS[:, L1_BANKS[m], 0:width], W1[slot][:, q, m * P:(m + 1) * P], xeT[:, q * stride:q * stride + width],
                                        start=(q == 0), stop=(q == 1))
                    ins.then_inc(sem("l1"), 1)
                by_layout(pe, wide, lambda was_wide: finish_results(g, place, was_wide))
                for m in range(4):
                    for q in range(4):
                        if m == 0:
                            pe.wait_ge(sem("g1"), 4 * g + q + 1)
                        ins = pe.matmul(PS[:, L2_BANKS[m], 0:width], W2[slot][:, q, m * P:(m + 1) * P], h1b[:, q, 0:width],
                                        start=(q == 0), stop=(q == 3))
                    ins.then_inc(sem("l2"), 1)

            pe.wait_ge(sem("zb_zero"), 2)
            pe.wait_ge(sem("last_zero"), 3)
            pe.sem_inc(sem("xe_t"), 1)
            experts(pe, tile)
            v = packed(pe, EXPERTS)
            tiles = pe.snap(v & (PACK_WIDE - 1))
            def last(was_wide):
                finish_z(tiles, RING - 1, was_wide)
                finish_results(tiles, RING - 1, was_wide)
            by_layout(pe, v & PACK_WIDE, last)

        @block.vector
        def _(dve):
            init = sem("init")
            dve.memset(mhalf[:, :], -0.5).then_inc(init, 1)
            for t in (xT[0], xT[1], yT[0], yT[1]):
                dve.memset(t[HALF:HALF + 1, :, :], 1.0).then_inc(init, 1)
            for t in vblk:
                dve.memset(t[:, :, :, :, :], 0.0).then_inc(init, 1)
            dve.memset(onesb[:, :], 1.0).then_inc(init, 1)
            for t in WL:
                dve.memset(t[BOT:P, :], 0.0).then_inc(init, 1)
            dve.wait_ge(init, INIT)
            for t in vblk:
                dve.memset(t[0:PATCHES, :, :, 0, HD:HD + 1], 1.0).then_inc(sem("vones"), 1)
                dve.memset(t[PATCHES:P, :, :, 1, HD:HD + 1], 1.0).then_inc(sem("vones"), 1)
            dve.memset(before[:, :], 0.0).then_inc(sem("before_zero"), 1)
            dve.memset(cnt_i[:, :], 0).then_inc(sem("before_zero"), 1)
            dve.memset(ones1[:, :], 1.0).then_inc(sem("before_zero"), 1)
            dve.memset(start_i[:, :], 0).then_inc(sem("before_zero"), 1)
            dve.memset(packed_i[:, :], 0).then_inc(sem("before_zero"), 1)
            dve.memset(wides_i[:, :], 0).then_inc(sem("before_zero"), 1)
            dve.memset(b12T[:, EXPERTS, :], 0.0).then_inc(sem("before_zero"), 1)
            dve.memset(b3T[:, 0:1], 0.0).then_inc(sem("before_zero"), 1)
            dve.memset(zb[:, :], 0.0).then_inc(sem("zb_zero"), 1)
            dve.wait_ge(sem("zb_zero"), 1)
            dve.memset(zb[BOT:BOT + 1, :], 1.0).then_inc(sem("zb_zero"), 1)
            for c in range(2):
                for i in range(4):
                    dve.memset(row[c][i][:, D + 1:D + 2], 0.0).then_inc(sem("row_zero"), 1)
            dve.wait_ge(sem("cls_in"), 16)
            dve.bn_stats(st6[:, :], h[:, 0, :]).then_inc(sem("cls_st"), 1)
            dve.wait_ge(sem("cls_st"), 1)
            dve.bn_aggr(mv[:, 0, :], st6[:, :]).then_inc(sem("cls_st"), 1)
            dve.wait_ge(sem("cls_st"), 2)
            dve.tensor_scalar(ve1[:, 0:1], mv[:, 0, 1:2], EPS, None, ALU.add).then_inc(sem("cls_ve"), 1)
            dve.wait_ge(sem("wa_in"), 64)
            for c in range(2):
                dve.tensor_scalar(was[0:HALF, c, :], wa[0:HALF, c, :], scalec[:, c:c + 1], None, ALU.mult).then_inc(sem("was"), 1)
            dve.wait_ge(sem("bias_w"), 1)
            dve.tensor_tensor(was[HALF:HALF + 1, 1, :].rearrange("p (j n) -> p j n", j=2), PS[HALF:HALF + 1, 5:7, 0:288],
                              wa[HALF:HALF + 1, 1, :].rearrange("p (j n) -> p j n", j=2), ALU.add).then_inc(sem("was"), 1)
            dve.wait_ge(sem("cls_rs"), 1)
            dve.tensor_scalar(xhat[0][:, :], h[:, 0, :], mv[:, 0, 0:1], rs1[:, 0:1], ALU.subtract, ALU.mult).then_inc(sem("cls_xhat"), 1)
            dve.wait_ge(sem("wp_in"), 48)
            dve.tensor_scalar(wps[0:HALF, 0, :], wp[0:HALF, 0, :], rez[0:HALF, :], None, ALU.mult).then_inc(sem("wps"), 1)
            dve.tensor_scalar(wps[:, 1, :], wp[:, 1, :], rez[:, :], None, ALU.mult).then_inc(sem("wps"), 1)
            dve.wait_ge(sem("cls_qk"), 2)
            dve.wait_ge(sem("sink_in"), 16)
            dve.tensor_tensor(pvc[0][:, :], qk[0][:, 0:D], qk[0][:, D:2 * D], ALU.mult).then_inc(sem("cls_s"), 1)
            dve.wait_ge(sem("cls_s"), 1)
            dve.tensor_reduce(den[0][:, :], pvc[0][:, :].rearrange("p (h d) -> p h d", d=HD), AX.X, ALU.add).then_inc(sem("cls_s"), 1)
            dve.wait_ge(sem("cls_s"), 2)
            dve.tensor_tensor(mx[0][:, :], den[0][:, :], sinkb[:, :], ALU.max).then_inc(sem("cls_sub"), 1)
            dve.wait_ge(sem("cls_sub"), 1)
            dve.tensor_tensor(psum2[0][:, :], den[0][:, :], mx[0][:, :], ALU.subtract).then_inc(sem("cls_sub"), 1)
            dve.tensor_tensor(psum2[1][:, :], sinkb[:, :], mx[0][:, :], ALU.subtract).then_inc(sem("cls_sub"), 1)
            dve.wait_ge(sem("cls_kT"), 1)
            for i in range(2):
                for b_ in range(2):
                    dve.tensor_tensor(kblk[i][b_][:, :, :, PATCHES], qkT[0][:, 2:4, 0:1].to_broadcast([HALF, 2, HH]),
                                      cst[0:HALF, C_HEAD:C_HEAD + HH].unsqueeze(1).to_broadcast([HALF, 2, HH]), ALU.mult).then_inc(sem("kcls"), 1)
            dve.wait_ge(sem("cls_exp"), 2)
            dve.tensor_tensor(den[1][:, :], psum2[0][:, :], psum2[1][:, :], ALU.add).then_inc(sem("cls_y"), 1)
            dve.wait_ge(sem("cls_y"), 1)
            dve.reciprocal(rden[1][:, :], den[1][:, :]).then_inc(sem("cls_y"), 1)
            dve.wait_ge(sem("cls_y"), 2)
            dve.tensor_tensor(rden[0][:, :], rden[1][:, :], psum2[0][:, :], ALU.mult).then_inc(sem("cls_y"), 1)
            dve.wait_ge(sem("cls_y"), 3)
            dve.wait_ge(sem("vcls"), 1)
            dve.tensor_tensor(y[0][:, :].rearrange("p (h d) -> p h d", d=HD), vcls[:, :].rearrange("p (h d) -> p h d", d=HD),
                              rden[0][:, :].unsqueeze(2).to_broadcast([P, HEADS, HD]), ALU.mult).then_inc(sem("y"), 1)
            dve.wait_ge(sem("init"), INIT)
            dve.memset(WL[RING - 1][0:BOT, :], 0.0).then_inc(sem("last_zero"), 1)
            dve.memset(W3[RING - 1][:, :, :], 0.0).then_inc(sem("last_zero"), 1)
            dve.wait_ge(sem("tokw_t"), 4)
            dve.memset(h2b[:, :, :], 0.0).then_inc(sem("last_zero"), 1)

            def norm1_stats(n):
                dve.wait_ge(sem("h"), n)
                need(dve, "mv1", n - 1)
                dve.bn_stats(st6[:, :], h[:, n, :]).then_inc(sem("st1"), 1)
                dve.wait_ge(sem("st1"), n)
                dve.bn_aggr(mv[:, n, :], st6[:, :]).then_inc(sem("mv1"), 1)
                if n % 8 == 0:
                    dve.wait_ge(sem("mv1"), n)
                    dve.tensor_scalar(ve1[:, n - 7:n + 1], mv[:, n - 7:n + 1, 1], EPS, None, ALU.add).then_inc(sem("ve1"), 1)

            def norm1(n, j):
                need(dve, "x_t", n - 2)
                dve.tensor_scalar(xhat[j % 2][:, :], h[:, bass.ds(n, 1), :].rearrange("p a d -> p (a d)"), mv[:, bass.ds(n, 1), 0],
                                  rs1[:, bass.ds(n, 1)], ALU.subtract, ALU.mult).then_inc(sem("xhat"), 1)

            dve.wait_ge(sem("tokb_in"), 16)
            for hf in range(2):
                for g in range(GROUPS):
                    n = hf * GROUPS + g
                    dve.wait_ge(sem("pix_t"), n + 1)
                    need(dve, "embed", n - 1)
                    dve.tensor_copy(pix[n % 2][:, :].rearrange("p (t j) -> p j t", j=GRID)[:, 4:8, :],
                                    PS[:, 5 + 2 * (n % 2), :].rearrange("p (j t) -> p j t", j=4)).then_inc(sem("pix_v"), 1)
                    if hf:
                        norm1_stats(g + 1)
                dve.wait_ge(sem("embed"), (hf + 1) * GROUPS)
                for t in range(8):
                    n = 1 + 8 * hf + t
                    dve.tensor_tensor(h[:, n, :], PS[:, t // 2, (t % 2) * D:(t % 2 + 1) * D], tokb[:, :], ALU.add).then_inc(sem("h"), 1)
            def step(k, j, stages):
                a, b, c, d, e, f = (k - i for i in range(6))
                ja, jb, jc, jd, je, jf = (j - i for i in range(6))
                if "B" in stages:
                    dve.wait_ge(sem("qkT"), b)
                    need(dve, "scores", b - 2)
                    for half in range(2):
                        ins = dve.tensor_tensor(
                            kblk[jb % 2][0][:, half, :, 0:PATCHES],
                            qkT[jb % 2][:, 2 + half:3 + half, 0:PATCHES].to_broadcast([HALF, HH, PATCHES]),
                            cst[0:HALF, C_HEAD:C_HEAD + HH].unsqueeze(2).to_broadcast([HALF, HH, PATCHES]), ALU.mult)
                    ins.then_inc(sem("kblk0"), 1)
                if "C" in stages:
                    dve.wait_ge(sem("p_t"), c)
                    need(dve, "pv", c - 2)
                    dve.tensor_copy(pT[jc % 2][:, 4:6, :], p_pTb).then_inc(sem("pTb"), 1)
                if not isinstance(k, int) or k < TILES:
                    norm1(k + 1, j + 1)
                if "F" in stages:
                    dve.wait_ge(sem("tail"), f + 2)
                    lg, t8 = lgs[jf % 2][:, :], top8[jf % 2][:, :]
                    dve.wait_ge(sem("kept"), 2 * (f + 1))
                    dve.tensor_copy(lg, p_gate).then_inc(sem("logits"), 1)
                    dve.wait_ge(sem("logits"), f + 1)
                    alone(dve)
                    dve.max(t8, lg).then_inc(sem("top8"), 1)
                    dve.wait_ge(sem("top8"), f + 1)
                    alone(dve)
                    dve.max_index(idx8[jf % 2][:, :], t8, lg).then_inc(sem("idx8"), 1)
                    dve.wait_ge(sem("idx8"), f + 1)
                    dve.tensor_copy(idxf[jf % 2][:, :], idx8[jf % 2][:, 0:2]).then_inc(sem("idxf"), 1)
                    dve.wait_ge(sem("idxf"), f + 1)
                    for ch in range(2):
                        dve.tensor_scalar(pick[jf % 2][:, ch, :], iota, idxf[jf % 2][:, ch:ch + 1],
                                          cst[:, bass.ds(C_KEEP + f, 1)], ALU.is_equal, ALU.mult).then_inc(sem("pick"), 1)
                    dve.wait_ge(sem("pick"), 2 * f + 2)
                    dve.tensor_tensor(member[jf % 2][:, :], pick[jf % 2][:, 0, :], pick[jf % 2][:, 1, :], ALU.add).then_inc(sem("member"), 1)
                if "A" in stages:
                    dve.wait_ge(sem("qkv"), a)
                    need(dve, "qk", a - 2)
                    src = p_qk.rearrange("p (w h d) -> p w h d", w=2, d=HD)
                    dve.tensor_tensor(rope_c[ja % 2][:, :].rearrange("p (w h d) -> p w h d", w=2, d=HD), src,
                                      cst[:, C_ROPE_C:C_ROPE_C + 2 * HD].rearrange("p (w a d) -> p w a d", w=2, a=1).to_broadcast([P, 2, HEADS, HD]),
                                      ALU.mult).then_inc(sem("rope_c"), 1)
                    for w in range(2):
                        ins = dve.tensor_tensor(
                            rope_s[ja % 2][:, w * D:(w + 1) * D].rearrange("p (h d o) -> p h d o", h=HEADS, o=2),
                            p_qk[:, w * D:(w + 1) * D].rearrange("p (h d o) -> p h d o", h=HEADS, o=2)[:, :, :, ::-1],
                            cst[:, C_ROPE_S + w * HD:C_ROPE_S + (w + 1) * HD].rearrange("p (a d o) -> p a d o", a=1, o=2).to_broadcast([P, HEADS, HD // 2, 2]),
                            ALU.mult)
                    ins.then_inc(sem("rope_s"), 1)
                if "B" in stages:
                    dve.wait_ge(sem("scores"), b)
                    dve.tensor_reduce(mx[jb % 2][:, :].rearrange("p (c g) -> p c g", c=2), p_s, AX.X, ALU.max).then_inc(sem("rowmax"), 1)
                    dve.wait_ge(sem("rowmax"), b)
                    dve.tensor_tensor(mx[jb % 2][:, :], mx[jb % 2][:, :], sinkb[:, :], ALU.max).then_inc(sem("max"), 1)
                    dve.wait_ge(sem("max"), b)
                    need(dve, "p_t", b - 2)
                    need(dve, "pvc", b - 2)
                    need(dve, "psum2", b - 2)
                    dve.tensor_tensor(p_sink[jb % 2], sinkb[:, :], mx[jb % 2][:, :], ALU.subtract).then_inc(sem("shifted"), 1)
                    dve.tensor_tensor(p_class[jb % 2].rearrange("p (c g) -> p c g", c=2), p_s[:, :, :, PATCHES],
                                      mx[jb % 2][:, :].rearrange("p (c g) -> p c g", c=2), ALU.subtract).then_inc(sem("shifted"), 1)
                    dve.tensor_tensor(p_patch[jb % 2].rearrange("p (c g k) -> p c g k", c=2, g=HH), p_s[:, :, :, 0:PATCHES],
                                      mx[jb % 2][:, :].rearrange("p (c g a) -> p c g a", c=2, a=1).to_broadcast([P, 2, HH, PATCHES]),
                                      ALU.subtract).then_inc(sem("shifted"), 1)
                if "C" in stages:
                    dve.wait_ge(sem("pv"), c)
                    dve.wait_ge(sem("psum2"), c)
                    dve.tensor_tensor(den[jc % 2][:, :], psum2[jc % 2][:, :], p_y[:, :, HD], ALU.add).then_inc(sem("den"), 1)
                    dve.wait_ge(sem("pvc"), c)
                    dve.tensor_tensor(yv[jc % 2][:, :].rearrange("p (h d) -> p h d", d=HD), pvc[jc % 2][:, :].rearrange("p (h d) -> p h d", d=HD),
                                      p_y[:, :, 0:HD], ALU.add).then_inc(sem("yv"), 1)
                    dve.wait_ge(sem("den"), c)
                    dve.reciprocal(rden[jc % 2][:, :], den[jc % 2][:, :]).then_inc(sem("rden"), 1)
                    dve.wait_ge(sem("rden"), c)
                    dve.wait_ge(sem("yv"), c)
                    need(dve, "yx_t", c - 1)
                    dve.tensor_tensor(y[jc % 2][:, :].rearrange("p (h d) -> p h d", d=HD), yv[jc % 2][:, :].rearrange("p (h d) -> p h d", d=HD),
                                      rden[jc % 2][:, :].unsqueeze(2).to_broadcast([P, HEADS, HD]), ALU.mult).then_inc(sem("y"), 1)
                if "D" in stages:
                    hd_ = h[:, bass.ds(d, 1), :].rearrange("p a d -> p (a d)")
                    dve.wait_ge(sem("tail"), d + 1)
                    dve.tensor_tensor(hd_, hd_, p_proj, ALU.add).then_inc(sem("h1"), 1)
                    dve.wait_ge(sem("h1"), d + 1)
                    need(dve, "mv2", d)
                    alone(dve)
                    dve.bn_stats(st6b[:, :], hd_).then_inc(sem("st2"), 1)
                    dve.wait_ge(sem("st2"), d + 1)
                    need(dve, "x2", d - 1)
                    alone(dve)
                    dve.bn_aggr(mv2[jd % 2][:, 0:2], st6b[:, :]).then_inc(sem("mv2"), 1)
                    dve.wait_ge(sem("mv2"), d + 1)
                    need(dve, "rs2", d - 1)
                    dve.tensor_scalar(mv2[jd % 2][:, 2:3], mv2[jd % 2][:, 1:2], EPS, None, ALU.add).then_inc(sem("ve2"), 1)
                if "F" in stages:
                    dve.wait_ge(sem("tail"), f + 3)
                    dve.tensor_tensor(before[:, :], before[:, :], member[jf % 2][:, :], ALU.add).then_inc(sem("before"), 1)
                    dve.tensor_tensor(rankc[jf % 2][:, :], p_rank, ecap, ALU.add).then_inc(sem("rankc"), 1)
                    dve.wait_ge(sem("rankc"), f + 1)
                    dve.tensor_tensor(slp[jf % 2][:, :, :], pick[jf % 2][:, :, :], rankc[jf % 2][:, :].unsqueeze(1).to_broadcast([P, 2, EXPERTS]),
                                      ALU.mult).then_inc(sem("slp"), 1)
                    dve.wait_ge(sem("slp"), f + 1)
                    dve.tensor_reduce(slf[jf % 2][:, :], slp[jf % 2][:, :, :], AX.X, ALU.add).then_inc(sem("slf"), 1)
                    dve.wait_ge(sem("slf"), f + 1)
                    scattered(dve, f - 3, jf - 3)
                    dve.tensor_tensor(slu[jf % 4][:, :], slf[jf % 2][:, :],
                                      cst[:, bass.ds(C_SPARE + 2 * f, 2)], ALU.add).then_inc(sem("slot"), 1)
                if "D" in stages:
                    dve.wait_ge(sem("rs2"), d + 1)
                    scattered(dve, d - 4, jd - 4)
                    dve.tensor_scalar(row[0][jd % 4][:, 0:D], hd_, mv2[jd % 2][:, 0:1], rs2[jd % 2][:, :],
                                      ALU.subtract, ALU.mult).then_inc(sem("x2"), 1)

            dve.wait_ge(sem("rs1"), 1)
            norm1(1, 1)
            for n in range(9, NT):
                norm1_stats(n)
            dve.wait_ge(sem("rs1"), 2)
            dve.wait_ge(sem("kcls"), 4)
            dve.wait_ge(sem("row_zero"), 8)
            dve.wait_ge(sem("before_zero"), 8)
            pipeline(dve, step)

            dve.wait_ge(sem("counts"), 1)
            dve.tensor_copy(cnt[:, :], p_rank[0:1, :]).then_inc(sem("cnt"), 1)
            dve.wait_ge(sem("cnt"), 1)
            dve.tensor_copy(cnt_i[0:1, 0:EXPERTS], cnt[:, :]).then_inc(sem("tables"), 1)
            dve.tensor_tensor(over[:, :, :], cnt[:, :].unsqueeze(2).to_broadcast([1, EXPERTS, CHUNKS - 1]),
                              cst[0:1, C_STEP:C_STEP + CHUNKS - 1].unsqueeze(1).to_broadcast([1, EXPERTS, CHUNKS - 1]), ALU.is_gt).then_inc(sem("over"), 1)
            dve.wait_ge(sem("over"), 1)
            dve.tensor_reduce(ntile[:, :], over[:, :, :], AX.X, ALU.add).then_inc(sem("over"), 1)
            dve.memset(startf[:, 0:1], 0.0).then_inc(sem("over"), 1)
            dve.wait_ge(sem("over"), 3)
            dve.tensor_tensor_scan(startf[:, 1:EXPERTS + 1], ones1[:, :], ntile[:, :], 0.0, ALU.add, ALU.add).then_inc(sem("over"), 1)
            dve.wait_ge(sem("over"), 4)
            dve.tensor_copy(start_i[:, 1:EXPERTS + 2], startf[:, :]).then_inc(sem("tables"), 1)
            dve.tensor_tensor(over4[:, :, :], cnt[:, :].unsqueeze(2).to_broadcast([1, EXPERTS, 4]),
                              cst[0:1, C_WIDE:C_WIDE + 4].unsqueeze(1).to_broadcast([1, EXPERTS, 4]), ALU.is_gt).then_inc(sem("over"), 1)
            dve.wait_ge(sem("over"), 5)
            dve.tensor_tensor(over4[:, :, :], over4[:, :, :],
                              cst[0:1, C_WIDE + 4:C_WIDE + 8].unsqueeze(1).to_broadcast([1, EXPERTS, 4]), ALU.mult).then_inc(sem("over"), 1)
            dve.wait_ge(sem("over"), 6)
            dve.tensor_reduce(widef[:, :], over4[:, :, :], AX.X, ALU.add).then_inc(sem("over"), 1)
            dve.wait_ge(sem("over"), 7)
            dve.scalar_tensor_tensor(packedf[:, 1:EXPERTS + 1], widef[:, :], float(PACK_WIDE), startf[:, 1:EXPERTS + 1], ALU.mult, ALU.add).then_inc(sem("over"), 1)
            dve.memset(packedf[:, 0:1], 0.0).then_inc(sem("over"), 1)
            dve.wait_ge(sem("over"), 9)
            dve.scalar_tensor_tensor(packedf[:, 0:EXPERTS], cnt[:, :], float(PACK_COUNT), packedf[:, 0:EXPERTS], ALU.mult, ALU.add).then_inc(sem("over"), 1)
            dve.wait_ge(sem("over"), 10)
            dve.tensor_copy(packed_i[:, :], packedf[:, :]).then_inc(sem("tables"), 1)
            dve.tensor_tensor_scan(widesf[:, :], ones1[:, :], widef[:, :], 0.0, ALU.mult, ALU.add).then_inc(sem("over"), 1)
            dve.wait_ge(sem("over"), 11)
            dve.tensor_copy(wides_i[:, 1:EXPERTS + 1], widesf[:, :]).then_inc(sem("wides"), 1)

            dve.wait_ge(sem("kept"), 4 + 2 * NT)
            dve.tensor_tensor(gmx[:, :, :], logits[:, :, :], top2[:, :, 0:1].to_broadcast([P, NT, EXPERTS]), ALU.subtract).then_inc(sem("g_sub"), 1)
            dve.tensor_tensor(gs2[:, :, :], top2[:, :, 0:2], top2[:, :, 0:1].to_broadcast([P, NT, 2]), ALU.subtract).then_inc(sem("g_sub"), 1)
            dve.wait_ge(sem("g_exp"), 2)
            dve.tensor_reduce(gz[:, :], gmx[:, :, :], AX.X, ALU.add).then_inc(sem("g_w"), 1)
            dve.wait_ge(sem("g_w"), 1)
            dve.reciprocal(gri[:, :], gz[:, :]).then_inc(sem("g_w"), 1)
            dve.wait_ge(sem("g_w"), 2)
            dve.tensor_tensor(wgt[:, :, :], gs2[:, :, :], gri[:, :].unsqueeze(2).to_broadcast([P, NT, 2]), ALU.mult).then_inc(sem("g_w"), 1)
            dve.wait_ge(sem("g_w"), 3)
            dve.scalar_tensor_tensor(gden[:, :], wgt[:, :, 0], 1e-20, wgt[:, :, 1], ALU.add, ALU.add).then_inc(sem("g_w"), 1)
            dve.wait_ge(sem("g_w"), 4)
            dve.reciprocal(gz[:, :], gden[:, :]).then_inc(sem("g_w"), 1)
            dve.wait_ge(sem("g_w"), 5)
            dve.tensor_tensor(wgt[:, :, :], wgt[:, :, :], gz[:, :].unsqueeze(2).to_broadcast([P, NT, 2]), ALU.mult).then_inc(sem("g_w"), 1)

            dve.wait_ge(sem("pad_set"), 2)
            dve.wait_ge(sem("zb_zero"), 2)
            dve.wait_ge(sem("biasT"), 4)
            dve.sem_inc(sem("dest"), 1)
            dve.sem_inc(sem("result"), 1)

            def finish(column, g, wide):
                width = WIDE if wide else P
                dve.wait_ge(sem("l3"), g + 1)
                dve.tensor_scalar(zb[0:BOT, 0:width], p_z[:, 0:width], b3T[:, bass.ds(column, 1)], None, ALU.add).then_inc(sem("z"), 1)
                dve.wait_ge(sem("sent"), g + 1)
                dve.wait_ge(sem("dest"), g + 1)
                dve.tensor_copy(dest_old[:, :], dest_new[:, :]).then_inc(sem("dest_old"), 1)
                dve.wait_ge(sem("l4"), g + 1)
                if wide:
                    dve.tensor_copy(yb[0:HALF, :], PS[0:HALF, 7, 0:2 * D]).then_inc(sem("result"), 1)
                else:
                    dve.tensor_copy(yb[:, 0:D], PS[:, 7, 0:D]).then_inc(sem("result"), 1)

            def tile(e, u, c, g, width, wide):
                pieces, piece = (2, HALF) if width == WIDE else (1, P)
                n = 2 * pieces * piece

                dve.wait_ge(sem("xe_t"), g + 2)
                dve.tensor_copy(xeT[:, 0:n], PS[0:HALF, 0, 0:n]).then_inc(sem("xeT"), 1)
                by_layout(dve, wide, lambda was_wide: finish(e if is_first(c) else e + 1, g, was_wide))
                dve.wait_ge(sem("dest_old"), g + 1)
                dve.tensor_copy(dest_new[0:piece, 0:pieces],
                                buf(u, c)[0:piece, :].rearrange("p (k d) -> p k d", k=2)[:, 0:pieces, D].bitcast(u32)).then_inc(sem("dest"), 1)
                if is_first(c):
                    dve.tensor_copy(bcur[(u + 1) % 2][:, :], b12T[:, bass.ds(e + 1, 1), :].rearrange("p a c -> p (a c)")).then_inc(sem("bcur"), 1)

            dve.tensor_copy(bcur[0][:, :], b12T[:, 0, :]).then_inc(sem("bcur"), 1)
            experts(dve, tile)
            v = packed(dve, EXPERTS)
            tiles = dve.snap(v & (PACK_WIDE - 1))
            by_layout(dve, v & PACK_WIDE, lambda was_wide: finish(EXPERTS, tiles, was_wide))

            dve.wait_ge(sem("g_w"), 6)
            for n in range(NT):
                i, turn = n % OUT_RING, n // OUT_RING
                rows = IMAGES if n == 0 else P
                if n == 0:
                    dve.wait_ge(sem("res_in0"), 32)
                else:
                    dve.wait_ge(sem(f"res_in{i}"), 16 * turn + (32 if i == 0 else 16))
                need(dve, "o2", n - OUT_RING + 1)
                dve.scalar_tensor_tensor(o1[i][0:rows, :], res[i][0:rows, 0, :], wgt[0:rows, n, 0:1], h[0:rows, n, :], ALU.mult, ALU.add).then_inc(sem("o1"), 1)
                dve.wait_ge(sem("o1"), n + 1)
                if turn:
                    dve.wait_ge(sem(f"out{i}"), 32 * turn - (16 if i == 0 else 0))
                dve.scalar_tensor_tensor(o2[i][0:rows, :], res[i][0:rows, 1, :], wgt[0:rows, n, 1:2], o1[i][0:rows, :], ALU.mult, ALU.add).then_inc(sem("o2"), 1)


def constants():
    import numpy as np
    t = np.zeros((P, C_END), np.float32)
    p = np.arange(P)
    t[:, C_ID:C_ID + P] = np.eye(P)
    t[:, C_TRI:C_TRI + P] = p[:, None] < p[None, :]
    freqs = np.float32(1.0) / np.power(np.float32(10000.0), np.arange(0, HD, 2, dtype=np.float32) / np.float32(HD))
    ang = (1 + p % PATCHES).astype(np.float32)[:, None] * freqs.astype(np.float32)[None, :]
    cos, sin = np.cos(ang), np.sin(ang)
    for w, scale in enumerate((HD ** -0.5, 1.0)):
        t[:, C_ROPE_C + w * HD:C_ROPE_C + (w + 1) * HD] = np.repeat(cos, 2, 1) * scale
        t[:, C_ROPE_S + w * HD:C_ROPE_S + (w + 1) * HD] = np.stack([-sin, sin], -1).reshape(P, HD) * scale
    mask = np.zeros((P, HH, KEYS), np.float32)
    mask[:, :, 0:PATCHES] = np.where(np.arange(PATCHES)[None, :] > (p % PATCHES)[:, None], MASKED, 0.0)[:, None, :]
    t[:, C_CAUSAL:C_CAUSAL + HH * KEYS] = mask.reshape(P, -1)
    t[:, C_IOTA:C_IOTA + EXPERTS] = np.arange(EXPERTS)
    t[:, C_ECAP:C_ECAP + EXPERTS] = np.arange(EXPERTS) * CAP
    t[:, C_STEP:C_STEP + CHUNKS - 1] = TILE_STEPS
    t[:, C_WIDE:C_WIDE + 4] = WIDE_STEPS
    t[:, C_WIDE + 4:C_WIDE + 8] = [1, -1, 1, -1]
    t[:HALF, C_HEAD:C_HEAD + HH] = (p[:HALF] // HD)[:, None] == np.arange(HH)[None, :]
    t[:, C_KEEP:C_KEEP + NT] = 1.0
    t[1:, C_KEEP] = 0.0
    t[1:, C_SPARE] = SPARE0 + p[1:]
    t[1:, C_SPARE + 1] = SPARE1 + p[1:]
    t[:, C_PADID] = RESULTS + p
    for ch in range(2):
        t[:, C_DEST + ch * NT:C_DEST + (ch + 1) * NT] = (np.arange(NT)[None, :] * P + p[:, None]) * 2 + ch
    return t


_INS = ['x', 'cls_tok', 'L0_tok_w', 'L0_tok_b', 'L0_attn_norm_scale', 'L0_attn_norm_bias', 'L0_attn_W_attn', 'L0_attn_b_attn',
        'L0_attn_W_proj', 'L0_attn_b_proj', 'L0_attn_sinks', 'L0_attn_rezero', 'L0_ffn_gate_w', 'L0_ffn_W1', 'L0_ffn_b1',
        'L0_ffn_W2', 'L0_ffn_b2', 'L0_ffn_W3', 'L0_ffn_b3', 'L0_ffn_Wl', 'L0_ffn_bl']


def kernel(**inputs):
    import numpy as _np
    import concourse.bacc as _bacc
    from concourse import mybir as _mybir
    from concourse.bass_utils import run_bass_kernel_spmd as _run

    nc = _bacc.Bacc("TRN2", target_bir_lowering=False, num_devices=1)
    arrays, args = {}, []
    for name in _INS + ["table"]:
        a = constants() if name == "table" else _np.ascontiguousarray(inputs[name])
        arrays[f"in_{name}_dram"] = a
        args.append(nc.dram_tensor(f"in_{name}_dram", a.shape, _mybir.dt.from_np(a.dtype), kind="ExternalInput").ap())
    args.append(nc.dram_tensor("out_0_dram", (IMAGES, KEYS, D), _mybir.dt.float32, kind="ExternalOutput").ap())
    vit_moe_kernel(nc, *args)
    r = _run(nc, [arrays], core_ids=[0])
    return r.results[0]["out_0_dram"]
```

```python
import concourse.bass as bass
from concourse import mybir
from contextlib import ExitStack

IMAGES, SIDE, PATCH = 32, 256, 32
D = 192
GRID = SIDE // PATCH
PATCHES = GRID * GRID
DP = PATCH * PATCH
HEADS, HD = 12, 16
EXPERTS, HID, BOT = 32, 512, 64
P = 128
HALF = D // 2
HH = HEADS // 2
TILE_IMAGES = P // PATCHES
TILES = IMAGES // TILE_IMAGES
NT = TILES + 1
GROUPS = DP // P
ROWS = P // PATCH
KEYS = PATCHES + 1
EPS = 1e-5
MASKED = -1e30

TOKENS = IMAGES * PATCHES + 1
CHUNKS = -(-TOKENS // P)
CAP = TOKENS + P
ROW = D + 2
SPARE2 = EXPERTS * CAP
SPARE0 = SPARE2 + CAP
SPARE1 = SPARE0 + P
SLOTS = SPARE1 + P
WIDE = 2 * HALF
TILE_STEPS = [WIDE, P + WIDE, 3 * P] + [P * c for c in range(4, CHUNKS)]
WIDE_STEPS = [P, WIDE, 2 * P, P + WIDE]
PACK_WIDE, PACK_COUNT = 128, 256
RESULTS = NT * P * 2
LOOP_START, LOOP_TURNS = 8, 2
LOOP_END = LOOP_START + 4 * LOOP_TURNS
OUT_GROUPS = [(1, 5), (5, 9), (9, 13), (13, 15), (15, 17)]
RING = 4

C_ID, C_TRI, C_ROPE_C, C_ROPE_S = 0, P, 2 * P, 2 * P + 2 * HD
C_CAUSAL = C_ROPE_S + 2 * HD
C_IOTA = C_CAUSAL + HH * KEYS
C_ECAP = C_IOTA + EXPERTS
C_STEP = C_ECAP + EXPERTS
C_WIDE = C_STEP + CHUNKS - 1
C_HEAD = C_WIDE + 8
C_KEEP = C_HEAD + HH
C_SPARE = C_KEEP + NT
C_PADID = C_SPARE + 2 * NT
C_DEST = C_PADID + 1
C_END = C_DEST + 2 * NT


def vit_moe_kernel(nc, x, cls_tok, tok_w, tok_b, n_scale, n_bias, w_attn, b_attn, w_proj, b_proj,
                   sinks, rezero, gate_w, w1, b1, w2, b2, w3, b3, wl, bl, table, out):
    f32, bf16 = mybir.dt.float32, mybir.dt.bfloat16
    i32, u32 = mybir.dt.int32, mybir.dt.uint32
    ALU, ACT, AX = mybir.AluOpType, mybir.ActivationFunctionType, mybir.AxisListType

    slots = nc.dram_tensor("slots", (SLOTS, ROW), f32).ap()
    results = nc.dram_tensor("results", (RESULTS + P, D), f32).ap()
    x_v = x.rearrange("b c (i g r) w -> (b c i) g (r w)", i=GRID, g=GROUPS)
    res_v = results[0:RESULTS, :].rearrange("(n p k) d -> p n (k d)", p=P, k=2)
    out_v = out.rearrange("(n b) t d -> b t n d", b=TILE_IMAGES)

    ctx = ExitStack()
    with ctx:
        def sb(name, shape, dt=f32):
            return ctx.enter_context(nc.sbuf_tensor(name, shape, dt))

        sems = {}

        def sem(name):
            if name not in sems:
                sems[name] = ctx.enter_context(nc.semaphore(name))
            return sems[name]

        def need(eng, name, value):
            if not isinstance(value, int) or value > 0:
                eng.wait_ge(sem(name), value)

        def alone(eng):
            eng.nop(nofuse=True)

        cst = sb("cst", [P, C_END])
        ident = cst[:, C_ID:C_ID + P]
        causal = sb("causal", [P, HH * KEYS], bf16)
        identb = sb("identb", [P, P], bf16)
        earlier = sb("earlier", [P, P], bf16)
        onesb = sb("onesb", [P, P], bf16)
        iota = cst[:, C_IOTA:C_IOTA + EXPERTS]
        ecap = cst[:, C_ECAP:C_ECAP + EXPERTS]
        scratch = sb("scratch", [P, 2 * DP])
        tokw = scratch[0:HALF, :].rearrange("p (c n) -> p c n", c=2)
        h1b = scratch[:, 0:4 * WIDE].rearrange("p (c t) -> p c t", c=4)
        h2b = scratch[:, 4 * WIDE:8 * WIDE].rearrange("p (c t) -> p c t", c=4)
        xeT = scratch[0:HALF, 8 * WIDE:10 * WIDE]
        tokwT = sb("tokwT", [P, GROUPS, D])
        tokb = sb("tokb", [P, D])
        scalec = sb("scalec", [HALF, 2])
        biasc = sb("biasc", [HALF, 2])
        wa = sb("wa", [HALF + 1, 2, 3 * D])
        was = sb("was", [HALF + 1, 2, 3 * D])
        wp = sb("wp", [HALF + 1, 2, D])
        wps = sb("wps", [HALF + 1, 2, D])
        rez = sb("rez", [HALF + 1, 1])
        sinkb = sb("sinkb", [P, HEADS])
        gw = sb("gw", [EXPERTS, D])
        gwT = sb("gwT", [HALF, 2, EXPERTS])
        b3r = sb("b3r", [EXPERTS, BOT])
        b12T = sb("b12T", [P, EXPERTS + 1, 8])
        bcur = [sb(f"bcur{i}", [P, 8]) for i in range(2)]
        b3T = sb("b3T", [BOT, EXPERTS + 1])
        raw = [sb(f"raw{i}", [P, ROWS * SIDE]) for i in range(4)]
        pix = [sb(f"pix{i}", [P, P * GRID]) for i in range(2)]
        b1r = pix[1][0:EXPERTS, 0:HID]
        b2r = pix[1][0:EXPERTS, HID:2 * HID]
        h = sb("h", [P, NT, D])
        st6 = sb("st6", [P, 6])
        mv = sb("mv", [P, NT, 2])
        ve1 = sb("ve1", [P, NT])
        rs1 = sb("rs1", [P, NT])
        mr1 = sb("mr1", [P, NT])
        zeros8 = sb("zeros8", [P, 8])
        mhalf = sb("mhalf", [P, NT])
        xhat = [sb(f"xhat{i}", [P, D]) for i in range(2)]
        xT = [sb(f"xT{i}", [HALF + 1, 2, P]) for i in range(2)]
        rope_c = [sb(f"ropec{i}", [P, 2 * D]) for i in range(2)]
        rope_s = [sb(f"ropes{i}", [P, 2 * D]) for i in range(2)]
        qk = [sb(f"qk{i}", [P, 2 * D]) for i in range(2)]
        qkT = [sb(f"qkT{i}", [HALF, 4, P]) for i in range(2)]
        kblk = [[sb(f"kblk{i}{b}", [HALF, 2, HH, KEYS]) for b in range(2)] for i in range(2)]
        vblk = [sb(f"vblk{i}", [P, 2, HH, 2, HD + 1]) for i in range(4)]
        mx = [sb(f"mx{i}", [P, HEADS]) for i in range(2)]
        probs = [sb(f"probs{i}", [P, HEADS * (PATCHES + 2)]) for i in range(2)]
        p_patch = [t[:, 0:HEADS * PATCHES] for t in probs]
        p_class = [t[:, HEADS * PATCHES:HEADS * KEYS] for t in probs]
        p_sink = [t[:, HEADS * KEYS:HEADS * (KEYS + 1)] for t in probs]
        pT = [sb(f"pT{i}", [P, HH, P]) for i in range(2)]
        vcls = sb("vcls", [P, D])
        pvc = [sb(f"pvc{i}", [P, D]) for i in range(2)]
        psum2 = [sb(f"psum2{i}", [P, HEADS]) for i in range(2)]
        den = [sb(f"den{i}", [P, HEADS]) for i in range(2)]
        rden = [sb(f"rden{i}", [P, HEADS]) for i in range(2)]
        yv = [sb(f"yv{i}", [P, D]) for i in range(2)]
        y = [sb(f"y{i}", [P, D]) for i in range(2)]
        yT = [sb(f"yT{i}", [HALF + 1, 2, P]) for i in range(2)]
        st6b = sb("st6b", [P, 6])
        mv2 = [sb(f"mv2{i}", [P, 3]) for i in range(2)]
        rs2 = [sb(f"rs2{i}", [P, 1]) for i in range(2)]
        row = [[sb(f"row{c}{i}", [P, ROW]) for i in range(4)] for c in range(2)]
        x2T = [sb(f"x2T{i}", [HALF, 2, P]) for i in range(2)]
        logits = sb("logits", [P, NT, EXPERTS])
        top2 = sb("top2", [P, NT, 2])
        lgs = [sb(f"lgs{i}", [P, EXPERTS]) for i in range(2)]
        top8 = [sb(f"top8{i}", [P, 8]) for i in range(2)]
        idx8 = [sb(f"idx8{i}", [P, 8], u32) for i in range(2)]
        idxf = [sb(f"idxf{i}", [P, 2]) for i in range(2)]
        pick = [sb(f"pick{i}", [P, 2, EXPERTS]) for i in range(2)]
        member = [sb(f"member{i}", [P, EXPERTS], bf16) for i in range(2)]
        before = sb("before", [P, EXPERTS], bf16)
        rankc = [sb(f"rankc{i}", [P, EXPERTS]) for i in range(2)]
        slp = [sb(f"slp{i}", [P, 2, EXPERTS]) for i in range(2)]
        slf = [sb(f"slf{i}", [P, 2]) for i in range(2)]
        sls = [sb(f"sls{i}", [P, 2]) for i in range(2)]
        slu = [sb(f"slu{i}", [P, 2], u32) for i in range(4)]
        wgt = sb("wgt", [P, NT, 2])
        gmx = sb("gmx", [P, NT, EXPERTS])
        gz = sb("gz", [P, NT])
        gri = sb("gri", [P, NT])
        gs2 = sb("gs2", [P, NT, 2])
        gden = sb("gden", [P, NT])
        cnt = sb("cnt", [1, EXPERTS])
        over = sb("over", [1, EXPERTS, CHUNKS - 1])
        ntile = sb("ntile", [1, EXPERTS])
        ones1 = sb("ones1", [1, EXPERTS])
        over4 = sb("over4", [1, EXPERTS, 4])
        widef = sb("widef", [1, EXPERTS])
        startf = sb("startf", [1, EXPERTS + 1])
        cnt_i = sb("cnt_i", [1, EXPERTS + 1], i32)
        packedf = sb("packedf", [1, EXPERTS + 1])
        packed_i = sb("packed_i", [1, EXPERTS + 1], i32)
        widesf = sb("widesf", [1, EXPERTS])
        wides_i = sb("wides_i", [1, EXPERTS + 1], i32)
        start_i = sb("start_i", [1, EXPERTS + 2], i32)
        W1 = [sb(f"W1_{i}", [HALF, 2, HID]) for i in range(RING)]
        W2 = [sb(f"W2_{i}", [P, 4, HID]) for i in range(RING)]
        blocks = [W2[RING - 1][:, 2 * i:2 * i + 2, :].rearrange("p a (j n) -> p (a j) n", j=4) for i in range(2)]
        W3 = [sb(f"W3_{i}", [P, 4, BOT]) for i in range(RING)]
        WL = [sb(f"WL_{i}", [P, D]) for i in range(RING)]
        pad = sb("pad", [P, ROW])
        xs = [[raw[2 * a + b][:, 0:2 * ROW] for b in range(2)] for a in range(2)]
        yb = raw[0][:, 2 * ROW:2 * ROW + 2 * D]
        zb = sb("zb", [P, WIDE])
        dest_new = sb("dest_new", [P, 2], u32)
        dest_old = sb("dest_old", [P, 2], u32)
        res_cls = W1[0][0:IMAGES, 0, 0:2 * D]
        res = [w[:, :, :].rearrange("p a n -> p (a n)")[:, 0:8 * D].rearrange("p (n k) -> p n k", n=4) for w in W2]

        PS = ctx.enter_context(nc.psum_tensor("PS", [P, 8, 512], f32))
        p_xT = PS[0:HALF, 0, 0:256].rearrange("p (c t) -> p c t", c=2)
        p_v = PS[:, 0, 256:256 + D]
        p_qkT = PS[0:HALF, 1, :].rearrange("p (c t) -> p c t", c=4)
        p_yT = PS[0:HALF, 1, 0:256].rearrange("p (c t) -> p c t", c=2)
        p_x2T = PS[0:HALF, 1, 256:512].rearrange("p (c t) -> p c t", c=2)
        p_qk = PS[:, 2, 0:2 * D]
        p_pTa = PS[:, 3, :].rearrange("p (g t) -> p g t", g=4)
        p_pTb = PS[:, 4, 0:256].rearrange("p (g t) -> p g t", g=2)
        p_y = PS[:, 4, 256:256 + HEADS * (HD + 1)].rearrange("p (h d) -> p h d", d=HD + 1)
        p_s = PS[:, 5:7, 0:HH * KEYS].rearrange("p c (g k) -> p c g k", k=KEYS)
        p_proj = PS[:, 7, 0:D]
        c_xT = PS[0:HALF, 6, 0:256].rearrange("p (c t) -> p c t", c=2)
        c_v = PS[:, 6, 256:256 + D]
        c_qk = PS[:, 7, 0:2 * D]
        p_gate = PS[:, 7, D:D + EXPERTS]
        p_rank = PS[:, 7, D + EXPERTS:D + 2 * EXPERTS]

        L1_BANKS, L2_BANKS = (1, 2, 3, 4), (5, 6, 1, 2)
        p_z = PS[0:BOT, 4, :]

        INIT = 15

        block = ctx.enter_context(nc.Block())

        def scattered(eng, n, jn):
            if not isinstance(n, int) or n >= 0:
                for ch in range(2):
                    eng.wait_ge(sem(f"scattered{ch}{jn % 4}"), 4 * (n - jn % 4) + 16)

        def pipeline(eng, step):
            def stages(k):
                s = {c for i, c in enumerate("ABC") if 1 <= k - i < NT}
                return s | {c for i, c in enumerate("DEFG", 3) if 0 <= k - i < NT}
            for k in range(1, LOOP_START):
                step(k, k, stages(k))
            with eng.Fori(0, LOOP_TURNS) as q:
                for j in range(4):
                    step(4 * q + LOOP_START + j, LOOP_START + j, set("ABCDEFG"))
            for k in range(LOOP_END, NT + 6):
                step(k, k, stages(k))

        def walk(eng, more, s, tile, wide):
            with eng.If(more(WIDE)):
                tile(0, s, P, wide)
                with eng.If(more(P + WIDE)):
                    tile(1, s + 1, P, False)
                    tile(2, s + 2, P, False)
                    with eng.If(more(3 * P)):
                        with eng.Fori(3, CHUNKS) as c:
                            with eng.If(more(c * P)):
                                tile(c, s + c, P, False)
                            eng.nop()
                    eng.nop()
                with eng.Else():
                    with eng.If(more(2 * P)):
                        tile(1, s + 1, WIDE, False)
                    with eng.Else():
                        tile(1, s + 1, P, False)
                    eng.nop()
                eng.nop()
            with eng.Else():
                with eng.If(more(P)):
                    tile(0, s, WIDE, wide)
                with eng.Else():
                    tile(0, s, P, wide)
                eng.nop()
            eng.nop()

        def experts(eng, tile, enter=None, layouts=True):
            eng.wait_ge(sem("tables"), 3)
            with eng.Fori(0, EXPERTS // RING) as q:
                for u in range(RING):
                    e = RING * q + u
                    v = packed(eng, e)
                    s = eng.snap(v & (PACK_WIDE - 1))
                    if enter:
                        enter(RING * q, u)
                    walk(eng, lambda x: v >= (x + 1) * PACK_COUNT, s,
                         lambda c, g, width, wide: tile(e, u, c, g, width, wide), v & PACK_WIDE if layouts else False)

        def packed(eng, e):
            return eng.value_load(packed_i[0:1, bass.ds(e, 1)], min_val=0, max_val=(TOKENS + 1) * PACK_COUNT - 1)

        def by_layout(eng, wide, do):
            if wide is False:
                do(False)
            else:
                with eng.If(wide > 0):
                    do(True)
                with eng.Else():
                    do(False)
                eng.nop()

        def is_first(c):
            return isinstance(c, int) and c == 0

        def buf(u, c):
            return xs[u % 2][0 if isinstance(c, int) and c in (0, 2) else 1]

        @block.sync
        def _(sp):
            sp.dma_start(cst[:, :], table).then_inc(sem("cst_in"), 16)
            sp.dma_start(tokw[:, :, :], tok_w.rearrange("(c p) n -> p c n", p=HALF)).then_inc(sem("tokw_in"), 16)
            for n in range(2):
                sp.dma_start(raw[n][:, :], x_v[0:P, n, :]).then_inc(sem(f"raw_in{n}"), 16)
            sp.dma_start(sinkb[:, :], sinks.rearrange("(a n) -> a n", a=1).broadcast_to([P, HEADS])).then_inc(sem("sink_in"), 16)
            sp.dma_start(wp[0:HALF, :, :], w_proj.rearrange("(c p) n -> p c n", p=HALF)).then_inc(sem("wp_in"), 16)
            sp.dma_start(wp[HALF:HALF + 1, 1, :], b_proj.rearrange("(a n) -> a n", a=1)).then_inc(sem("wp_in"), 16)
            sp.dma_start(rez[:, :], rezero.rearrange("(a n) -> a n", a=1).broadcast_to([HALF + 1, 1])).then_inc(sem("wp_in"), 16)
            sp.dma_start(gw[:, :], gate_w).then_inc(sem("bias_in"), 16)
            sp.dma_start(b1r[:, :], b1).then_inc(sem("bias_in"), 16)
            sp.dma_start(b2r[:, :], b2).then_inc(sem("bias_in"), 16)
            sp.dma_start(b3r[:, :], b3).then_inc(sem("bias_in"), 16)
            sp.dma_start(tokb[:, :], tok_b.rearrange("(a n) -> a n", a=1).broadcast_to([P, D])).then_inc(sem("tokb_in"), 16)
            for n in range(2, 4):
                sp.dma_start(raw[n][:, :], x_v[0:P, n, :]).then_inc(sem(f"raw_in{n}"), 16)
            def expert_load(slot, e):
                w_in = sem(f"w_in{slot}")
                one = bass.ds(e, 1)
                sp.dma_start(W1[slot][:, :, :], w1[one].rearrange("a (c p) n -> p (a c) n", p=HALF)).then_inc(w_in, 16)
                sp.dma_start(W2[slot][:, :, :], w2[one].rearrange("a (c p) n -> p (a c) n", p=P)).then_inc(w_in, 16)
                sp.dma_start(W3[slot][:, :, :], w3[one].rearrange("a (c p) n -> p (a c) n", p=P)).then_inc(w_in, 16)
                sp.dma_start(WL[slot][0:BOT, :], wl[one].rearrange("a p n -> (a p) n")).then_inc(w_in, 16)
                sp.dma_start(WL[slot][BOT:BOT + 1, :], bl[one, :]).then_inc(w_in, 16)
            for n in range(4, 2 * GROUPS):
                sp.wait_ge(sem("blocks"), n - 3)
                half, g = n // GROUPS, n % GROUPS
                sp.dma_start(raw[n % 4][:, :], x_v[half * P:(half + 1) * P, g, :]).then_inc(sem(f"raw_in{n % 4}"), 16)
            sp.wait_ge(sem("init"), INIT)
            for e in range(2):
                expert_load(e, e)
            sp.wait_ge(sem("tables"), 1)
            sp.wait_ge(sem("pad_set"), 1)
            n0 = sp.value_load(cnt_i[0:1, 0:1], min_val=0, max_val=TOKENS)
            sp.dma_start(slots[bass.ds(n0, P), :], pad[:, :]).then_inc(sem("pad_out0"), 16)
            sp.wait_ge(sem("tables"), 3)

            def xs_load(e, u, c, g, free, width):
                sp.wait_ge(sem("xe_t"), free)
                sp.wait_ge(sem("dest"), free)
                sp.wait_ge(sem("xs_in"), 16 * g + 16)
                if width == WIDE:
                    sp.dma_start(buf(u, c)[0:HALF, :].rearrange("p (k d) -> p k d", k=2),
                                 slots[bass.ds(e * CAP + c * P, WIDE), :].rearrange("(k p) d -> p k d", p=HALF)).then_inc(sem("xs_in"), 16)
                else:
                    sp.dma_start(buf(u, c)[:, 0:ROW],
                                 slots[bass.ds(e * CAP + c * P, P), :]).then_inc(sem("xs_in"), 16)

            def group(e0, full):
                for u in range(RING):
                    e = e0 + u
                    n = sp.value_load(cnt_i[0:1, bass.ds(e, 1)], min_val=0, max_val=TOKENS)
                    s = sp.value_load(start_i[0:1, bass.ds(e + 1, 1)], min_val=0, max_val=2 * EXPERTS)
                    back = sp.value_load(start_i[0:1, bass.ds(e, 1)], min_val=0, max_val=2 * EXPERTS)
                    sp.wait_ge(sem(f"pad_out{u % 2}"), 8 * e0 + 16 * (u // 2 + 1))
                    alone(sp)
                    def load(c, g, width, _):
                        free = back + 1 if isinstance(c, int) and c < 2 else s + 2 if isinstance(c, int) else s + c + 1
                        xs_load(e, u, c, g, free, width)
                    walk(sp, lambda x: n > x, s, load, False)
                    nn = sp.value_load(cnt_i[0:1, bass.ds(e + 1, 1)], min_val=0, max_val=TOKENS)
                    sp.dma_start(slots[bass.ds((e + 1) * CAP + nn, P), :], pad[:, :]).then_inc(sem(f"pad_out{(u + 1) % 2}"), 16)
                    if full or u < RING - 2:
                        sp.wait_ge(sem("l4"), back + 1)
                        alone(sp)
                        expert_load((u + 2) % RING, e + 2)

            with sp.Fori(0, EXPERTS // RING - 1) as q:
                group(RING * q, True)
            group(EXPERTS - RING, False)

            tiles = sp.value_load(start_i[0:1, EXPERTS + 1:EXPERTS + 2], min_val=EXPERTS, max_val=2 * EXPERTS)
            sp.wait_ge(sem("sent"), tiles + 2)
            sp.wait_ge(sem("pad_out0"), 8 * EXPERTS + 16)
            sp.wait_ge(sem("pad_out1"), 8 * EXPERTS)
            for i, (n0, n1) in enumerate(OUT_GROUPS):
                m = (n0 - 1) % 4
                sp.dma_start(res[(n0 - 1) // 4][:, m:m + n1 - n0, :], res_v[:, n0:n1, :]).then_inc(sem(f"res_in{i}"), 16)
            sp.dma_start(res_cls, bass.AP(results.tensor, 0, [[0, IMAGES], [1, 2 * D]])).then_inc(sem("cls_res"), 16)
            for i, (n0, n1) in enumerate(OUT_GROUPS):
                sp.wait_ge(sem("o2"), i + 1)
                m = (n0 - 1) % 4
                for b_ in range(2):
                    sp.dma_start(out_v[b_, 1:KEYS, n0 - 1:n1 - 1, :],
                                 res[(n0 - 1) // 4][b_ * PATCHES:(b_ + 1) * PATCHES, m:m + n1 - n0, D:2 * D]).then_inc(sem("out"), 16)
            sp.wait_ge(sem("o2"), len(OUT_GROUPS) + 1)
            sp.dma_start(out[:, 0, :], res_cls[:, D:2 * D]).then_inc(sem("out"), 16)
            sp.wait_ge(sem("out"), 16 * (2 * len(OUT_GROUPS) + 1))

        @block.gpsimd
        def _(pool):
            pool.memset(pad[:, :], 0.0).then_inc(sem("pad_zero"), 1)
            pool.wait_ge(sem("pad_zero"), 1)
            pool.wait_ge(sem("cst_in"), 16)
            pool.tensor_copy(pad[:, D:D + 1].bitcast(u32), cst[:, C_PADID:C_PADID + 1]).then_inc(sem("pad_set"), 1)
            pool.tensor_copy(dest_new[:, :], cst[:, C_PADID:C_PADID + 1].to_broadcast([P, 2])).then_inc(sem("pad_set"), 1)
            pool.sem_inc(sem("kept"), 4)
            pool.wait_ge(sem("cls_ve"), 1)
            pool.tensor_tensor(rs1[:, 0:1], ve1[:, 0:1], mhalf[:, 0:1], ALU.pow).then_inc(sem("cls_rs"), 1)
            def norm1_scale(hf):
                part = slice(8 * hf + 1, 8 * hf + 9)
                pool.wait_ge(sem("ve1"), hf + 1)
                pool.tensor_tensor(rs1[:, part], ve1[:, part], mhalf[:, 0:8], ALU.pow).then_inc(sem("rs1"), 1)
                pool.wait_ge(sem("rs1"), 2 * hf + 1)
                pool.tensor_tensor(mr1[:, part], mv[:, part, 0], rs1[:, part], ALU.mult).then_inc(sem("rs1"), 1)
                pool.wait_ge(sem("rs1"), 2 * hf + 2)
                pool.tensor_tensor(mr1[:, part], zeros8[:, :], mr1[:, part], ALU.subtract).then_inc(sem("mr1"), 1)
            norm1_scale(0)

            def step(k, j, stages):
                a, b, c, d, e, _, f = (k - i for i in range(7))
                ja, jb, jc, jd, je, _, jf = (j - i for i in range(7))
                if "B" in stages:
                    pool.wait_ge(sem("qkT"), b)
                    need(pool, "scores", b - 2)
                    for half in range(2):
                        ins = pool.tensor_tensor(
                            kblk[jb % 2][1][:, half, :, 0:PATCHES],
                            qkT[jb % 2][:, 2 + half:3 + half, PATCHES:P].to_broadcast([HALF, HH, PATCHES]),
                            cst[0:HALF, C_HEAD:C_HEAD + HH].unsqueeze(2).to_broadcast([HALF, HH, PATCHES]), ALU.mult)
                    ins.then_inc(sem("kblk1"), 1)
                if "E" in stages:
                    pool.wait_ge(sem("ve2"), e + 1)
                    need(pool, "x2", e - 1)
                    pool.tensor_tensor(rs2[je % 2][:, :], mv2[je % 2][:, 2:3], mhalf[:, 0:1], ALU.pow).then_inc(sem("rs2"), 1)
                if "G" in stages:
                    pool.wait_ge(sem("slot"), f + 1)
                    pool.wait_ge(sem("row"), 3 * f + 3)
                    alone(pool)
                    for ch in range(2):
                        pool.indirect_dma_start(
                            out=slots, out_offset=bass.IndirectOffsetOnAxis(ap=slu[jf % 4][:, ch:ch + 1], axis=0),
                            in_=row[ch][jf % 4][:, :], in_offset=None).then_inc(sem(f"scattered{ch}{jf % 4}"), 16)
                if "A" in stages:
                    pool.wait_ge(sem("rope_c"), a)
                    pool.wait_ge(sem("rope_s"), a)
                    need(pool, "qk_t", a - 2)
                    pool.tensor_tensor(qk[ja % 2][:, :], rope_c[ja % 2][:, :], rope_s[ja % 2][:, :], ALU.add).then_inc(sem("qk"), 1)
                if "C" in stages:
                    pool.wait_ge(sem("exp"), c)
                    need(pool, "yv", c - 2)
                    need(pool, "den", c - 2)
                    pool.tensor_tensor(pvc[jc % 2][:, :].rearrange("p (h d) -> p h d", d=HD),
                                       p_class[jc % 2].unsqueeze(2).to_broadcast([P, HEADS, HD]),
                                       vcls[:, :].rearrange("p (h d) -> p h d", d=HD), ALU.mult).then_inc(sem("pvc"), 1)
                    pool.tensor_tensor(psum2[jc % 2][:, :], p_class[jc % 2], p_sink[jc % 2], ALU.add).then_inc(sem("psum2"), 1)
                if "E" in stages:
                    pool.wait_ge(sem("x2"), e + 1)
                    scattered(pool, e - 4, je - 4)
                    alone(pool)
                    pool.tensor_copy(row[1][je % 4][:, 0:D], row[0][je % 4][:, 0:D]).then_inc(sem("row"), 1)
                    for ch in range(2):
                        pool.tensor_copy(row[ch][je % 4][:, D:D + 1].bitcast(u32),
                                         cst[:, bass.ds(C_DEST + ch * NT + e, 1)]).then_inc(sem("row"), 1)
                if "G" in stages:
                    pool.wait_ge(sem("top8"), f + 1)
                    pool.tensor_copy(logits[:, bass.ds(f, 1), :].rearrange("p a e -> p (a e)"), lgs[jf % 2][:, :]).then_inc(sem("kept"), 1)
                    pool.tensor_copy(top2[:, bass.ds(f, 1), :].rearrange("p a e -> p (a e)"), top8[jf % 2][:, 0:2]).then_inc(sem("kept"), 1)
                if isinstance(k, int) and k == 5:
                    norm1_scale(1)

            pipeline(pool, step)
            for n in range(NT - 4, NT):
                scattered(pool, n, n)
            pool.sem_inc(sem("xs_in"), 16)

            pool.sem_inc(sem("sent"), 1)
            def send(e, g, wide):
                pool.wait_ge(sem("result"), g + 2)
                alone(pool)
                def parts(was_wide):
                    for k in range(1 + was_wide):
                        rows = HALF if was_wide else P
                        pool.indirect_dma_start(
                            out=results, out_offset=bass.IndirectOffsetOnAxis(ap=dest_old[0:rows, k:k + 1], axis=0),
                            in_=yb[0:rows, k * D:(k + 1) * D], in_offset=None).then_inc(sem(("result_out", "second_out")[k]), 16)
                    if was_wide:
                        wides = pool.value_load(wides_i[0:1, bass.ds(e, 1)], min_val=1, max_val=EXPERTS)
                        pool.wait_ge(sem("second_out"), 16 * wides)
                by_layout(pool, wide, parts)
                pool.wait_ge(sem("result_out"), 16 * g + 16)
                pool.sem_inc(sem("sent"), 1)

            pool.wait_ge(sem("wides"), 5)
            experts(pool, lambda e, u, c, g, width, wide: send(e, g, wide))
            v = packed(pool, EXPERTS)
            send(EXPERTS, pool.snap(v & (PACK_WIDE - 1)), v & PACK_WIDE)

        @block.scalar
        def _(act):
            act.dma_start(h[:, 0, :], cls_tok.rearrange("a b d -> (a b) d").broadcast_to([P, D])).then_inc(sem("cls_in"), 16)
            act.dma_start(wa[0:HALF, :, :], w_attn.rearrange("(c p) n -> p c n", p=HALF)).then_inc(sem("wa_in"), 16)
            act.dma_start(wa[HALF:HALF + 1, 1, :], b_attn.rearrange("(a n) -> a n", a=1)).then_inc(sem("wa_in"), 16)
            with nc.allow_non_contiguous_dma("per-feature scale and bias, once"):
                act.dma_start(scalec[:, :], n_scale.rearrange("(c p) -> p c", p=HALF)).then_inc(sem("wa_in"), 16)
                act.dma_start(biasc[:, :], n_bias.rearrange("(c p) -> p c", p=HALF)).then_inc(sem("wa_in"), 16)
            def sort_pixels(n):
                act.wait_ge(sem(f"raw_in{n % 4}"), 16 * (n // 4 + 1))
                need(act, "pix_t", n - 1)
                act.activation(blocks[n % 2][:, :, :].rearrange("p j (r c) -> p j r c", r=ROWS),
                               raw[n % 4][:, :].rearrange("p (r j c) -> p j r c", r=ROWS, j=GRID), ACT.Copy).then_inc(sem("blocks"), 1)
            sort_pixels(0)
            for q in range(4):
                act.wait_ge(sem("tokw_t"), q + 1)
                act.activation(tokwT[:, 2 * q:2 * q + 2, :], PS[:, q, 0:2 * D].rearrange("p (g n) -> p g n", g=2), ACT.Copy).then_inc(sem("tokwT"), 1)
            act.wait_ge(sem("bias_t"), 1)
            for w in range(2):
                act.activation(b12T[:, 0:EXPERTS, 4 * w:4 * w + 4], PS[:, 7, w * P:(w + 1) * P].rearrange("p (c e) -> p e c", c=4), ACT.Copy).then_inc(sem("biasT"), 1)
            act.activation(gwT[:, :, :], PS[0:HALF, 7, 2 * P:2 * P + 64].rearrange("p (c e) -> p c e", c=2), ACT.Copy).then_inc(sem("biasT"), 1)
            act.activation(b3T[:, 1:EXPERTS + 1], PS[0:BOT, 7, 320:352], ACT.Copy).then_inc(sem("biasT"), 1)
            sort_pixels(1)
            act.wait_ge(sem("cst_in"), 16)
            act.activation(identb[:, :], ident, ACT.Copy).then_inc(sem("tab"), 1)
            act.activation(earlier[:, :], cst[:, C_TRI:C_TRI + P], ACT.Copy).then_inc(sem("tab"), 1)
            act.activation(causal[:, :], cst[:, C_CAUSAL:C_CAUSAL + HH * KEYS], ACT.Copy).then_inc(sem("tab"), 1)
            for hf in range(2):
                for g in range(GROUPS):
                    n = hf * GROUPS + g
                    act.wait_ge(sem("pix_t"), n + 1)
                    need(act, "embed", n - 1)
                    act.activation(pix[n % 2][:, :].rearrange("p (t j) -> p j t", j=GRID)[:, 0:4, :],
                                   PS[:, 4 + 2 * (n % 2), :].rearrange("p (j t) -> p j t", j=4), ACT.Copy).then_inc(sem("pix_a"), 1)
                    if n + 2 < 2 * GROUPS:
                        sort_pixels(n + 2)
                    if n == GROUPS:
                        act.wait_ge(sem("cls_xt"), 1)
                        act.activation(xT[0][0:HALF, :, :], c_xT, ACT.Copy).then_inc(sem("cls_xT"), 1)
                        act.wait_ge(sem("cls_qkv"), 1)
                        act.activation(qk[0][:, D:2 * D], c_qk[:, D:2 * D], ACT.Copy).then_inc(sem("cls_qk"), 1)
                        act.activation(qk[0][:, 0:D], c_qk[:, 0:D], ACT.Copy, scale=HD ** -0.5).then_inc(sem("cls_qk"), 1)
                        act.activation(vcls[:, :], c_v, ACT.Copy).then_inc(sem("vcls"), 1)
                        act.wait_ge(sem("cls_kt"), 1)
                        act.activation(qkT[0][:, 2:4, :], c_xT, ACT.Copy).then_inc(sem("cls_kT"), 1)
                    if n == GROUPS + 2:
                        act.wait_ge(sem("cls_sub"), 3)
                        act.activation(psum2[0][:, :], psum2[0][:, :], ACT.Exp).then_inc(sem("cls_exp"), 1)
                        act.activation(psum2[1][:, :], psum2[1][:, :], ACT.Exp).then_inc(sem("cls_exp"), 1)

            def norm1(n, j):
                need(act, "x_t", n - 2)
                alone(act)
                act.activation(xhat[j % 2][:, :], h[:, bass.ds(n, 1), :].rearrange("p a d -> p (a d)"), ACT.Identity,
                               bias=mr1[:, bass.ds(n, 1)], scale=rs1[:, bass.ds(n, 1)]).then_inc(sem("xhat"), 1)

            def rows_in(n, j):
                act.wait_ge(sem("x_t"), n)
                need(act, "qkv", n - 2)
                act.activation(xT[j % 2][0:HALF, :, :], p_xT, ACT.Copy).then_inc(sem("xT"), 1)

            act.wait_ge(sem("mr1"), 1)
            norm1(1, 1)
            rows_in(1, 1)

            def step(k, j, stages):
                a, b, c, d, e, f = (k - i for i in range(6))
                ja, jb, jc, jd, je, jf = (j - i for i in range(6))
                if "B" in stages:
                    act.wait_ge(sem("qk_t"), b)
                    need(act, "kblk0", b - 2)
                    need(act, "kblk1", b - 2)
                    need(act, "scores", b - 2)
                    act.activation(qkT[jb % 2][:, :, :], p_qkT, ACT.Copy).then_inc(sem("qkT"), 1)
                if "C" in stages:
                    act.wait_ge(sem("p_t"), c)
                    need(act, "pv", c - 2)
                    act.activation(pT[jc % 2][:, 0:4, :], p_pTa, ACT.Copy).then_inc(sem("pTa"), 1)
                    act.activation(pT[jc % 2][:, 4:6, :], p_pTb, ACT.Copy).then_inc(sem("pTb"), 1)
                if "A" in stages:
                    act.wait_ge(sem("qkv"), a)
                    need(act, "pv", a - 4)
                    for b_ in range(2):
                        for odd in range(2):
                            ins = act.activation(
                                vblk[ja % 4][odd * PATCHES:(odd + 1) * PATCHES, b_, :, odd, 0:HD],
                                PS[b_ * PATCHES:(b_ + 1) * PATCHES, 0, 256:256 + D].rearrange("p (g o d) -> p g o d", o=2, d=HD)[:, :, odd, :],
                                ACT.Copy)
                    ins.then_inc(sem("vblk"), 1)
                if not isinstance(k, int) or k < TILES:
                    if isinstance(k, int) and k == 7:
                        act.wait_ge(sem("mr1"), 2)
                    norm1(k + 1, j + 1)
                if "D" in stages:
                    act.wait_ge(sem("yx_t"), k - 2)
                    need(act, "tail", d - 1)
                    act.activation(yT[jd % 2][0:HALF, :, :], p_yT, ACT.Copy).then_inc(sem("yT"), 1)
                if "E" in stages:
                    act.wait_ge(sem("yx_t"), k - 2)
                    need(act, "tail", e)
                    act.activation(x2T[je % 2][:, :, :], p_x2T, ACT.Copy).then_inc(sem("x2T"), 1)
                if not isinstance(k, int) or k < TILES:
                    rows_in(k + 1, j + 1)
                if "B" in stages:
                    act.wait_ge(sem("shifted"), 3 * b)
                    act.activation(probs[jb % 2][:, :], probs[jb % 2][:, :], ACT.Exp).then_inc(sem("exp"), 1)

            pipeline(act, step)
            act.wait_ge(sem("g_sub"), 2)
            act.activation(gmx[:, :, :], gmx[:, :, :], ACT.Exp).then_inc(sem("g_exp"), 1)
            act.activation(gs2[:, :, :], gs2[:, :, :], ACT.Exp).then_inc(sem("g_exp"), 1)

            act.wait_ge(sem("last_zero"), 3)
            act.sem_inc(sem("g2"), 4)

            def tile(e, u, c, g, width, wide):
                for m in range(4):
                    act.wait_ge(sem("l1"), 4 * g + m + 1)
                    act.activation(h1b[:, m, 0:width], PS[:, L1_BANKS[m], 0:width], ACT.Gelu,
                                   bias=bcur[u % 2][:, m:m + 1]).then_inc(sem("g1"), 1)
                for m in range(4):
                    act.wait_ge(sem("l2"), 4 * g + m + 1)
                    act.activation(h2b[:, m, 0:width], PS[:, L2_BANKS[m], 0:width], ACT.Gelu,
                                   bias=bcur[u % 2][:, 4 + m:5 + m]).then_inc(sem("g2"), 1)

            def enter(e0, u):
                act.wait_ge(sem("bcur"), e0 + u + 1)
                alone(act)

            experts(act, tile, enter=enter, layouts=False)
            act.wait_ge(sem("g_w"), 6)
            for i, (n0, n1) in enumerate(OUT_GROUPS):
                act.wait_ge(sem(f"res_in{i}"), 16)
                for n in range(n0, n1):
                    r = res[(n - 1) // 4][:, (n - 1) % 4, D:2 * D]
                    ins = act.activation(r, r, ACT.Copy, scale=wgt[:, n, 1:2])
                ins.then_inc(sem("second"), 1)

        @block.tensor
        def _(pe):
            pe.wait_ge(sem("cst_in"), 16)
            pe.wait_ge(sem("tokw_in"), 16)
            for q in range(4):
                for i in range(2):
                    for c in range(2):
                        ins = pe.transpose(PS[:, q, i * D + c * HALF:i * D + (c + 1) * HALF],
                                           tokw[:, c, (2 * q + i) * P:(2 * q + i + 1) * P], ident[0:HALF, 0:HALF])
                ins.then_inc(sem("tokw_t"), 1)
            def project_in(src, to_qk, to_v):
                for c in range(2):
                    kk = HALF + c
                    pe.matmul(to_qk, src[0:kk, c, :], was[0:kk, c, 0:2 * D], start=(c == 0), stop=(c == 1))
                for c in range(2):
                    kk = HALF + c
                    ins = pe.matmul(to_v, src[0:kk, c, :], was[0:kk, c, 2 * D:3 * D], start=(c == 0), stop=(c == 1))
                return ins

            def class_token():
                pe.wait_ge(sem("cls_xhat"), 1)
                pe.wait_ge(sem("pix_a"), GROUPS)
                pe.wait_ge(sem("pix_v"), GROUPS)
                for c in range(2):
                    ins = pe.transpose(c_xT[:, c, :], xhat[0][:, c * HALF:(c + 1) * HALF], ident)
                ins.then_inc(sem("cls_xt"), 1)
                pe.wait_ge(sem("cls_xT"), 1)
                pe.wait_ge(sem("was"), 3)
                project_in(xT[0], c_qk, c_v).then_inc(sem("cls_qkv"), 1)

            def class_keys():
                pe.wait_ge(sem("cls_qk"), 2)
                pe.wait_ge(sem("vcls"), 1)
                for c in range(2):
                    ins = pe.transpose(c_xT[:, c, :], qk[0][:, D + c * HALF:D + (c + 1) * HALF], ident)
                ins.then_inc(sem("cls_kt"), 1)

            def pixels(n):
                pe.wait_ge(sem("blocks"), n + 1)
                if n == 1:
                    pe.wait_ge(sem("was"), 3)
                if n == GROUPS + 1:
                    pe.wait_ge(sem("cls_kT"), 1)
                need(pe, "pix_a", n - 1)
                need(pe, "pix_v", n - 1)
                for j in range(GRID):
                    ins = pe.transpose(PS[:, 4 + 2 * (n % 2) + j // 4, (j % 4) * P:(j % 4 + 1) * P], blocks[n % 2][:, j, :], ident)
                ins.then_inc(sem("pix_t"), 1)

            def embed(n):
                g = n % GROUPS
                pe.wait_ge(sem("pix_a"), n + 1)
                pe.wait_ge(sem("pix_v"), n + 1)
                if g == 0 and n:
                    pe.wait_ge(sem("h"), GROUPS)
                for t in range(8):
                    ins = pe.matmul(PS[:, t // 2, (t % 2) * D:(t % 2 + 1) * D], pix[n % 2][:, t * P:(t + 1) * P], tokwT[:, g, :],
                                    start=(g == 0 and t % 2 == 0), stop=(g == GROUPS - 1), skip_group_check=True)
                ins.then_inc(sem("embed"), 1)

            pixels(0)
            pe.wait_ge(sem("bias_in"), 64)
            for c in range(4):
                pe.transpose(PS[:, 7, 32 * c:32 * c + 32], b1r[:, c * P:(c + 1) * P], ident[0:EXPERTS, 0:EXPERTS])
                pe.transpose(PS[:, 7, P + 32 * c:P + 32 * c + 32], b2r[:, c * P:(c + 1) * P], ident[0:EXPERTS, 0:EXPERTS])
            for c in range(2):
                pe.transpose(PS[0:HALF, 7, 2 * P + 32 * c:2 * P + 32 * c + 32], gw[:, c * HALF:(c + 1) * HALF], ident[0:EXPERTS, 0:EXPERTS])
            pe.transpose(PS[0:BOT, 7, 320:352], b3r[:, :], ident[0:EXPERTS, 0:EXPERTS]).then_inc(sem("bias_t"), 1)
            pe.wait_ge(sem("biasT"), 4)
            pe.wait_ge(sem("wa_in"), 64)
            for j in range(2):
                for c in range(2):
                    ins = pe.matmul(PS[HALF:HALF + 1, 6 + j, 0:288], biasc[:, c:c + 1], wa[0:HALF, c, 288 * j:288 * (j + 1)],
                                    start=(c == 0), stop=(c == 1), tile_position=(0, HALF))
            ins.then_inc(sem("bias_w"), 1)
            pe.wait_ge(sem("tokwT"), 4)
            for n in range(2 * GROUPS):
                if n == GROUPS:
                    class_token()
                    embed(n)
                    class_keys()
                    pixels(n + 1)
                else:
                    if n + 1 < 2 * GROUPS:
                        pixels(n + 1)
                    embed(n)

            def step(k, j, stages):
                a, b, c, d, e, f = (k - i for i in range(6))
                ja, jb, jc, jd, je, jf = (j - i for i in range(6))
                if "A" in stages:
                    pe.wait_ge(sem("xhat"), a)
                    need(pe, "vblk", a - 1)
                    for q in range(2):
                        ins = pe.transpose(p_xT[:, q, :], xhat[ja % 2][:, q * HALF:(q + 1) * HALF], ident)
                    ins.then_inc(sem("x_t"), 1)
                if "B" in stages:
                    pe.wait_ge(sem("qk"), b)
                    need(pe, "yT", d)
                    need(pe, "x2T", e)
                    for q in range(4):
                        ins = pe.transpose(p_qkT[:, q, :], qk[jb % 2][:, q * HALF:(q + 1) * HALF], ident)
                    ins.then_inc(sem("qk_t"), 1)
                if "A" in stages:
                    pe.wait_ge(sem("xT"), a)
                    need(pe, "rope_c", a - 1)
                    need(pe, "rope_s", a - 1)
                    project_in(xT[ja % 2], p_qk, p_v).then_inc(sem("qkv"), 1)
                if "C" in stages:
                    pe.wait_ge(sem("exp"), c)
                    need(pe, "pTa", c - 1)
                    need(pe, "yv", c - 1)
                    need(pe, "den", c - 1)
                    for q in range(HH):
                        dst = p_pTa[:, q, :] if q < 4 else p_pTb[:, q - 4, :]
                        ins = pe.transpose(dst, p_patch[jc % 2][:, q * P:(q + 1) * P], ident)
                    ins.then_inc(sem("p_t"), 1)
                if "B" in stages:
                    pe.wait_ge(sem("kblk0"), b)
                    pe.wait_ge(sem("kblk1"), b)
                    need(pe, "shifted", 3 * b - 3)
                    for half in range(2):
                        pe.matmul(PS[:, 5 + half, 0:HH * KEYS], identb[:, :], causal[:, :], start=True, stop=False, skip_group_check=True)
                        for b_ in range(2):
                            ins = pe.matmul(PS[b_ * PATCHES:(b_ + 1) * PATCHES, 5 + half, 0:HH * KEYS],
                                            qkT[jb % 2][:, half, b_ * PATCHES:(b_ + 1) * PATCHES],
                                            kblk[jb % 2][b_][:, half, :, :].rearrange("p g k -> p (g k)"),
                                            start=False, stop=True, skip_group_check=True)
                    ins.then_inc(sem("scores"), 1)
                if "D" in stages or "E" in stages:
                    if "B" in stages:
                        pe.wait_ge(sem("qkT"), b)
                    if "D" in stages:
                        pe.wait_ge(sem("y"), d + 1)
                        if "B" not in stages:
                            need(pe, "yT", d)
                        for q in range(2):
                            ins = pe.transpose(p_yT[:, q, :], y[jd % 2][:, q * HALF:(q + 1) * HALF], ident)
                    if "E" in stages:
                        pe.wait_ge(sem("x2"), e + 1)
                        if "B" not in stages:
                            need(pe, "x2T", e)
                            need(pe, "yT", min(d, NT))
                        for q in range(2):
                            ins = pe.transpose(p_x2T[:, q, :], row[0][je % 4][:, q * HALF:(q + 1) * HALF], ident)
                    ins.then_inc(sem("yx_t"), 1)
                if "C" in stages:
                    pe.wait_ge(sem("pTa"), c)
                    pe.wait_ge(sem("pTb"), c)
                    pe.wait_ge(sem("vblk"), c)
                    for b_ in range(2):
                        for q in range(HH):
                            ins = pe.matmul(PS[b_ * PATCHES:(b_ + 1) * PATCHES, 4, 256 + 34 * q:256 + 34 * (q + 1)],
                                            pT[jc % 2][:, q, b_ * PATCHES:(b_ + 1) * PATCHES],
                                            vblk[jc % 4][:, b_, q, :, :].rearrange("p o d -> p (o d)"), start=True, stop=True)
                    ins.then_inc(sem("pv"), 1)
                if "D" in stages:
                    need(pe, "h1", d)
                if "F" in stages:
                    pe.wait_ge(sem("logits"), f + 1)
                    need(pe, "rankc", f)
                if "D" in stages:
                    pe.wait_ge(sem("yT"), d + 1)
                    if "E" not in stages:
                        need(pe, "h1", d)
                    for q in range(2):
                        kk = HALF + q
                        ins = pe.matmul(p_proj, yT[jd % 2][0:kk, q, :], wps[0:kk, q, :], start=(q == 0), stop=(q == 1))
                if "E" in stages:
                    pe.wait_ge(sem("x2T"), e + 1)
                    if "D" not in stages:
                        pe.wait_ge(sem("h1"), NT)
                    for q in range(2):
                        ins = pe.matmul(p_gate, x2T[je % 2][:, q, :], gwT[:, q, :], start=(q == 0), stop=(q == 1))
                if "F" in stages:
                    pe.wait_ge(sem("member"), f + 1)
                    need(pe, "before", f)
                    pe.matmul(p_rank, earlier[:, :], member[jf % 2][:, :], start=True, stop=False)
                    ins = pe.matmul(p_rank, onesb[:, :], before[:, :], start=False, stop=True)
                if "D" in stages or "E" in stages or "F" in stages:
                    ins.then_inc(sem("tail"), 1)

            pe.wait_ge(sem("h"), 2 * GROUPS)
            pe.wait_ge(sem("kcls"), 4)
            pe.wait_ge(sem("vones"), 8)
            pe.wait_ge(sem("tab"), 3)
            pe.wait_ge(sem("wps"), 2)
            pe.wait_ge(sem("before_zero"), 8)
            pipeline(pe, step)
            pe.wait_ge(sem("before"), NT)
            pe.wait_ge(sem("rankc"), NT)
            pe.matmul(p_rank, onesb[:, :], before[:, :], start=True, stop=True).then_inc(sem("counts"), 1)

            def finish_z(g, place, wide):
                width = WIDE if wide else P
                for q in range(4):
                    pe.wait_ge(sem("g2"), 4 * g + q + 1)
                    ins = pe.matmul(p_z[:, 0:width], W3[place][:, q, :], h2b[:, q, 0:width], start=(q == 0), stop=(q == 3))
                ins.then_inc(sem("l3"), 1)

            def finish_results(g, place, wide):
                pieces, piece = (2, HALF) if wide else (1, P)
                pe.wait_ge(sem("z"), g + 1)
                pe.wait_ge(sem("result"), g + 1)
                for k in range(pieces):
                    ins = pe.matmul(PS[0:piece, 7, k * D:(k + 1) * D], zb[:, k * piece:(k + 1) * piece], WL[place][:, :], start=True, stop=True)
                ins.then_inc(sem("l4"), 1)

            def tile(e, u, c, g, width, wide):
                src, slot = buf(u, c), u % RING
                pieces, piece = (2, HALF) if width == WIDE else (1, P)
                stride = pieces * piece

                pe.wait_ge(sem("xs_in"), 16 * g + 32)
                for q in range(2):
                    for k in range(pieces):
                        ins = pe.transpose(PS[0:HALF, 0, q * stride + k * piece:q * stride + (k + 1) * piece],
                                           src[0:piece, k * ROW + q * HALF:k * ROW + (q + 1) * HALF], ident[0:piece, 0:piece])
                ins.then_inc(sem("xe_t"), 1)
                place = (u + RING - 1) % RING if is_first(c) else slot
                by_layout(pe, wide, lambda was_wide: finish_z(g, place, was_wide))
                if is_first(c):
                    pe.wait_ge(sem(f"w_in{u}"), (80 // RING) * (e - u) + 80)
                pe.wait_ge(sem("xeT"), g + 1)
                for m in range(4):
                    if m == 3:
                        pe.wait_ge(sem("z"), g + 1)
                    for q in range(2):
                        ins = pe.matmul(PS[:, L1_BANKS[m], 0:width], W1[slot][:, q, m * P:(m + 1) * P], xeT[:, q * stride:q * stride + width],
                                        start=(q == 0), stop=(q == 1))
                    ins.then_inc(sem("l1"), 1)
                by_layout(pe, wide, lambda was_wide: finish_results(g, place, was_wide))
                for m in range(4):
                    for q in range(4):
                        if m == 0:
                            pe.wait_ge(sem("g1"), 4 * g + q + 1)
                        ins = pe.matmul(PS[:, L2_BANKS[m], 0:width], W2[slot][:, q, m * P:(m + 1) * P], h1b[:, q, 0:width],
                                        start=(q == 0), stop=(q == 3))
                    ins.then_inc(sem("l2"), 1)

            pe.wait_ge(sem("zb_zero"), 2)
            pe.wait_ge(sem("last_zero"), 3)
            pe.sem_inc(sem("xe_t"), 1)
            experts(pe, tile)
            v = packed(pe, EXPERTS)
            tiles = pe.snap(v & (PACK_WIDE - 1))
            def last(was_wide):
                finish_z(tiles, RING - 1, was_wide)
                finish_results(tiles, RING - 1, was_wide)
            by_layout(pe, v & PACK_WIDE, last)

        @block.vector
        def _(dve):
            init = sem("init")
            dve.memset(mhalf[:, :], -0.5).then_inc(init, 1)
            dve.memset(zeros8[:, :], 0.0).then_inc(init, 1)
            for t in (xT[0], xT[1], yT[0], yT[1]):
                dve.memset(t[HALF:HALF + 1, :, :], 1.0).then_inc(init, 1)
            for t in vblk:
                dve.memset(t[:, :, :, :, :], 0.0).then_inc(init, 1)
            dve.memset(onesb[:, :], 1.0).then_inc(init, 1)
            for t in WL:
                dve.memset(t[BOT:P, :], 0.0).then_inc(init, 1)
            dve.wait_ge(init, INIT)
            for t in vblk:
                dve.memset(t[0:PATCHES, :, :, 0, HD:HD + 1], 1.0).then_inc(sem("vones"), 1)
                dve.memset(t[PATCHES:P, :, :, 1, HD:HD + 1], 1.0).then_inc(sem("vones"), 1)
            dve.memset(before[:, :], 0.0).then_inc(sem("before_zero"), 1)
            dve.memset(cnt_i[:, :], 0).then_inc(sem("before_zero"), 1)
            dve.memset(ones1[:, :], 1.0).then_inc(sem("before_zero"), 1)
            dve.memset(start_i[:, :], 0).then_inc(sem("before_zero"), 1)
            dve.memset(packed_i[:, :], 0).then_inc(sem("before_zero"), 1)
            dve.memset(wides_i[:, :], 0).then_inc(sem("before_zero"), 1)
            dve.memset(b12T[:, EXPERTS, :], 0.0).then_inc(sem("before_zero"), 1)
            dve.memset(b3T[:, 0:1], 0.0).then_inc(sem("before_zero"), 1)
            dve.memset(zb[:, :], 0.0).then_inc(sem("zb_zero"), 1)
            dve.wait_ge(sem("zb_zero"), 1)
            dve.memset(zb[BOT:BOT + 1, :], 1.0).then_inc(sem("zb_zero"), 1)
            for c in range(2):
                for i in range(4):
                    dve.memset(row[c][i][:, D + 1:D + 2], 0.0).then_inc(sem("row_zero"), 1)
            dve.wait_ge(sem("cls_in"), 16)
            dve.bn_stats(st6[:, :], h[:, 0, :]).then_inc(sem("cls_st"), 1)
            dve.wait_ge(sem("cls_st"), 1)
            dve.bn_aggr(mv[:, 0, :], st6[:, :]).then_inc(sem("cls_st"), 1)
            dve.wait_ge(sem("cls_st"), 2)
            dve.tensor_scalar(ve1[:, 0:1], mv[:, 0, 1:2], EPS, None, ALU.add).then_inc(sem("cls_ve"), 1)
            dve.wait_ge(sem("wa_in"), 64)
            for c in range(2):
                dve.tensor_scalar(was[0:HALF, c, :], wa[0:HALF, c, :], scalec[:, c:c + 1], None, ALU.mult).then_inc(sem("was"), 1)
            dve.wait_ge(sem("bias_w"), 1)
            dve.tensor_tensor(was[HALF:HALF + 1, 1, :].rearrange("p (j n) -> p j n", j=2), PS[HALF:HALF + 1, 6:8, 0:288],
                              wa[HALF:HALF + 1, 1, :].rearrange("p (j n) -> p j n", j=2), ALU.add).then_inc(sem("was"), 1)
            dve.wait_ge(sem("cls_rs"), 1)
            dve.tensor_scalar(xhat[0][:, :], h[:, 0, :], mv[:, 0, 0:1], rs1[:, 0:1], ALU.subtract, ALU.mult).then_inc(sem("cls_xhat"), 1)
            dve.wait_ge(sem("wp_in"), 48)
            dve.tensor_scalar(wps[0:HALF, 0, :], wp[0:HALF, 0, :], rez[0:HALF, :], None, ALU.mult).then_inc(sem("wps"), 1)
            dve.tensor_scalar(wps[:, 1, :], wp[:, 1, :], rez[:, :], None, ALU.mult).then_inc(sem("wps"), 1)
            dve.wait_ge(sem("init"), INIT)
            dve.memset(WL[RING - 1][0:BOT, :], 0.0).then_inc(sem("last_zero"), 1)
            dve.memset(W3[RING - 1][:, :, :], 0.0).then_inc(sem("last_zero"), 1)
            dve.wait_ge(sem("tokw_t"), 4)
            dve.memset(h2b[:, :, :], 0.0).then_inc(sem("last_zero"), 1)

            def norm1_stats(n):
                dve.wait_ge(sem("h"), n)
                need(dve, "mv1", n - 1)
                dve.bn_stats(st6[:, :], h[:, n, :]).then_inc(sem("st1"), 1)
                dve.wait_ge(sem("st1"), n)
                dve.bn_aggr(mv[:, n, :], st6[:, :]).then_inc(sem("mv1"), 1)
                if n % 8 == 0:
                    dve.wait_ge(sem("mv1"), n)
                    dve.tensor_scalar(ve1[:, n - 7:n + 1], mv[:, n - 7:n + 1, 1], EPS, None, ALU.add).then_inc(sem("ve1"), 1)

            dve.wait_ge(sem("tokb_in"), 16)
            for hf in range(2):
                for g in range(GROUPS):
                    n = hf * GROUPS + g
                    dve.wait_ge(sem("pix_t"), n + 1)
                    need(dve, "embed", n - 1)
                    dve.tensor_copy(pix[n % 2][:, :].rearrange("p (t j) -> p j t", j=GRID)[:, 4:8, :],
                                    PS[:, 5 + 2 * (n % 2), :].rearrange("p (j t) -> p j t", j=4)).then_inc(sem("pix_v"), 1)
                    if hf:
                        norm1_stats(g + 1)
                    if n == GROUPS:
                        dve.wait_ge(sem("cls_qk"), 2)
                        dve.wait_ge(sem("sink_in"), 16)
                        dve.tensor_tensor(pvc[0][:, :], qk[0][:, 0:D], qk[0][:, D:2 * D], ALU.mult).then_inc(sem("cls_s"), 1)
                        dve.wait_ge(sem("cls_s"), 1)
                        dve.tensor_reduce(den[0][:, :], pvc[0][:, :].rearrange("p (h d) -> p h d", d=HD), AX.X, ALU.add).then_inc(sem("cls_s"), 1)
                        dve.wait_ge(sem("cls_s"), 2)
                        dve.tensor_tensor(mx[0][:, :], den[0][:, :], sinkb[:, :], ALU.max).then_inc(sem("cls_sub"), 1)
                        dve.wait_ge(sem("cls_sub"), 1)
                        dve.tensor_tensor(psum2[0][:, :], den[0][:, :], mx[0][:, :], ALU.subtract).then_inc(sem("cls_sub"), 1)
                        dve.tensor_tensor(psum2[1][:, :], sinkb[:, :], mx[0][:, :], ALU.subtract).then_inc(sem("cls_sub"), 1)
                    if n == GROUPS + 1:
                        dve.wait_ge(sem("cls_kT"), 1)
                        for i in range(2):
                            for b_ in range(2):
                                dve.tensor_tensor(kblk[i][b_][:, :, :, PATCHES], qkT[0][:, 2:4, 0:1].to_broadcast([HALF, 2, HH]),
                                                  cst[0:HALF, C_HEAD:C_HEAD + HH].unsqueeze(1).to_broadcast([HALF, 2, HH]), ALU.mult).then_inc(sem("kcls"), 1)
                    if n == GROUPS + 2:
                        dve.wait_ge(sem("cls_exp"), 2)
                        dve.tensor_tensor(den[1][:, :], psum2[0][:, :], psum2[1][:, :], ALU.add).then_inc(sem("cls_y"), 1)
                        dve.wait_ge(sem("cls_y"), 1)
                        dve.reciprocal(rden[1][:, :], den[1][:, :]).then_inc(sem("cls_y"), 1)
                        dve.wait_ge(sem("cls_y"), 2)
                        dve.tensor_tensor(rden[0][:, :], rden[1][:, :], psum2[0][:, :], ALU.mult).then_inc(sem("cls_y"), 1)
                        dve.wait_ge(sem("cls_y"), 3)
                        dve.wait_ge(sem("vcls"), 1)
                        dve.tensor_tensor(y[0][:, :].rearrange("p (h d) -> p h d", d=HD), vcls[:, :].rearrange("p (h d) -> p h d", d=HD),
                                          rden[0][:, :].unsqueeze(2).to_broadcast([P, HEADS, HD]), ALU.mult).then_inc(sem("y"), 1)
                dve.wait_ge(sem("embed"), (hf + 1) * GROUPS)
                for t in range(8):
                    n = 1 + 8 * hf + t
                    dve.tensor_tensor(h[:, n, :], PS[:, t // 2, (t % 2) * D:(t % 2 + 1) * D], tokb[:, :], ALU.add).then_inc(sem("h"), 1)
            def step(k, j, stages):
                a, b, c, d, e, f = (k - i for i in range(6))
                ja, jb, jc, jd, je, jf = (j - i for i in range(6))
                A, B, C, D_, E, F = (stage in stages for stage in "ABCDEF")
                lg, t8 = lgs[jf % 2][:, :], top8[jf % 2][:, :]
                if B:
                    dve.wait_ge(sem("qkT"), b)
                    need(dve, "scores", b - 2)
                    for half in range(2):
                        ins = dve.tensor_tensor(
                            kblk[jb % 2][0][:, half, :, 0:PATCHES],
                            qkT[jb % 2][:, 2 + half:3 + half, 0:PATCHES].to_broadcast([HALF, HH, PATCHES]),
                            cst[0:HALF, C_HEAD:C_HEAD + HH].unsqueeze(2).to_broadcast([HALF, HH, PATCHES]), ALU.mult)
                    ins.then_inc(sem("kblk0"), 1)
                if F:
                    dve.wait_ge(sem("tail"), f + 2)
                    dve.wait_ge(sem("kept"), 2 * (f + 1))
                    dve.tensor_copy(lg, p_gate).then_inc(sem("logits"), 1)
                if A:
                    dve.wait_ge(sem("qkv"), a)
                    need(dve, "qk", a - 2)
                    src = p_qk.rearrange("p (w h d) -> p w h d", w=2, d=HD)
                    dve.tensor_tensor(rope_c[ja % 2][:, :].rearrange("p (w h d) -> p w h d", w=2, d=HD), src,
                                      cst[:, C_ROPE_C:C_ROPE_C + 2 * HD].rearrange("p (w a d) -> p w a d", w=2, a=1).to_broadcast([P, 2, HEADS, HD]),
                                      ALU.mult).then_inc(sem("rope_c"), 1)

                def rotate(w):
                    return dve.tensor_tensor(
                        rope_s[ja % 2][:, w * D:(w + 1) * D].rearrange("p (h d o) -> p h d o", h=HEADS, o=2),
                        p_qk[:, w * D:(w + 1) * D].rearrange("p (h d o) -> p h d o", h=HEADS, o=2)[:, :, :, ::-1],
                        cst[:, C_ROPE_S + w * HD:C_ROPE_S + (w + 1) * HD].rearrange("p (a d o) -> p a d o", a=1, o=2).to_broadcast([P, HEADS, HD // 2, 2]),
                        ALU.mult)
                if F:
                    dve.wait_ge(sem("logits"), f + 1)
                    alone(dve)
                    dve.max(t8, lg).then_inc(sem("top8"), 1)
                if A:
                    rotate(0)
                if F:
                    dve.wait_ge(sem("top8"), f + 1)
                    alone(dve)
                    dve.max_index(idx8[jf % 2][:, :], t8, lg).then_inc(sem("idx8"), 1)
                if A:
                    rotate(1).then_inc(sem("rope_s"), 1)
                if F:
                    dve.wait_ge(sem("idx8"), f + 1)
                    dve.tensor_copy(idxf[jf % 2][:, :], idx8[jf % 2][:, 0:2]).then_inc(sem("idxf"), 1)
                if E:
                    dve.wait_ge(sem("rs2"), e + 1)
                    scattered(dve, e - 4, je - 4)
                    dve.tensor_scalar(row[0][je % 4][:, 0:D], h[:, bass.ds(e, 1), :].rearrange("p a d -> p (a d)"), mv2[je % 2][:, 0:1], rs2[je % 2][:, :],
                                      ALU.subtract, ALU.mult).then_inc(sem("x2"), 1)
                if F:
                    dve.wait_ge(sem("idxf"), f + 1)
                    for ch in range(2):
                        dve.tensor_scalar(pick[jf % 2][:, ch, :], iota, idxf[jf % 2][:, ch:ch + 1],
                                          cst[:, bass.ds(C_KEEP + f, 1)], ALU.is_equal, ALU.mult).then_inc(sem("pick"), 1)
                if B:
                    dve.wait_ge(sem("scores"), b)
                    dve.tensor_reduce(mx[jb % 2][:, :].rearrange("p (c g) -> p c g", c=2), p_s, AX.X, ALU.max).then_inc(sem("rowmax"), 1)
                if B:
                    dve.wait_ge(sem("rowmax"), b)
                    dve.tensor_tensor(mx[jb % 2][:, :], mx[jb % 2][:, :], sinkb[:, :], ALU.max).then_inc(sem("max"), 1)
                if F:
                    dve.wait_ge(sem("pick"), 2 * f + 2)
                    dve.tensor_tensor(member[jf % 2][:, :], pick[jf % 2][:, 0, :], pick[jf % 2][:, 1, :], ALU.add).then_inc(sem("member"), 1)
                if B:
                    dve.wait_ge(sem("max"), b)
                    need(dve, "p_t", b - 2)
                    need(dve, "pvc", b - 2)
                    need(dve, "psum2", b - 2)
                    dve.tensor_tensor(p_sink[jb % 2], sinkb[:, :], mx[jb % 2][:, :], ALU.subtract).then_inc(sem("shifted"), 1)
                    dve.tensor_tensor(p_class[jb % 2].rearrange("p (c g) -> p c g", c=2), p_s[:, :, :, PATCHES],
                                      mx[jb % 2][:, :].rearrange("p (c g) -> p c g", c=2), ALU.subtract).then_inc(sem("shifted"), 1)
                    dve.tensor_tensor(p_patch[jb % 2].rearrange("p (c g k) -> p c g k", c=2, g=HH), p_s[:, :, :, 0:PATCHES],
                                      mx[jb % 2][:, :].rearrange("p (c g a) -> p c g a", c=2, a=1).to_broadcast([P, 2, HH, PATCHES]),
                                      ALU.subtract).then_inc(sem("shifted"), 1)
                hd_ = h[:, bass.ds(d, 1), :].rearrange("p a d -> p (a d)") if D_ else None
                if C:
                    dve.wait_ge(sem("pv"), c)
                    dve.wait_ge(sem("psum2"), c)
                    dve.tensor_tensor(den[jc % 2][:, :], psum2[jc % 2][:, :], p_y[:, :, HD], ALU.add).then_inc(sem("den"), 1)
                    dve.wait_ge(sem("pvc"), c)
                    dve.tensor_tensor(yv[jc % 2][:, :].rearrange("p (h d) -> p h d", d=HD), pvc[jc % 2][:, :].rearrange("p (h d) -> p h d", d=HD),
                                      p_y[:, :, 0:HD], ALU.add).then_inc(sem("yv"), 1)
                    dve.wait_ge(sem("den"), c)
                    dve.reciprocal(rden[jc % 2][:, :], den[jc % 2][:, :]).then_inc(sem("rden"), 1)
                    dve.wait_ge(sem("rden"), c)
                    dve.wait_ge(sem("yv"), c)
                    need(dve, "yx_t", c - 1)
                    dve.tensor_tensor(y[jc % 2][:, :].rearrange("p (h d) -> p h d", d=HD), yv[jc % 2][:, :].rearrange("p (h d) -> p h d", d=HD),
                                      rden[jc % 2][:, :].unsqueeze(2).to_broadcast([P, HEADS, HD]), ALU.mult).then_inc(sem("y"), 1)
                if D_:
                    dve.wait_ge(sem("tail"), d + 1)
                    dve.tensor_tensor(hd_, hd_, p_proj, ALU.add).then_inc(sem("h1"), 1)
                if F:
                    dve.wait_ge(sem("tail"), f + 3)
                    dve.tensor_tensor(rankc[jf % 2][:, :], p_rank, ecap, ALU.add).then_inc(sem("rankc"), 1)
                    dve.tensor_tensor(before[:, :], before[:, :], member[jf % 2][:, :], ALU.add).then_inc(sem("before"), 1)
                if D_:
                    dve.wait_ge(sem("h1"), d + 1)
                    need(dve, "mv2", d)
                    alone(dve)
                    dve.bn_stats(st6b[:, :], hd_).then_inc(sem("st2"), 1)
                if F:
                    dve.wait_ge(sem("rankc"), f + 1)
                    dve.tensor_tensor(slp[jf % 2][:, :, :], pick[jf % 2][:, :, :], rankc[jf % 2][:, :].unsqueeze(1).to_broadcast([P, 2, EXPERTS]),
                                      ALU.mult).then_inc(sem("slp"), 1)
                if D_:
                    dve.wait_ge(sem("st2"), d + 1)
                    need(dve, "x2", d - 1)
                    alone(dve)
                    dve.bn_aggr(mv2[jd % 2][:, 0:2], st6b[:, :]).then_inc(sem("mv2"), 1)
                if F:
                    dve.wait_ge(sem("slp"), f + 1)
                    dve.tensor_reduce(slf[jf % 2][:, :], slp[jf % 2][:, :, :], AX.X, ALU.add).then_inc(sem("slf"), 1)
                if D_:
                    dve.wait_ge(sem("mv2"), d + 1)
                    need(dve, "rs2", d - 1)
                    dve.tensor_scalar(mv2[jd % 2][:, 2:3], mv2[jd % 2][:, 1:2], EPS, None, ALU.add).then_inc(sem("ve2"), 1)
                if F:
                    dve.wait_ge(sem("slf"), f + 1)
                    scattered(dve, f - 3, jf - 3)
                    dve.tensor_tensor(slu[jf % 4][:, :], slf[jf % 2][:, :],
                                      cst[:, bass.ds(C_SPARE + 2 * f, 2)], ALU.add).then_inc(sem("slot"), 1)
                if isinstance(k, int) and k <= 4:
                    norm1_stats(2 * k + 7)
                    norm1_stats(2 * k + 8)

            dve.wait_ge(sem("kcls"), 4)
            dve.wait_ge(sem("row_zero"), 8)
            dve.wait_ge(sem("before_zero"), 8)
            pipeline(dve, step)

            dve.wait_ge(sem("counts"), 1)
            dve.tensor_copy(cnt[:, :], p_rank[0:1, :]).then_inc(sem("cnt"), 1)
            dve.wait_ge(sem("cnt"), 1)
            dve.tensor_copy(cnt_i[0:1, 0:EXPERTS], cnt[:, :]).then_inc(sem("tables"), 1)
            dve.tensor_tensor(over[:, :, :], cnt[:, :].unsqueeze(2).to_broadcast([1, EXPERTS, CHUNKS - 1]),
                              cst[0:1, C_STEP:C_STEP + CHUNKS - 1].unsqueeze(1).to_broadcast([1, EXPERTS, CHUNKS - 1]), ALU.is_gt).then_inc(sem("over"), 1)
            dve.tensor_tensor(over4[:, :, :], cnt[:, :].unsqueeze(2).to_broadcast([1, EXPERTS, 4]),
                              cst[0:1, C_WIDE:C_WIDE + 4].unsqueeze(1).to_broadcast([1, EXPERTS, 4]), ALU.is_gt).then_inc(sem("wides"), 1)
            dve.wait_ge(sem("over"), 1)
            dve.tensor_reduce(ntile[:, :], over[:, :, :], AX.X, ALU.add).then_inc(sem("over"), 1)
            dve.wait_ge(sem("wides"), 1)
            dve.tensor_tensor(over4[:, :, :], over4[:, :, :],
                              cst[0:1, C_WIDE + 4:C_WIDE + 8].unsqueeze(1).to_broadcast([1, EXPERTS, 4]), ALU.mult).then_inc(sem("wides"), 1)
            dve.memset(startf[:, 0:1], 0.0).then_inc(sem("over"), 1)
            dve.wait_ge(sem("over"), 3)
            dve.tensor_tensor_scan(startf[:, 1:EXPERTS + 1], ones1[:, :], ntile[:, :], 0.0, ALU.add, ALU.add).then_inc(sem("over"), 1)
            dve.wait_ge(sem("wides"), 2)
            dve.tensor_reduce(widef[:, :], over4[:, :, :], AX.X, ALU.add).then_inc(sem("wides"), 1)
            dve.wait_ge(sem("over"), 4)
            dve.tensor_copy(start_i[:, 1:EXPERTS + 2], startf[:, :]).then_inc(sem("tables"), 1)
            dve.wait_ge(sem("wides"), 3)
            dve.scalar_tensor_tensor(packedf[:, 1:EXPERTS + 1], widef[:, :], float(PACK_WIDE), startf[:, 1:EXPERTS + 1], ALU.mult, ALU.add).then_inc(sem("over"), 1)
            dve.memset(packedf[:, 0:1], 0.0).then_inc(sem("over"), 1)
            dve.wait_ge(sem("over"), 6)
            dve.scalar_tensor_tensor(packedf[:, 0:EXPERTS], cnt[:, :], float(PACK_COUNT), packedf[:, 0:EXPERTS], ALU.mult, ALU.add).then_inc(sem("over"), 1)
            dve.tensor_tensor_scan(widesf[:, :], ones1[:, :], widef[:, :], 0.0, ALU.mult, ALU.add).then_inc(sem("wides"), 1)
            dve.wait_ge(sem("over"), 7)
            dve.tensor_copy(packed_i[:, :], packedf[:, :]).then_inc(sem("tables"), 1)
            dve.wait_ge(sem("wides"), 4)
            dve.tensor_copy(wides_i[:, 1:EXPERTS + 1], widesf[:, :]).then_inc(sem("wides"), 1)

            dve.wait_ge(sem("pad_set"), 2)
            dve.wait_ge(sem("zb_zero"), 2)
            dve.wait_ge(sem("biasT"), 4)
            dve.sem_inc(sem("dest"), 1)
            dve.sem_inc(sem("result"), 1)

            dve.wait_ge(sem("kept"), 4 + 2 * NT)
            dve.tensor_tensor(gmx[:, :, :], logits[:, :, :], top2[:, :, 0:1].to_broadcast([P, NT, EXPERTS]), ALU.subtract).then_inc(sem("g_sub"), 1)
            dve.tensor_tensor(gs2[:, :, :], top2[:, :, 0:2], top2[:, :, 0:1].to_broadcast([P, NT, 2]), ALU.subtract).then_inc(sem("g_sub"), 1)
            dve.wait_ge(sem("g_exp"), 2)
            dve.tensor_reduce(gz[:, :], gmx[:, :, :], AX.X, ALU.add).then_inc(sem("g_w"), 1)
            dve.wait_ge(sem("g_w"), 1)
            dve.reciprocal(gri[:, :], gz[:, :]).then_inc(sem("g_w"), 1)
            dve.wait_ge(sem("g_w"), 2)
            dve.tensor_tensor(wgt[:, :, :], gs2[:, :, :], gri[:, :].unsqueeze(2).to_broadcast([P, NT, 2]), ALU.mult).then_inc(sem("g_w"), 1)
            dve.wait_ge(sem("g_w"), 3)
            dve.scalar_tensor_tensor(gden[:, :], wgt[:, :, 0], 1e-20, wgt[:, :, 1], ALU.add, ALU.add).then_inc(sem("g_w"), 1)
            dve.wait_ge(sem("g_w"), 4)
            dve.reciprocal(gz[:, :], gden[:, :]).then_inc(sem("g_w"), 1)
            dve.wait_ge(sem("g_w"), 5)
            dve.tensor_tensor(wgt[:, :, :], wgt[:, :, :], gz[:, :].unsqueeze(2).to_broadcast([P, NT, 2]), ALU.mult).then_inc(sem("g_w"), 1)


            def finish(column, g, wide):
                width = WIDE if wide else P
                dve.wait_ge(sem("l3"), g + 1)
                dve.tensor_scalar(zb[0:BOT, 0:width], p_z[:, 0:width], b3T[:, bass.ds(column, 1)], None, ALU.add).then_inc(sem("z"), 1)
                dve.wait_ge(sem("sent"), g + 1)
                dve.wait_ge(sem("dest"), g + 1)
                dve.tensor_copy(dest_old[:, :], dest_new[:, :]).then_inc(sem("dest_old"), 1)
                dve.wait_ge(sem("l4"), g + 1)
                if wide:
                    dve.tensor_copy(yb[0:HALF, :], PS[0:HALF, 7, 0:2 * D]).then_inc(sem("result"), 1)
                else:
                    dve.tensor_copy(yb[:, 0:D], PS[:, 7, 0:D]).then_inc(sem("result"), 1)

            def tile(e, u, c, g, width, wide):
                pieces, piece = (2, HALF) if width == WIDE else (1, P)
                n = 2 * pieces * piece

                dve.wait_ge(sem("xe_t"), g + 2)
                dve.tensor_copy(xeT[:, 0:n], PS[0:HALF, 0, 0:n]).then_inc(sem("xeT"), 1)
                by_layout(dve, wide, lambda was_wide: finish(e if is_first(c) else e + 1, g, was_wide))
                dve.wait_ge(sem("dest_old"), g + 1)
                dve.tensor_copy(dest_new[0:piece, 0:pieces],
                                buf(u, c)[0:piece, :].rearrange("p (k d) -> p k d", k=2)[:, 0:pieces, D].bitcast(u32)).then_inc(sem("dest"), 1)
                if is_first(c):
                    dve.tensor_copy(bcur[(u + 1) % 2][:, :], b12T[:, bass.ds(e + 1, 1), :].rearrange("p a c -> p (a c)")).then_inc(sem("bcur"), 1)

            dve.tensor_copy(bcur[0][:, :], b12T[:, 0, :]).then_inc(sem("bcur"), 1)
            experts(dve, tile)
            v = packed(dve, EXPERTS)
            tiles = dve.snap(v & (PACK_WIDE - 1))
            by_layout(dve, v & PACK_WIDE, lambda was_wide: finish(EXPERTS, tiles, was_wide))

            dve.wait_ge(sem("g_w"), 6)
            def first(n, r, rows):
                return dve.scalar_tensor_tensor(h[0:rows, n, :], r[:, 0:D], wgt[0:rows, n, 0:1], h[0:rows, n, :], ALU.mult, ALU.add)
            for i, (n0, n1) in enumerate(OUT_GROUPS):
                dve.wait_ge(sem(f"res_in{i}"), 16)
                for n in range(n0, n1):
                    ins = first(n, res[(n - 1) // 4][:, (n - 1) % 4, :], P)
                ins.then_inc(sem("o1"), 1)
                dve.wait_ge(sem("o1"), i + 1)
                dve.wait_ge(sem("second"), i + 1)
                m = (n0 - 1) % 4
                r = res[(n0 - 1) // 4][:, m:m + n1 - n0, D:2 * D]
                dve.tensor_tensor(r, r, h[:, n0:n1, :], ALU.add).then_inc(sem("o2"), 1)
            dve.wait_ge(sem("cls_res"), 16)
            first(0, res_cls, IMAGES).then_inc(sem("o1"), 1)
            dve.wait_ge(sem("o1"), len(OUT_GROUPS) + 1)
            dve.scalar_tensor_tensor(res_cls[:, D:2 * D], res_cls[:, D:2 * D], wgt[0:IMAGES, 0, 1:2], h[0:IMAGES, 0, :], ALU.mult, ALU.add).then_inc(sem("o2"), 1)


def constants():
    import numpy as np
    t = np.zeros((P, C_END), np.float32)
    p = np.arange(P)
    t[:, C_ID:C_ID + P] = np.eye(P)
    t[:, C_TRI:C_TRI + P] = p[:, None] < p[None, :]
    freqs = np.float32(1.0) / np.power(np.float32(10000.0), np.arange(0, HD, 2, dtype=np.float32) / np.float32(HD))
    ang = (1 + p % PATCHES).astype(np.float32)[:, None] * freqs.astype(np.float32)[None, :]
    cos, sin = np.cos(ang), np.sin(ang)
    for w, scale in enumerate((HD ** -0.5, 1.0)):
        t[:, C_ROPE_C + w * HD:C_ROPE_C + (w + 1) * HD] = np.repeat(cos, 2, 1) * scale
        t[:, C_ROPE_S + w * HD:C_ROPE_S + (w + 1) * HD] = np.stack([-sin, sin], -1).reshape(P, HD) * scale
    mask = np.zeros((P, HH, KEYS), np.float32)
    mask[:, :, 0:PATCHES] = np.where(np.arange(PATCHES)[None, :] > (p % PATCHES)[:, None], MASKED, 0.0)[:, None, :]
    t[:, C_CAUSAL:C_CAUSAL + HH * KEYS] = mask.reshape(P, -1)
    t[:, C_IOTA:C_IOTA + EXPERTS] = np.arange(EXPERTS)
    t[:, C_ECAP:C_ECAP + EXPERTS] = np.arange(EXPERTS) * CAP
    t[:, C_STEP:C_STEP + CHUNKS - 1] = TILE_STEPS
    t[:, C_WIDE:C_WIDE + 4] = WIDE_STEPS
    t[:, C_WIDE + 4:C_WIDE + 8] = [1, -1, 1, -1]
    t[:HALF, C_HEAD:C_HEAD + HH] = (p[:HALF] // HD)[:, None] == np.arange(HH)[None, :]
    t[:, C_KEEP:C_KEEP + NT] = 1.0
    t[1:, C_KEEP] = 0.0
    t[1:, C_SPARE] = SPARE0 + p[1:]
    t[1:, C_SPARE + 1] = SPARE1 + p[1:]
    t[:, C_PADID] = RESULTS + p
    for ch in range(2):
        t[:, C_DEST + ch * NT:C_DEST + (ch + 1) * NT] = (np.arange(NT)[None, :] * P + p[:, None]) * 2 + ch
    return t


_INS = ['x', 'cls_tok', 'L0_tok_w', 'L0_tok_b', 'L0_attn_norm_scale', 'L0_attn_norm_bias', 'L0_attn_W_attn', 'L0_attn_b_attn',
        'L0_attn_W_proj', 'L0_attn_b_proj', 'L0_attn_sinks', 'L0_attn_rezero', 'L0_ffn_gate_w', 'L0_ffn_W1', 'L0_ffn_b1',
        'L0_ffn_W2', 'L0_ffn_b2', 'L0_ffn_W3', 'L0_ffn_b3', 'L0_ffn_Wl', 'L0_ffn_bl']


def kernel(**inputs):
    import numpy as _np
    import concourse.bacc as _bacc
    from concourse import mybir as _mybir
    from concourse.bass_utils import run_bass_kernel_spmd as _run

    nc = _bacc.Bacc("TRN2", target_bir_lowering=False, num_devices=1)
    arrays, args = {}, []
    for name in _INS + ["table"]:
        a = constants() if name == "table" else _np.ascontiguousarray(inputs[name])
        arrays[f"in_{name}_dram"] = a
        args.append(nc.dram_tensor(f"in_{name}_dram", a.shape, _mybir.dt.from_np(a.dtype), kind="ExternalInput").ap())
    args.append(nc.dram_tensor("out_0_dram", (IMAGES, KEYS, D), _mybir.dt.float32, kind="ExternalOutput").ap())
    vit_moe_kernel(nc, *args)
    r = _run(nc, [arrays], core_ids=[0])
    return r.results[0]["out_0_dram"]
```
